# Optimizing a Trainium2 kernel written in Bass

```python
import numpy as np
import jax
import jax.numpy as jnp

def _softmax(x, axis=-1):
    return jax.nn.softmax(x, axis=axis)

def _gelu(x):
    return jax.nn.gelu(x, approximate=True)

def _silu(x):
    return jax.nn.silu(x)

def _sigmoid(x):
    return jax.nn.sigmoid(x)

def _layernorm(x, axis=-1, eps=1e-05):
    m = jnp.mean(x, axis=axis, keepdims=True)
    v = jnp.var(x, axis=axis, keepdims=True)
    return (x - m) / jnp.sqrt(v + eps)

def _scatter_add(tgt, idx, src, axis=0):
    return tgt.at[idx].add(src)

def _segment_sum(src, seg, n):
    return jax.ops.segment_sum(src, seg, n)
kernel_name = 'mk_adaln_d1_jaxref_r8_49027b'

def setup_inputs(seed: int=0):
    np.random.seed(seed)
    _w = jnp.asarray

    def _L0_attn_setup():
        import jax, jax.numpy as jnp
        import numpy as np
        HIDDEN = 256
        KEY = 256
        EPS = 1e-05
        key = jax.random.key(seed)
        k1, k2, k3 = jax.random.split(key, 3)
        B, S = (4, 256)
        x = jax.random.normal(k1, (B, S, HIDDEN), dtype=jnp.float32)
        bq = 1.0 / np.sqrt(HIDDEN)
        qkv = jax.random.uniform(k2, (HIDDEN, KEY * 3), minval=-bq, maxval=bq, dtype=jnp.float32)
        bo = 1.0 / np.sqrt(KEY)
        o_proj = jax.random.uniform(k3, (KEY, HIDDEN), minval=-bo, maxval=bo, dtype=jnp.float32)
        gamma = jnp.ones((HIDDEN,), dtype=jnp.float32)
        beta = jnp.zeros((HIDDEN,), dtype=jnp.float32)
        return {'x': x, 'qkv': qkv, 'o_proj': o_proj, 'gamma': gamma, 'beta': beta}
    _L0_attn_in = _L0_attn_setup()

    def _L0_ffn_setup():
        import jax, jax.numpy as jnp
        import numpy as np
        B, S, D = (4, 256, 256)
        DFF = 704
        E, K, R = (8, 2, 16)
        SCALING = 32.0 / 16.0
        key = jax.random.key(seed)
        ks = jax.random.split(key, 12)
        s = lambda k, shape, scale: jax.random.normal(k, shape, dtype=jnp.float32) * scale
        return {'x': s(ks[0], (B, S, D), 1.0), 'Wg': s(ks[1], (DFF, D), 0.02), 'Wu': s(ks[2], (DFF, D), 0.02), 'Wd': s(ks[3], (D, DFF), 0.02), 'Wr': s(ks[4], (E, D), 0.02), 'Ag': s(ks[5], (E, R, D), 0.02), 'Bg': s(ks[6], (E, DFF, R), 0.02), 'Au': s(ks[7], (E, R, D), 0.02), 'Bu': s(ks[8], (E, DFF, R), 0.02), 'Ad': s(ks[9], (E, R, DFF), 0.02), 'Bd': s(ks[10], (E, D, R), 0.02)}
    _L0_ffn_in = _L0_ffn_setup()
    _L0_c = _w((lambda *s: np.random.randn(*s).astype(np.float32) * 0.05)(4, 256))
    _L0_wmod = _w((lambda *s: np.random.randn(*s).astype(np.float32) * 0.05)(256, 6 * 256) * 256 ** (-0.5))
    _d = {'L0_attn_x': _L0_attn_in['x'], 'L0_attn_qkv': _L0_attn_in['qkv'], 'L0_attn_o_proj': _L0_attn_in['o_proj'], 'L0_attn_gamma': _L0_attn_in['gamma'], 'L0_attn_beta': _L0_attn_in['beta'], 'L0_ffn_Wg': _L0_ffn_in['Wg'], 'L0_ffn_Wu': _L0_ffn_in['Wu'], 'L0_ffn_Wd': _L0_ffn_in['Wd'], 'L0_ffn_Wr': _L0_ffn_in['Wr'], 'L0_ffn_Ag': _L0_ffn_in['Ag'], 'L0_ffn_Bg': _L0_ffn_in['Bg'], 'L0_ffn_Au': _L0_ffn_in['Au'], 'L0_ffn_Bu': _L0_ffn_in['Bu'], 'L0_ffn_Ad': _L0_ffn_in['Ad'], 'L0_ffn_Bd': _L0_ffn_in['Bd'], 'L0_c': _L0_c, 'L0_wmod': _L0_wmod}
    _x0 = _d['L0_attn_x']
    _d['L0_attn_x'] = jax.random.normal(jax.random.fold_in(jax.random.key(seed), 1), (4, 1024, 256), dtype=_x0.dtype)
    del _x0
    return _d

def reference(L0_attn_x, L0_attn_qkv, L0_attn_o_proj, L0_attn_gamma, L0_attn_beta, L0_ffn_Wg, L0_ffn_Wu, L0_ffn_Wd, L0_ffn_Wr, L0_ffn_Ag, L0_ffn_Bg, L0_ffn_Au, L0_ffn_Bu, L0_ffn_Ad, L0_ffn_Bd, L0_c, L0_wmod):

    def _L0_attn_ref(x, qkv, o_proj, gamma, beta):
        import jax, jax.numpy as jnp
        import numpy as np
        HIDDEN = 256
        KEY = 256
        EPS = 1e-05
        residual = x
        mu = jnp.mean(x, axis=-1, keepdims=True)
        var = jnp.mean((x - mu) ** 2, axis=-1, keepdims=True)
        x_norm = (x - mu) / jnp.sqrt(var + EPS) * gamma + beta
        q = x_norm @ qkv[:, :KEY]
        k = x_norm @ qkv[:, KEY:2 * KEY]
        v = x_norm @ qkv[:, 2 * KEY:]
        scale = 1.0 / jnp.sqrt(jnp.float32(KEY))
        scores = jnp.einsum('bsk,btk->bst', q, k) * scale
        S_len = x.shape[1]
        causal = jnp.tril(jnp.ones((S_len, S_len), dtype=bool))
        scores = jnp.where(causal[None], scores, -jnp.inf)
        attn = jax.nn.softmax(scores, axis=-1)
        out = attn @ v
        out = out @ o_proj
        return out + residual

    def _L0_ffn_ref(x, Wg, Wu, Wd, Wr, Ag, Bg, Au, Bu, Ad, Bd):
        import jax, jax.numpy as jnp
        import numpy as np
        B, S, D = (4, 256, 256)
        DFF = 704
        E, K, R = (8, 2, 16)
        SCALING = 32.0 / 16.0
        b, s, d = x.shape
        xf = x.reshape(-1, d)
        gate_base = xf @ Wg.T
        up_base = xf @ Wu.T
        base_out = jax.nn.silu(gate_base) * up_base @ Wd.T
        router_logits = xf @ Wr.T
        probs = jax.nn.softmax(router_logits.astype(jnp.float32), axis=-1)
        topw, topi = jax.lax.top_k(probs, K)
        topw = topw.astype(x.dtype)
        expert_w = jnp.sum(jax.nn.one_hot(topi, E, dtype=x.dtype) * topw[..., None], axis=1)

        def expert_step(acc, params):
            Ag_e, Bg_e, Au_e, Bu_e, Ad_e, Bd_e, we = params
            g_lora = xf @ Ag_e.T @ Bg_e.T * SCALING
            u_lora = xf @ Au_e.T @ Bu_e.T * SCALING
            h = jax.nn.silu(gate_base + g_lora) * (up_base + u_lora)
            d_delta = h @ Ad_e.T @ Bd_e.T * SCALING
            return (acc + d_delta * we[:, None], None)
        acc0 = jnp.zeros_like(base_out)
        acc, _ = jax.lax.scan(expert_step, acc0, (Ag, Bg, Au, Bu, Ad, Bd, expert_w.T))
        return (base_out + acc).reshape(b, s, d)
    x = L0_attn_x
    mod = (_silu(L0_c) @ L0_wmod).reshape(L0_c.shape[0], 6, 1, -1)
    sa, ca, ga, sb, cb, gb = (mod[:, 0], mod[:, 1], mod[:, 2], mod[:, 3], mod[:, 4], mod[:, 5])
    ga = (2 * (ga >= 0) - 1) * jnp.maximum(jnp.abs(ga), 0.25)
    gb = (2 * (gb >= 0) - 1) * jnp.maximum(jnp.abs(gb), 0.25)
    h = _layernorm(x, axis=-1) * (1 + ca) + sa
    x = x + ga * _L0_attn_ref(h, L0_attn_qkv, L0_attn_o_proj, L0_attn_gamma, L0_attn_beta)
    h = _layernorm(x, axis=-1) * (1 + cb) + sb
    x = x + gb * _L0_ffn_ref(h, L0_ffn_Wg, L0_ffn_Wu, L0_ffn_Wd, L0_ffn_Wr, L0_ffn_Ag, L0_ffn_Bg, L0_ffn_Au, L0_ffn_Bu, L0_ffn_Ad, L0_ffn_Bd)
    return x

_drawn_inputs = setup_inputs


def setup_inputs(seed=0):
    import zlib

    import numpy as np

    out = dict(_drawn_inputs(seed))
    spreads = {'L0_attn_gamma': (1.0, 0.6), 'L0_attn_beta': (0.0, 0.8)}
    factors = {'L0_attn_qkv': 5.337,
     'L0_attn_o_proj': 5.523,
     'L0_ffn_Wg': 7.993,
     'L0_ffn_Wu': 7.641,
     'L0_ffn_Wd': 7.553,
     'L0_ffn_Wr': 8.0,
     'L0_ffn_Ag': 8.0,
     'L0_ffn_Bg': 8.0,
     'L0_ffn_Au': 8.0,
     'L0_ffn_Bu': 8.0,
     'L0_ffn_Ad': 8.0,
     'L0_ffn_Bd': 8.0}
    for name, (base, spread) in spreads.items():
        noise = np.random.default_rng([zlib.crc32(name.encode()), seed]).standard_normal(out[name].shape)
        drawn = base * np.exp(spread * noise) if base else spread * noise
        out[name] = jnp.asarray(drawn.astype(out[name].dtype))
    for name, factor in factors.items():
        out[name] = (out[name] * factor).astype(out[name].dtype)
    return out
```

```python
import concourse.bass as bass
from concourse import mybir
from contextlib import ExitStack


class Signal:

    def __init__(self, sem, per_batch, credit=0):
        self.sem, self.n, self.credit = sem, per_batch, credit

    def at(self, b, k):
        return b * self.n + (self.credit + k + 1)


def adaln_attention_moe_lora(nc, x, qkv, o_proj, gamma, beta, Wg, Wu, Wd, Wr, Ag, Bg, Au, Bu, Ad, Bd, c, wmod, out):
    fp32 = mybir.dt.float32
    f32r = mybir.dt.float32r
    bf16 = mybir.dt.bfloat16
    i32 = mybir.dt.int32
    u32 = mybir.dt.uint32
    ALU = mybir.AluOpType
    ACT = mybir.ActivationFunctionType
    X = mybir.AxisListType.X

    P = 128
    B, S, D = x.shape
    F = Wg.shape[1]
    E = Wr.shape[1]
    ER = Ag.shape[1]
    R = ER // E
    KT = D // P
    NT = S // P
    CH = 512
    NC = S // CH
    TC = CH // P
    FT = -(-F // P)
    FP = FT * P
    FREST = F - (FT - 1) * P
    GROUPS = FT // 2
    UPC = 3 * FT
    RING = 8
    EPS = 1e-5
    SCALING = 2.0
    SCORE_SCALE = 1.0 / 16.0
    MASKED = -1e30
    NPT = sum(-(-(i + 1) // TC) for i in range(NT))
    assert ER == P and KT == 2 and D == 256 and FT % 2 == 0 and TC == 4 and NC == 2

    ctx = ExitStack()
    with ctx:
        def sb(name, shape, dt, where=ctx):
            return where.enter_context(nc.sbuf_tensor(name, shape, dt))

        def sem(name):
            return ctx.enter_context(nc.semaphore(name))

        wqk = [sb(f"wqk_{h}", [P, KT, D], f32r) for h in ("hi", "lo")]
        wvo = [sb(f"wvo_{h}", [P, KT, D], f32r) for h in ("hi", "lo")]
        wgT = [sb(f"wgT_{h}", [P, KT, FP], f32r) for h in ("hi", "lo")]
        wuT = [sb(f"wuT_{h}", [P, KT, FP], f32r) for h in ("hi", "lo")]
        aT = [sb(f"aT_{h}", [P, 2, KT, ER], f32r) for h in ("hi", "lo")]
        wrT = [sb(f"wrT_{h}", [P, KT, E], f32r) for h in ("hi", "lo")]
        bgT = [sb(f"bgT_{h}", [P, FP], f32r) for h in ("hi", "lo")]
        buT = [sb(f"buT_{h}", [P, FP], f32r) for h in ("hi", "lo")]
        wdT = [sb(f"wdT_{h}", [P, FT, D], f32r) for h in ("hi", "lo")]
        adT = [sb(f"adT_{h}", [P, FT, ER], f32r) for h in ("hi", "lo")]
        bdT = [sb(f"bdT_{h}", [P, D], f32r) for h in ("hi", "lo")]
        ident = sb("ident", [P, P], fp32)
        identb = sb("identb", [P, P], bf16)
        causal = sb("causal", [P, P], bf16)
        iota8 = sb("iota8", [P, E], fp32)
        gammaT = sb("gammaT", [P, KT], fp32)
        betaT = sb("betaT", [P, KT], fp32)
        cT = sb("cT", [P, KT, B], fp32)
        scT = sb("scT", [P, KT, B], fp32)
        modT = sb("modT", [P, 2, KT, B], fp32)
        SA, CA, GA, GB = range(4)
        bc = sb("bc", [P, B, 4, D], fp32)

        xs = sb("xs", [P, NT, D], fp32)
        zb = sb("zb", [P, NT, D], fp32)
        xr = sb("xr", [P, NT, D], fp32)
        xT = [sb(f"xT_{h}", [P, 3, KT, CH], f32r) for h in ("hi", "lo")]
        tr_full = sb("tr_full", [P, 2, CH], fp32)
        t_full = sb("t_full", [P, 2, CH], fp32)
        t_mask = sb("t_mask", [P, CH], fp32)
        y_gb = t_mask[:, :].rearrange("p (t d) -> p t d", d=D)
        wmask = sb("wmask", [P, 2, CH], fp32)
        gated = sb("gated", [P, 2, D], fp32)

        stat = sb("stat", [P, NT, 6], fp32)
        mv = sb("mv", [P, NT, 2], fp32)
        rstd = sb("rstd", [P, NT], fp32)
        nr_v = sb("nr_v", [P, NT], fp32)
        nr_a = sb("nr_a", [P, NT], fp32)
        nr_i = sb("nr_i", [P, NT], i32)
        rowmax = sb("rowmax", [P, NT], fp32)
        rowsum = sb("rowsum", [P, NT], fp32)
        rinv = sb("rinv", [P, NT], fp32)
        lg = sb("lg", [P, TC, E], fp32)
        pr = sb("pr", [P, TC, E], fp32)
        lmax = sb("lmax", [P, TC], fp32)
        lsum = sb("lsum", [P, TC], fp32)
        top = sb("top", [P, TC, 8], fp32)
        topi = sb("topi", [P, TC, 8], u32)
        topf = sb("topf", [P, TC, 8], fp32)
        onehot = sb("onehot", [P, 2, TC, E], fp32)
        pick = sb("pick", [P, 4, TC, E], fp32)

        stage_ctx = ExitStack()
        with stage_ctx:
            def st(name, shape):
                return sb(name, shape, fp32, stage_ctx)
            s_qkvT = st("s_qkvT", [P, 3, KT, D])
            s_o = st("s_o", [P, KT, D])
            s_mod = st("s_mod", [P, KT, 6 * D])
            s_wg = st("s_wg", [P, KT, F])
            s_wu = st("s_wu", [P, KT, F])
            s_wd = st("s_wd", [P, FT, D])
            s_a = st("s_a", [P, 2, KT, ER])
            s_wr = st("s_wr", [P, KT, E])
            s_bd = st("s_bd", [P, D])
        s_scb = tr_full[:, :, :].rearrange("p k (b n) -> p k b n", n=P)
        s_sgn = t_full[:, 0, :].rearrange("p (t d) -> p t d", d=D)
        s_abs = t_full[:, 1, :].rearrange("p (t d) -> p t d", d=D)
        s_bg = xr[:, 0:3, :].rearrange("p i d -> p (i d)")[:, 0:F]
        s_bu = xr[:, 3:6, :].rearrange("p i d -> p (i d)")[:, 0:F]
        s_ad = wmask[:, :, :].rearrange("p s n -> p (s n)")[:, 0:FT * ER].rearrange("p (j e) -> p j e", e=ER)

        at_ctx = ExitStack()
        with at_ctx:
            qT = [sb(f"qT_{h}", [P, KT, S], f32r, at_ctx) for h in ("hi", "lo")]
            vv = [sb(f"vv_{h}", [P, NT, D], f32r, at_ctx) for h in ("hi", "lo")]
            pT = [sb(f"pT_{h}", [P, 2, NT, P], f32r, at_ctx) for h in ("hi", "lo")]
            probs = sb("probs", [P, 2, S], fp32, at_ctx)
        mask_ctx = ExitStack()
        with mask_ctx:
            sb("ring_front", [P, RING - 4, CH], f32r, mask_ctx)
            pick_er = sb("pick_er", [P, 4, TC, ER], fp32, mask_ctx)
        ring = [sb(f"ring_{h}", [P, RING, CH], f32r) for h in ("hi", "lo")]
        tm = [sb(f"tm_{h}", [P, 4, CH], f32r) for h in ("hi", "lo")]
        act_s = sb("act_s", [P, 2, CH], fp32)
        hid = sb("hid", [P, 2, CH], fp32)

        ps = ctx.enter_context(nc.psum_tensor("ps", [P, 8, 512], fp32))

        consts_made = sem("consts_made")
        pads_made = sem("pads_made")
        loaded = {k: sem("ld_" + k) for k in ("qkv", "o", "mod", "c", "ln", "wg", "wu", "wd", "a", "wr", "bg", "bu", "ad", "bd")}
        sc_ready = sem("sc_ready")
        scb_ready = sem("scb_ready")
        mod_ready = sem("mod_ready")
        mod_copied = sem("mod_copied")
        gates_ready = sem("gates_ready")
        product_ready = sem("product_ready")
        product_hi = sem("product_hi")
        product_lo = sem("product_lo")
        weight_hi = sem("weight_hi")
        weight_lo = sem("weight_lo")
        x_loaded = sem("x_loaded")
        stored = sem("stored")
        vstep = sem("vstep")
        unwaited = sem("unwaited")

        def signal(name, per_batch, credit=0):
            return Signal(sem(name), per_batch, credit)
        z_ready = signal("z_ready", NT)
        t_gated = signal("t_gated", NT)
        r_ready = signal("r_ready", NT)
        TR = 2 * KT * NC
        transposed = signal("transposed", TR)
        tr_full_ready = signal("tr_full_ready", TR)
        tr_hi = signal("tr_hi", TR)
        tr_lo = signal("tr_lo", TR)
        proj_ready = signal("proj_ready", 8)
        proj_hi = signal("proj_hi", 8)
        proj_lo = signal("proj_lo", 8)
        scores_ready = signal("scores_ready", NT)
        rowmax_ready = signal("rowmax_ready", NT)
        probs_ready = signal("probs_ready", NT)
        pt_ready = signal("pt_ready", NPT)
        pt_hi = signal("pt_hi", NPT)
        pt_lo = signal("pt_lo", NPT)
        pv_ready = signal("pv_ready", NT)
        x1_ready = signal("x1_ready", NT)
        z2_ready = signal("z2_ready", NT)
        logits_ready = signal("logits_ready", NC)
        shifted_ready = signal("shifted_ready", NC)
        rexp_ready = signal("rexp_ready", NC)
        pick_ready = signal("pick_ready", 2 * NC)
        masks_ready = signal("masks_ready", 4 * NC)
        wmask_ready = signal("wmask_ready", 2 * NC)
        t_ready = signal("t_ready", 2 * NC)
        t_copied = signal("t_copied", 2 * NC)
        t_masked = signal("t_masked", 4 * NC)
        tm_hi = signal("tm_hi", 4 * NC)
        tm_lo = signal("tm_lo", 4 * NC)
        UPB = UPC * NC
        gate_up_ready = signal("gate_up_ready", UPB)
        silu_ready = signal("silu_ready", UPB)
        h_ready = signal("h_ready", UPB, credit=1)
        h_hi = signal("h_hi", UPB)
        h_lo = signal("h_lo", UPB)
        h_used = signal("h_used", UPB)
        dsum_ready = signal("dsum_ready", NC, credit=1)
        dsum_hi = signal("dsum_hi", NC)
        dsum_lo = signal("dsum_lo", NC)
        y_ready = signal("y_ready", NT // 2)
        y_scaled = signal("y_scaled", NT, credit=1)
        out_ready = signal("out_ready", NT)

        def unit(ci, g, slot, a):
            return ci * UPC + g * 6 + slot * 2 + a

        def down_order(g):
            slots = (0, 1, 2) if g < GROUPS - 1 else (1, 2, 0)
            return [(slot, a) for slot in slots for a in range(2)]

        def down_position(n):
            g, rest = n % UPC // 6, n % 6
            return n - rest + down_order(g).index((rest // 2, rest % 2))

        def pt_banks(i):
            first = sum(-(-(j + 1) // TC) for j in range(i))
            return [(first + q, q * TC, min(TC, i + 1 - q * TC)) for q in range(-(-(i + 1) // TC))]

        SPLITS = [("wg", s_wg[:, k, :], [w[:, k, 0:F] for w in wgT]) for k in range(KT)]
        SPLITS += [("wu", s_wu[:, k, :], [w[:, k, 0:F] for w in wuT]) for k in range(KT)]
        SPLITS += [("wr", s_wr[:, :, :], [w[:, :, :] for w in wrT]),
                   ("a", s_a[:, :, :, :].rearrange("p g k e -> p (g k e)"), [w[:, :, :, :].rearrange("p g k e -> p (g k e)") for w in aT]),
                   ("bg", s_bg, [w[:, 0:F] for w in bgT]), ("bu", s_bu, [w[:, 0:F] for w in buT]),
                   ("wd", s_wd[:, 0:FT - 1, :], [w[:, 0:FT - 1, :] for w in wdT]),
                   ("wd", s_wd[0:FREST, FT - 1, :], [w[0:FREST, FT - 1, :] for w in wdT]),
                   ("ad", s_ad[:, 0:FT - 1, :], [w[:, 0:FT - 1, :] for w in adT]),
                   ("ad", s_ad[0:FREST, FT - 1, :], [w[0:FREST, FT - 1, :] for w in adT]),
                   ("bd", s_bd[:, :], [w[:, :] for w in bdT])]
        LOADS = {"wd": 2, "ad": 2, "a": 2, "ln": 2}

        block = ctx.enter_context(nc.Block())

        def batches(eng, body):
            with eng.Fori(0, B - 1) as b:
                body(b, False)
            body(B - 1, True)

        @block.sync
        def _(sp):
            sp.sem_inc(stored, 16)

            def load(key, dst, src):
                sp.dma_start(dst, src).then_inc(loaded[key], 16)
            load("c", cT[:, :, :], c.rearrange("(k p) b -> p k b", p=P))
            load("mod", s_mod[:, :, :], wmod.rearrange("(k p) n -> p k n", p=P))
            sp.dma_start(xs[:, :, :], x[0].rearrange("(i p) d -> p i d", p=P)).then_inc(x_loaded, 16)
            load("qkv", s_qkvT[:, :, :, :].rearrange("p w k d -> p (w k) d"), qkv.rearrange("(k p) d -> p k d", p=P))
            load("o", s_o[:, :, :], o_proj.rearrange("(k p) n -> p k n", p=P))
            load("ln", gammaT[:, :], gamma)
            load("ln", betaT[:, :], beta)
            load("wg", s_wg[:, :, :], Wg.rearrange("(k p) f -> p k f", p=P))
            load("wu", s_wu[:, :, :], Wu.rearrange("(k p) f -> p k f", p=P))
            load("wr", s_wr[:, :, :], Wr.rearrange("(k p) e -> p k e", p=P))
            load("a", s_a[:, 0, :, :], Ag.rearrange("(k p) e -> p k e", p=P))
            load("a", s_a[:, 1, :, :], Au.rearrange("(k p) e -> p k e", p=P))
            load("bg", s_bg, Bg)
            load("bu", s_bu, Bu)
            for key, dst, src in (("wd", s_wd, Wd), ("ad", s_ad, Ad)):
                load(key, dst[:, 0:FT - 1, :], src[0:(FT - 1) * P, :].rearrange("(j p) n -> p j n", p=P))
                load(key, dst[0:FREST, FT - 1, :], src[(FT - 1) * P:F, :])
            load("bd", s_bd[:, :], Bd)

            def body(b, last):
                if not last:
                    sp.wait_ge(x1_ready.sem, x1_ready.at(b, NT - 1))
                    sp.dma_start(xs[:, :, :], x[b + 1].rearrange("(i p) d -> p i d", p=P)).then_inc(x_loaded, 16)
                for ci in range(NC):
                    sp.wait_ge(out_ready.sem, out_ready.at(b, ci * TC + TC - 1))
                    sp.dma_start(out[b, ci * CH:(ci + 1) * CH, :].rearrange("(i p) d -> p i d", p=P),
                                 xr[:, ci * TC:(ci + 1) * TC, :]).then_inc(stored, 16)
            batches(sp, body)
            sp.wait_ge(stored, 16 + 16 * NC * B)

        @block.gpsimd
        def _(pool):
            pool.memset(ident[:, :], 0.0).then_inc(consts_made, 1)
            pool.memset(causal[:, :], 0.0).then_inc(consts_made, 1)
            pool.wait_ge(consts_made, 2)
            pool.affine_select(out=ident[:, :], in_=ident[:, :], compare_op=ALU.not_equal, fill=1.0, base=0,
                               pattern=[[-1, P]], channel_multiplier=1).then_inc(consts_made, 1)
            pool.affine_select(out=causal[:, :], in_=causal[:, :], compare_op=ALU.is_ge, fill=MASKED, base=0,
                               pattern=[[-1, P]], channel_multiplier=1).then_inc(consts_made, 1)
            pool.iota(iota8[:, :], pattern=[[1, E]], base=0, channel_multiplier=0,
                      allow_small_or_imprecise_dtypes=True).then_inc(consts_made, 1)
            pool.wait_ge(consts_made, 5)
            pool.tensor_copy(identb[:, :], ident[:, :]).then_inc(consts_made, 1)
            for w in wgT + wuT:
                pool.memset(w[:, :, F:FP].bitcast(fp32), 0.0).then_inc(pads_made, 1)
            for w in bgT + buT:
                pool.memset(w[:, F:FP].bitcast(fp32), 0.0).then_inc(pads_made, 1)
            pool.wait_ge(pads_made, 8)
            for w in wdT + adT:
                pool.memset(w[FREST:P, FT - 1, :].bitcast(fp32), 0.0).then_inc(pads_made, 1)
            pool.wait_ge(pads_made, 12)

            def residual(b, i):
                pool.wait_ge(t_gated.sem, t_gated.at(b, i))
                pool.tensor_add(xs[:, i, :], xs[:, i, :], gated[:, i % 2, :]).then_inc(r_ready.sem, 1)

            def tr_low(b, q, dst):
                pool.wait_ge(tr_hi.sem, tr_hi.at(b, q))
                pool.tensor_sub(dst[1], tr_full[:, q % 2, :], dst[0].bitcast(fp32)).then_inc(tr_lo.sem, 1)

            def attention_inputs(b, q):
                n, k = divmod(q, KT)
                tr_low(b, q, [t[:, n, k, :] for t in xT])

            def hid_low(b, n):
                pool.wait_ge(h_hi.sem, h_hi.at(b, n))
                pool.tensor_sub(ring[1][:, n % RING, :], hid[:, n % 2, :],
                                ring[0][:, n % RING, :].bitcast(fp32)).then_inc(h_lo.sem, 1)

            for i in range(NT):
                residual(0, i)
            for q in range(KT * NC):
                attention_inputs(0, q)

            def body(b, last):
                for ci in range(NC):
                    if ci == 0:
                        for k in range(KT):
                            tr_low(b, KT * NC + k, [t[:, 0, k, :] for t in xT])
                    for m in range(4):
                        pool.wait_ge(tm_hi.sem, tm_hi.at(b, ci * 4 + m))
                        pool.tensor_sub(tm[1][:, m, :], t_mask[:, :], tm[0][:, m, :].bitcast(fp32)).then_inc(tm_lo.sem, 1)
                        if m < 2:
                            hid_low(b, ci * UPC + m)
                    for g in range(GROUPS):
                        for r in range(6):
                            n = unit(ci, g, 0, 0) + r
                            if n - ci * UPC >= 2:
                                hid_low(b, n)
                            if not last and ci == 0 and g >= 1:
                                s = (g - 1) * 6 + r
                                if s >= 4:
                                    residual(b + 1, s - 4)
                        if g == 0 and ci == 0:
                            for k in range(KT):
                                tr_low(b, KT * NC + KT + k, [t[:, 2, k, :] for t in xT])
                        if g == 0 and ci == 1 and not last:
                            for q in range(KT * NC):
                                attention_inputs(b + 1, q)
                    for t in range(TC):
                        i = ci * TC + t
                        pool.wait_ge(y_scaled.sem, y_scaled.at(b, i))
                        pool.tensor_add(xr[:, i, :], xr[:, i, :], y_gb[:, t % 2, :]).then_inc(out_ready.sem, 1)
            batches(pool, body)

        @block.scalar
        def _(act):
            act.wait_ge(loaded["c"], 16)
            nc.scalar.activation(scT[:, :, :], cT[:, :, :], ACT.Silu).then_inc(sc_ready, 1)
            for b in range(B):
                for h in range(2):
                    act.wait_ge(mod_ready, 2 * b + h + 1)
                    nc.scalar.activation(bc[:, b, 2 * h:2 * h + 2, :].rearrange("p t d -> p (t d)"),
                                         ps[:, (2 * b + h) % 4, :], ACT.Copy).then_inc(mod_copied, 1)
            act.wait_ge(mod_ready, 2 * B + 1)
            nc.scalar.activation(modT[:, :, :, :].rearrange("p t k b -> p (t k b)"), ps[:, 0, 0:2 * KT * B], ACT.Copy).then_inc(mod_copied, 1)

            def tr_high(b, q, dst):
                act.wait_ge(tr_full_ready.sem, tr_full_ready.at(b, q))
                nc.scalar.activation(dst, tr_full[:, q % 2, :], ACT.Copy).then_inc(tr_hi.sem, 1)

            for j, (w, scale) in enumerate(((wqk, SCORE_SCALE), (wvo, 1.0))):
                act.wait_ge(product_ready, j + 1)
                nc.scalar.activation(w[0][:, :, :].rearrange("p k d -> p (k d)"), ps[:, 4 + j, :], ACT.Copy,
                                     scale=scale).then_inc(product_hi, 1)
            for key, src, (hi, _) in SPLITS:
                act.wait_ge(loaded[key], 16 * LOADS.get(key, 1))
                nc.scalar.activation(hi, src, ACT.Copy).then_inc(weight_hi, 1)
            for q in range(KT * NC):
                tr_high(0, q, xT[0][:, q // KT, q % KT, :])

            def body(b, last):
                for j in range(8):
                    act.wait_ge(proj_ready.sem, proj_ready.at(b, j))
                    if j < 4:
                        n, m = divmod(j, KT)
                        nc.scalar.activation(qT[0][:, m, n * CH:(n + 1) * CH], ps[:, 4 + j, :], ACT.Copy).then_inc(proj_hi.sem, 1)
                    else:
                        i = 2 * (j - 4)
                        nc.scalar.activation(vv[0][:, i:i + 2, :].rearrange("p i d -> p (i d)"), ps[:, j - 4, :], ACT.Copy).then_inc(proj_hi.sem, 1)
                for i in range(NT + 1):
                    if i < NT:
                        w = (i + 1) * P
                        act.wait_ge(rowmax_ready.sem, rowmax_ready.at(b, i))
                        if i >= 2:
                            act.wait_ge(pt_ready.sem, pt_ready.at(b, pt_banks(i - 2)[-1][0]))
                        banks = ps[:, 2 * (i % 2):2 * (i % 2) + 2, :].rearrange("p n s -> p (n s)")
                        nc.scalar.activation(probs[:, i % 2, 0:w], banks[:, 0:w], ACT.Exp, bias=rowmax[:, i:i + 1],
                                             accum_out=rowsum[:, i:i + 1]).then_inc(probs_ready.sem, 1)
                    if i >= 1:
                        t = i - 1
                        for e, j0, nj in pt_banks(t):
                            act.wait_ge(pt_ready.sem, pt_ready.at(b, e))
                            if t >= 2:
                                act.wait_ge(pv_ready.sem, pv_ready.at(b, t - 2))
                            nc.scalar.activation(pT[0][:, t % 2, j0:j0 + nj, :].rearrange("p j s -> p (j s)"),
                                                 ps[:, 4 + e % 2, 0:nj * P], ACT.Copy).then_inc(pt_hi.sem, 1)
                for ci in range(NC):
                    if ci == 0:
                        for k in range(KT):
                            tr_high(b, KT * NC + k, xT[0][:, 0, k, :])
                    act.wait_ge(shifted_ready.sem, shifted_ready.at(b, ci))
                    nc.scalar.activation(pr[:, :, :], lg[:, :, :], ACT.Exp).then_inc(rexp_ready.sem, 1)

                    def silu(n):
                        act.wait_ge(gate_up_ready.sem, gate_up_ready.at(b, n))
                        if n >= 2:
                            act.wait_ge(h_ready.sem, h_ready.at(b, n - 2))
                        nc.scalar.activation(act_s[:, n % 2, :], ps[:, 2 * (n % 2), :], ACT.Silu).then_inc(silu_ready.sem, 1)

                    def high(n):
                        act.wait_ge(h_ready.sem, h_ready.at(b, n))
                        if n >= RING:
                            act.wait_ge(h_used.sem, h_used.at(b, down_position(n - RING)))
                        nc.scalar.activation(ring[0][:, n % RING, :], hid[:, n % 2, :], ACT.Copy).then_inc(h_hi.sem, 1)

                    n0 = ci * UPC
                    silu(n0)
                    for g in range(2):
                        act.wait_ge(t_ready.sem, t_ready.at(b, ci * 2 + g))
                        nc.scalar.activation(t_full[:, g, :], ps[:, 4 + g, :], ACT.Copy).then_inc(t_copied.sem, 1)
                    silu(n0 + 1)
                    for m in range(4):
                        act.wait_ge(t_masked.sem, t_masked.at(b, ci * 4 + m))
                        nc.scalar.activation(tm[0][:, m, :], t_mask[:, :], ACT.Copy).then_inc(tm_hi.sem, 1)
                        if m < 2:
                            high(n0 + m)
                    for m in range(2):
                        act.wait_ge(masks_ready.sem, masks_ready.at(b, ci * 4 + 2 + m))
                        nc.scalar.activation(wmask[:, m, :], ps[:, 4 + m, :], ACT.Copy).then_inc(wmask_ready.sem, 1)
                    for n in range(n0 + 2, n0 + UPC):
                        silu(n)
                        if n - 1 >= n0 + 2:
                            high(n - 1)
                        if n == n0 + 6:
                            if ci == 0:
                                for k in range(KT):
                                    tr_high(b, KT * NC + KT + k, xT[0][:, 2, k, :])
                            elif not last:
                                for q in range(KT * NC):
                                    tr_high(b + 1, q, xT[0][:, q // KT, q % KT, :])
                    high(n0 + UPC - 1)
                    act.wait_ge(dsum_ready.sem, dsum_ready.at(b, ci))
                    nc.scalar.activation(tm[0][:, 0, :], wmask[:, 0, :], ACT.Copy).then_inc(dsum_hi.sem, 1)
            batches(act, body)

        @block.vector
        def _(dve):
            V = nc.vector
            for s in (h_ready, dsum_ready, y_scaled):
                dve.sem_inc(s.sem, 1)
            steps = [0, 0]

            def link(ins):
                steps[1] += 1
                ins.then_inc(vstep, 1)
                dve.wait_ge(vstep, steps[0] + steps[1])

            def link_apart(ins):
                link(ins)
                dve.sem_inc(unwaited, 1)

            RSQRT_STEPS = 3 + 3 * 4
            VSTEPS = NT * 4 + NC * RSQRT_STEPS + NC * 10 + NC * 2 + NT * (2 + 4) + 2 * RSQRT_STEPS

            def rsqrt(lo, n):
                v, a, y = nr_v[:, lo:lo + n], nr_a[:, lo:lo + n], rstd[:, lo:lo + n]
                link(V.tensor_scalar_add(v, mv[:, lo:lo + n, 1], EPS))
                link(V.tensor_scalar(nr_i[:, lo:lo + n], v.bitcast(i32), 1, None, ALU.logical_shift_right))
                link(V.tensor_scalar(y.bitcast(i32), nr_i[:, lo:lo + n], -1.0, float(0x5f3759df), ALU.mult, ALU.add))
                for _ in range(4):
                    link(V.tensor_mul(a, y, y))
                    link(V.scalar_tensor_tensor(a, a, -0.5, v, ALU.mult, ALU.mult))
                    link(V.scalar_tensor_tensor(y, a, 1.5, y, ALU.add, ALU.mult))

            def ln1_x_stats(i):
                link_apart(V.bn_stats(stat[:, i, :], xs[:, i, :]))
                link(V.bn_aggr(mv[:, i, :], stat[:, i, :]))

            def ln1_h(b, i):
                link(V.scalar_tensor_tensor(zb[:, i, :], xs[:, i, :], mv[:, i, 0:1], bc[:, b, CA, :], ALU.subtract, ALU.mult))
                link(V.scalar_tensor_tensor(zb[:, i, :], zb[:, i, :], rstd[:, i:i + 1], bc[:, b, SA, :], ALU.mult, ALU.add))
                if i >= 2:
                    dve.wait_ge(r_ready.sem, r_ready.at(b, i - 2))
                V.tensor_mul(gated[:, i % 2, :], zb[:, i, :], bc[:, b, GA, :]).then_inc(t_gated.sem, 1)
                link_apart(V.bn_stats(stat[:, i, :], zb[:, i, :]))
                link(V.bn_aggr(mv[:, i, :], stat[:, i, :]))

            def normalise(i, src, dst, sig):
                V.tensor_scalar(dst[:, i, :], src[:, i, :], mv[:, i, 0:1], rstd[:, i:i + 1], ALU.subtract, ALU.mult).then_inc(sig.sem, 1)

            def tr_scale(b, q, bank, scale, bias):
                dve.wait_ge(transposed.sem, transposed.at(b, q))
                if not (isinstance(b, int) and b == 0 and q < 2):
                    dve.wait_ge(tr_lo.sem, tr_lo.at(b, q - 2))
                V.tensor_scalar(tr_full[:, q % 2, :], ps[:, bank, :], scale, bias, ALU.mult, ALU.add).then_inc(tr_full_ready.sem, 1)

            def attention_scale(b, q):
                k = q % KT
                tr_scale(b, q, 6 + q % 2, gammaT[:, k:k + 1], betaT[:, k:k + 1])

            dve.wait_ge(sc_ready, 1)
            V.tensor_copy(s_scb[:, :, :, :].rearrange("p k b n -> p (k b) n"),
                          scT[:, :, :].rearrange("p k b -> p (k b)").unsqueeze(2).to_broadcast([P, KT * B, P])).then_inc(scb_ready, 1)
            for b in range(B):
                dve.wait_ge(mod_copied, 2 * b + 1)
                V.tensor_scalar_add(bc[:, b, CA, :], bc[:, b, CA, :], 1.0).then_inc(gates_ready, 1)
                dve.wait_ge(mod_copied, 2 * b + 2)
                g = bc[:, b, GA:GB + 1, :]
                V.tensor_scalar(s_sgn, g, 0.0, 2.0, ALU.is_ge, ALU.mult)
                link(V.scalar_tensor_tensor(s_abs, g, -1.0, g, ALU.mult, ALU.max))
                link(V.tensor_scalar_max(s_abs, s_abs, 0.25))
                V.scalar_tensor_tensor(g, s_sgn, -1.0, s_abs, ALU.add, ALU.mult).then_inc(gates_ready, 1)
                if b == 0:
                    dve.wait_ge(x_loaded, 16)
                    for i in range(NT):
                        ln1_x_stats(i)
                    rsqrt(0, NT)
                    dve.wait_ge(gates_ready, 2)
                    for i in range(NT):
                        ln1_h(0, i)
                    rsqrt(0, NT)
                    for i in range(NT):
                        normalise(i, zb, zb, z_ready)
                else:
                    dve.wait_ge(gates_ready, 2 * b + 2)
            dve.wait_ge(mod_copied, 2 * B + 1)
            link(V.tensor_scalar_add(modT[:, 1, :, :], modT[:, 1, :, :], 1.0))
            for j, (w, scale) in enumerate(((wqk, SCORE_SCALE), (wvo, 1.0))):
                dve.wait_ge(product_hi, j + 1)
                hi, lo = [t[:, :, :].rearrange("p k d -> p (k d)") for t in w]
                V.scalar_tensor_tensor(lo, ps[:, 4 + j, :], scale, hi.bitcast(fp32), ALU.mult, ALU.subtract).then_inc(product_lo, 1)
            for j, (_, src, (hi, lo)) in enumerate(SPLITS):
                dve.wait_ge(weight_hi, j + 1)
                V.tensor_sub(lo, src, hi.bitcast(fp32)).then_inc(weight_lo, 1)
            dve.wait_ge(loaded["ln"], 32)
            for q in range(KT * NC):
                attention_scale(0, q)
            setup_steps = steps[1]

            def body(b, last):
                steps[0], steps[1] = b * VSTEPS + setup_steps, 0
                for j in range(8):
                    dve.wait_ge(proj_hi.sem, proj_hi.at(b, j))
                    if j < 4:
                        n, m = divmod(j, KT)
                        hi, lo = [t[:, m, n * CH:(n + 1) * CH] for t in qT]
                        V.tensor_sub(lo, ps[:, 4 + j, :], hi.bitcast(fp32)).then_inc(proj_lo.sem, 1)
                    else:
                        i = 2 * (j - 4)
                        hi, lo = [t[:, i:i + 2, :].rearrange("p i d -> p (i d)") for t in vv]
                        V.tensor_sub(lo, ps[:, j - 4, :], hi.bitcast(fp32)).then_inc(proj_lo.sem, 1)
                for i in range(NT + 2):
                    if i < NT:
                        w = (i + 1) * P
                        banks = ps[:, 2 * (i % 2):2 * (i % 2) + 2, :].rearrange("p n s -> p (n s)")
                        dve.wait_ge(scores_ready.sem, scores_ready.at(b, i))
                        V.tensor_reduce(rowmax[:, i:i + 1], banks[:, 0:w], X, ALU.max, negate=True).then_inc(rowmax_ready.sem, 1)
                    if 1 <= i <= NT:
                        t = i - 1
                        for e, j0, nj in pt_banks(t):
                            dve.wait_ge(pt_hi.sem, pt_hi.at(b, e))
                            hi, lo = [p[:, t % 2, j0:j0 + nj, :].rearrange("p j s -> p (j s)") for p in pT]
                            V.tensor_sub(lo, ps[:, 4 + e % 2, 0:nj * P], hi.bitcast(fp32)).then_inc(pt_lo.sem, 1)
                    if i >= 2:
                        t = i - 2
                        dve.wait_ge(pv_ready.sem, pv_ready.at(b, t))
                        link(V.reciprocal(rinv[:, t:t + 1], rowsum[:, t:t + 1]))
                        if t == 0:
                            dve.wait_ge(stored, b * (16 * NC) + 16)
                            dve.wait_ge(r_ready.sem, r_ready.at(b, NT - 1))
                        link(V.scalar_tensor_tensor(xr[:, t, :], ps[:, 6 + t % 2, 0:D], rinv[:, t:t + 1], bc[:, b, GA, :], ALU.mult, ALU.mult))
                        V.tensor_add(xr[:, t, :], xr[:, t, :], xs[:, t, :]).then_inc(x1_ready.sem, 1)
                        dve.wait_ge(x1_ready.sem, x1_ready.at(b, t))
                        link_apart(V.bn_stats(stat[:, t, :], xr[:, t, :]))
                        link(V.bn_aggr(mv[:, t, :], stat[:, t, :]))
                        if t % TC == TC - 1:
                            rsqrt(t - TC + 1, TC)
                            for tt in range(t - TC + 1, t + 1):
                                normalise(tt, xr, zb, z2_ready)
                for ci in range(NC):
                    def ffn_scale(c2, bank0):
                        for k in range(KT):
                            tr_scale(b, KT * NC + c2 * KT + k, bank0 + k, modT[:, 1, k, bass.ds(b, 1)], modT[:, 0, k, bass.ds(b, 1)])
                    if ci == 0:
                        ffn_scale(0, 0)
                    logits = ps[:, 6, 0:TC * E].rearrange("p (t e) -> p t e", e=E)
                    dve.wait_ge(logits_ready.sem, logits_ready.at(b, ci))
                    link(V.tensor_reduce(lmax[:, :], logits, X, ALU.max))
                    V.tensor_sub(lg[:, :, :], logits, lmax[:, :].unsqueeze(2).to_broadcast([P, TC, E])).then_inc(shifted_ready.sem, 1)
                    dve.wait_ge(rexp_ready.sem, rexp_ready.at(b, ci))
                    link(V.tensor_reduce(lsum[:, :], pr[:, :, :], X, ALU.add))
                    link(V.reciprocal(lsum[:, :], lsum[:, :]))
                    link_apart(V.tensor_mul(pr[:, :, :], pr[:, :, :], lsum[:, :].unsqueeze(2).to_broadcast([P, TC, E])))
                    for t in range(TC):
                        last_max = V.max(top[:, t, :], pr[:, t, :])
                    link_apart(last_max)
                    for t in range(TC):
                        last_idx = V.max_index(topi[:, t, :], top[:, t, :], pr[:, t, :])
                    link(last_idx)
                    link(V.tensor_copy(topf[:, :, 0:2], topi[:, :, 0:2]))
                    for s in range(2):
                        last_hot = V.tensor_tensor(onehot[:, s, :, :], iota8[:, :].unsqueeze(1).to_broadcast([P, TC, E]),
                                                   topf[:, :, s:s + 1].to_broadcast([P, TC, E]), ALU.is_equal)
                    link(last_hot)
                    link(V.tensor_sub(pick[:, 1, :, :], onehot[:, 1, :, :], onehot[:, 0, :, :]))
                    V.tensor_scalar_mul(pick[:, 1, :, :], pick[:, 1, :, :], SCALING)
                    V.tensor_scalar_mul(pick[:, 0, :, :], onehot[:, 0, :, :], SCALING)
                    for s in range(2):
                        last_w = V.scalar_tensor_tensor(pick[:, 2 + s, :, :], onehot[:, s, :, :], SCALING,
                                                        top[:, :, s:s + 1].to_broadcast([P, TC, E]), ALU.mult, ALU.mult)
                    link(last_w)
                    for h in range(2):
                        V.tensor_copy(pick_er[:, 2 * h:2 * h + 2, :, :].rearrange("p m t (e r) -> p (m t e) r", r=R),
                                      pick[:, 2 * h:2 * h + 2, :, :].rearrange("p m t e -> p (m t e)").unsqueeze(2)
                                      .to_broadcast([P, 2 * TC * E, R])).then_inc(pick_ready.sem, 1)

                    def hidden(n):
                        dve.wait_ge(silu_ready.sem, silu_ready.at(b, n))
                        if n >= 2:
                            dve.wait_ge(h_lo.sem, h_lo.at(b, n - 2))
                        V.tensor_mul(hid[:, n % 2, :], act_s[:, n % 2, :], ps[:, 2 * (n % 2) + 1, :]).then_inc(h_ready.sem, 1)

                    n0 = ci * UPC
                    hidden(n0)
                    hidden(n0 + 1)
                    for m in range(4):
                        which, g = divmod(m, 2)
                        dve.wait_ge(masks_ready.sem, masks_ready.at(b, ci * 4 + which))
                        dve.wait_ge(t_copied.sem, t_copied.at(b, ci * 2 + g))
                        if m == 0 and ci == 1:
                            dve.wait_ge(out_ready.sem, out_ready.at(b, TC - 1))
                        if m > 0:
                            dve.wait_ge(tm_lo.sem, tm_lo.at(b, ci * 4 + m - 1))
                        V.tensor_mul(t_mask[:, :], t_full[:, g, :], ps[:, 6 + which, :]).then_inc(t_masked.sem, 1)
                    for r in range(2, UPC):
                        hidden(n0 + r)
                        if r == 5:
                            if ci == 0:
                                ffn_scale(1, 6)
                            elif not last:
                                for q in range(KT * NC):
                                    attention_scale(b + 1, q)
                        if not last and ci == 0 and r >= 6:
                            s = r - 6
                            if s == 0:
                                dve.wait_ge(x_loaded, (b + 1) * 16 + 16)
                                dve.wait_ge(transposed.sem, transposed.at(b, TR - 1))
                            if s < 4:
                                ln1_x_stats(2 * s)
                                ln1_x_stats(2 * s + 1)
                                if s == 3:
                                    rsqrt(0, NT)
                            else:
                                ln1_h(b + 1, s - 4)
                    if not last and ci == 0:
                        rsqrt(0, NT)
                        for i in range(NT):
                            normalise(i, zb, zb, z_ready)
                    for s in range(2):
                        dve.wait_ge(wmask_ready.sem, wmask_ready.at(b, ci * 2 + s))
                        dve.wait_ge(h_used.sem, h_used.at(b, down_position(unit(ci, GROUPS - 1, 1 + s, 1))))
                        link(V.tensor_mul(wmask[:, s, :], wmask[:, s, :], ps[:, 4 + s, :]))
                    V.tensor_add(wmask[:, 0, :], wmask[:, 0, :], wmask[:, 1, :]).then_inc(dsum_ready.sem, 1)
                    dve.wait_ge(dsum_hi.sem, dsum_hi.at(b, ci))
                    V.tensor_sub(tm[1][:, 0, :], wmask[:, 0, :], tm[0][:, 0, :].bitcast(fp32)).then_inc(dsum_lo.sem, 1)
                    for t in range(TC):
                        i = ci * TC + t
                        dve.wait_ge(y_ready.sem, y_ready.at(b, i // 2))
                        if t >= 2:
                            dve.wait_ge(out_ready.sem, out_ready.at(b, i - 2))
                        V.tensor_mul(y_gb[:, t % 2, :], ps[:, 6 + t // 2, t % 2 * D:(t % 2 + 1) * D], bc[:, b, GB, :]).then_inc(y_scaled.sem, 1)
                if not last:
                    assert steps[1] == VSTEPS, steps
            batches(dve, body)

        @block.tensor
        def _(pe):
            def mm(o, w, v, start, stop):
                return nc.tensor.matmul(o, w, v, start=start, stop=stop, skip_group_check=True)

            def product(o, w, v, start, stop):
                mm(o, w[0], v[0], start, False)
                mm(o, w[0], v[1], False, False)
                return mm(o, w[1], v[0], False, stop)

            def transpose(o, src, idn):
                return nc.tensor.transpose(o, src, idn)

            pe.wait_ge(loaded["mod"], 16)
            pe.wait_ge(scb_ready, 1)
            for b in range(B):
                for h in range(2):
                    bank = (2 * b + h) % 4
                    if b >= 2:
                        pe.wait_ge(mod_copied, 2 * b + h - 3)
                    for p0, c0, w in (((0, 0, 2 * D),), ((0, 2 * D, D), (D, 5 * D, D)))[h]:
                        for k in range(KT):
                            last_mm = mm(ps[:, bank, p0:p0 + w], s_scb[:, k, b, :], s_mod[:, k, c0:c0 + w], k == 0, k == KT - 1)
                    last_mm.then_inc(mod_ready, 1)
            pe.wait_ge(mod_copied, 2 * B)
            for t in range(2):
                for m in range(KT):
                    o = ps[:, 0, (t * KT + m) * B:(t * KT + m + 1) * B]
                    for k in range(KT):
                        last_mm = mm(o, s_mod[:, k, (3 + t) * D + m * P:(3 + t) * D + (m + 1) * P], scT[:, k, :], k == 0, k == KT - 1)
            last_mm.then_inc(mod_ready, 1)
            pe.wait_ge(loaded["qkv"], 16)
            pe.wait_ge(loaded["o"], 16)
            for j, (left, right) in enumerate(((0, s_qkvT[:, 1, :, :]), (2, s_o))):
                for d in range(KT):
                    for k in range(KT):
                        last_mm = mm(ps[:, 4 + j, d * D:(d + 1) * D], s_qkvT[:, left, k, d * P:(d + 1) * P], right[:, k, :],
                                     k == 0, k == KT - 1)
                last_mm.then_inc(product_ready, 1)
            pe.wait_ge(consts_made, 6)

            def transposes(b, q, bank, k, tiles):
                for t, i in enumerate(tiles):
                    last = transpose(ps[:, bank, t * P:(t + 1) * P], zb[:, i, k * P:(k + 1) * P], ident[:, :])
                last.then_inc(transposed.sem, 1)

            def attention_transposes(b, in_setup):
                for q in range(KT * NC):
                    n, k = divmod(q, KT)
                    pe.wait_ge(z_ready.sem, z_ready.at(b, (n + 1) * TC - 1))
                    if q >= 2:
                        pe.wait_ge(tr_full_ready.sem, tr_full_ready.at(b, q - 2))
                    elif not in_setup:
                        pe.wait_ge(t_masked.sem, t_masked.at(b - 1, 4 * NC - 1))
                    transposes(b, q, 6 + q % 2, k, range(n * TC, (n + 1) * TC))
            attention_transposes(0, True)
            pe.wait_ge(product_lo, 2)
            pe.wait_ge(weight_lo, len(SPLITS))
            pe.wait_ge(pads_made, 12)
            pe.wait_ge(mod_copied, 2 * B + 1)

            def body(b, last):
                for j in range(4):
                    n, m = divmod(j, KT)
                    pe.wait_ge(tr_lo.sem, tr_lo.at(b, n * KT + 1))
                    if j == 0:
                        pe.wait_ge(dsum_ready.sem, dsum_ready.at(b, -1))
                    if j == 2:
                        pe.wait_ge(y_scaled.sem, y_scaled.at(b, -1))
                    for k in range(KT):
                        last_mm = product(ps[:, 4 + j, :], [w[:, k, m * P:(m + 1) * P] for w in wqk],
                                          [t[:, n, k, :] for t in xT], k == 0, k == KT - 1)
                    last_mm.then_inc(proj_ready.sem, 1)
                pe.wait_ge(h_ready.sem, h_ready.at(b, -1))
                for i in range(NT):
                    n, t = divmod(i, TC)
                    for k in range(KT):
                        last_mm = product(ps[:, i // 2, i % 2 * D:(i % 2 + 1) * D], [x_[:, n, k, t * P:(t + 1) * P] for x_ in xT],
                                          [w[:, k, :] for w in wvo], k == 0, k == KT - 1)
                    if i % 2:
                        last_mm.then_inc(proj_ready.sem, 1)
                for i in range(NT + 2):
                    if i < NT:
                        w = (i + 1) * P
                        if i < 2:
                            pe.wait_ge(proj_lo.sem, proj_lo.at(b, 5 + 2 * i))
                        else:
                            pe.wait_ge(probs_ready.sem, probs_ready.at(b, i - 2))
                        if i == TC:
                            pe.wait_ge(proj_lo.sem, proj_lo.at(b, 3))
                        for n in range(-(-w // CH)):
                            cw = min(CH, w - n * CH)
                            o = ps[:, 2 * (i % 2) + n, 0:cw]
                            diagonal = (n + 1) * CH >= w
                            for k in range(KT):
                                last_mm = product(o, [q[:, k, i * P:(i + 1) * P] for q in qT],
                                                  [t[:, n, k, 0:cw] for t in xT], k == 0, k == KT - 1 and not diagonal)
                            if diagonal:
                                last_mm = mm(ps[:, 2 * (i % 2) + n, cw - P:cw], identb[:, :], causal[:, :], False, True)
                        last_mm.then_inc(scores_ready.sem, 1)
                    if 1 <= i <= NT:
                        t = i - 1
                        pe.wait_ge(probs_ready.sem, probs_ready.at(b, t))
                        for e, j0, nj in pt_banks(t):
                            if e >= 2:
                                pe.wait_ge(pt_lo.sem, pt_lo.at(b, e - 2))
                            for j in range(nj):
                                last_mm = transpose(ps[:, 4 + e % 2, j * P:(j + 1) * P],
                                                    probs[:, t % 2, (j0 + j) * P:(j0 + j + 1) * P], ident[:, :])
                            last_mm.then_inc(pt_ready.sem, 1)
                    if i >= 2:
                        t = i - 2
                        pe.wait_ge(pt_lo.sem, pt_lo.at(b, pt_banks(t)[-1][0]))
                        if t >= 2:
                            pe.wait_ge(x1_ready.sem, x1_ready.at(b, t - 2))
                        for j in range(t + 1):
                            last_mm = product(ps[:, 6 + t % 2, 0:D], [p[:, t % 2, j, :] for p in pT], [v[:, j, :] for v in vv],
                                              j == 0, j == t)
                        last_mm.then_inc(pv_ready.sem, 1)
                for ci in range(NC):
                    slot_x = 2 * ci
                    xc = [[t[:, slot_x, k, :] for t in xT] for k in range(KT)]
                    if ci == 0:
                        for k in range(KT):
                            pe.wait_ge(z2_ready.sem, z2_ready.at(b, TC - 1))
                            transposes(b, KT * NC + k, k, k, range(TC))
                    pe.wait_ge(tr_lo.sem, tr_lo.at(b, KT * NC + ci * KT + 1))
                    if ci == 0:
                        pe.wait_ge(x1_ready.sem, x1_ready.at(b, NT - 1))
                    else:
                        pe.wait_ge(y_scaled.sem, y_scaled.at(b, TC - 1))
                    for t in range(TC):
                        for k in range(KT):
                            last_mm = product(ps[:, 6, t * E:(t + 1) * E], [x_[:, t * P:(t + 1) * P] for x_ in xc[k]],
                                              [w[:, k, :] for w in wrT], k == 0, k == KT - 1)
                    last_mm.then_inc(logits_ready.sem, 1)

                    def base(g, a):
                        n = unit(ci, g, 0, a)
                        j = 2 * g + a
                        if n >= 2:
                            pe.wait_ge(h_ready.sem, h_ready.at(b, n - 2))
                        for w, bank in ((wgT, 2 * a), (wuT, 2 * a + 1)):
                            for k in range(KT):
                                last_mm = product(ps[:, bank, :], [h[:, k, j * P:(j + 1) * P] for h in w], xc[k], k == 0, k == KT - 1)
                        last_mm.then_inc(gate_up_ready.sem, 1)

                    def adapters(g, slot, a):
                        n = unit(ci, g, slot, a)
                        j = 2 * g + a
                        pe.wait_ge(h_ready.sem, h_ready.at(b, n - 2))
                        if g == 0 and a == 0:
                            pe.wait_ge(tm_lo.sem, tm_lo.at(b, ci * 4 + 2 * slot - 1))
                        for m, (w, bank) in enumerate(((bgT, 2 * a), (buT, 2 * a + 1))):
                            last_mm = product(ps[:, bank, :], [h[:, j * P:(j + 1) * P] for h in w],
                                              [t[:, 2 * (slot - 1) + m, :] for t in tm], False, True)
                        last_mm.then_inc(gate_up_ready.sem, 1)

                    def down(g, slot, a):
                        n = unit(ci, g, slot, a)
                        j = 2 * g + a
                        pe.wait_ge(h_lo.sem, h_lo.at(b, n))
                        hn = [t[:, n % RING, :] for t in ring]
                        if slot == 0:
                            if j == 0:
                                if ci == 0:
                                    pe.wait_ge(tr_full_ready.sem, tr_full_ready.at(b, TR - 1))
                                elif not last:
                                    pe.wait_ge(tr_full_ready.sem, tr_full_ready.at(b + 1, KT * NC - 1))
                            for t in range(TC):
                                last_mm = product(ps[:, 6 + t // 2, t % 2 * D:(t % 2 + 1) * D], [h[:, t * P:(t + 1) * P] for h in hn],
                                                  [w[:, j, :] for w in wdT], j == 0 and t % 2 == 0, False)
                        else:
                            if j == 0:
                                pe.wait_ge(wmask_ready.sem, wmask_ready.at(b, ci * 2 + slot - 1))
                            last_mm = product(ps[:, 3 + slot, :], [w[:, j, :] for w in adT], hn, j == 0, j == FT - 1)
                        last_mm.then_inc(h_used.sem, 1)

                    base(0, 0)
                    if ci == 1:
                        pe.wait_ge(dsum_ready.sem, dsum_ready.at(b, 0))
                    for g in range(2):
                        for k in range(KT):
                            last_mm = product(ps[:, 4 + g, :], [w[:, g, k, :] for w in aT], xc[k], k == 0, k == KT - 1)
                        last_mm.then_inc(t_ready.sem, 1)
                    base(0, 1)
                    for m in range(4):
                        bank = (6, 7, 4, 5)[m]
                        pe.wait_ge(pick_ready.sem, pick_ready.at(b, 2 * ci + m // 2))
                        if m >= 2:
                            pe.wait_ge(t_copied.sem, t_copied.at(b, ci * 2 + m - 2))
                        for t in range(TC):
                            last_mm = transpose(ps[:, bank, t * P:(t + 1) * P],
                                                pick_er[:, m, t, :], ident[:, :])
                        last_mm.then_inc(masks_ready.sem, 1)
                    for g in range(GROUPS):
                        fill = [(g - 1, s, a) for s, a in down_order(g - 1)] if g else []
                        if g:
                            base(g, 0)
                            base(g, 1)
                        for slot in (1, 2):
                            for a in range(2):
                                for f in fill[:2]:
                                    down(*f)
                                fill = fill[2:]
                                adapters(g, slot, a)
                        for f in fill:
                            down(*f)
                        if g == 0:
                            if ci == 0:
                                for k in range(KT):
                                    pe.wait_ge(z2_ready.sem, z2_ready.at(b, NT - 1))
                                    pe.wait_ge(t_masked.sem, t_masked.at(b, 3))
                                    transposes(b, KT * NC + KT + k, 6 + k, k, range(TC, NT))
                            elif not last:
                                attention_transposes(b + 1, False)
                    for s, a in down_order(GROUPS - 1):
                        down(GROUPS - 1, s, a)
                    pe.wait_ge(dsum_lo.sem, dsum_lo.at(b, ci))
                    for t in range(TC):
                        last_mm = product(ps[:, 6 + t // 2, t % 2 * D:(t % 2 + 1) * D], [h[:, 0, t * P:(t + 1) * P] for h in tm],
                                          [w[:, :] for w in bdT], False, True)
                        if t % 2:
                            last_mm.then_inc(y_ready.sem, 1)
            batches(pe, body)


_INS = ['L0_attn_x', 'L0_attn_qkv', 'L0_attn_o_proj', 'L0_attn_gamma', 'L0_attn_beta', 'L0_ffn_Wg', 'L0_ffn_Wu', 'L0_ffn_Wd',
        'L0_ffn_Wr', 'L0_ffn_Ag', 'L0_ffn_Bg', 'L0_ffn_Au', 'L0_ffn_Bu', 'L0_ffn_Ad', 'L0_ffn_Bd', 'L0_c', 'L0_wmod']


_LAYOUT = {
    'L0_attn_qkv': lambda a: a.T, 'L0_attn_gamma': lambda a: a.reshape(-1, 128).T, 'L0_attn_beta': lambda a: a.reshape(-1, 128).T,
    'L0_ffn_Wg': lambda a: a.T, 'L0_ffn_Wu': lambda a: a.T, 'L0_ffn_Wd': lambda a: a.T, 'L0_ffn_Wr': lambda a: a.T,
    'L0_ffn_Ag': lambda a: a.reshape(-1, a.shape[2]).T, 'L0_ffn_Au': lambda a: a.reshape(-1, a.shape[2]).T,
    'L0_ffn_Ad': lambda a: a.reshape(-1, a.shape[2]).T,
    'L0_ffn_Bg': lambda a: a.transpose(0, 2, 1).reshape(-1, a.shape[1]),
    'L0_ffn_Bu': lambda a: a.transpose(0, 2, 1).reshape(-1, a.shape[1]),
    'L0_ffn_Bd': lambda a: a.transpose(0, 2, 1).reshape(-1, a.shape[1]),
    'L0_c': lambda a: a.T,
}


def kernel(**inputs):
    import numpy as _np
    import concourse.bacc as _bacc
    from concourse import mybir as _mybir
    from concourse.bass_utils import run_bass_kernel_spmd as _run

    nc = _bacc.Bacc("TRN2", target_bir_lowering=False, num_devices=1)
    arrays, args = {}, []
    for name in _INS:
        a = _LAYOUT.get(name, lambda v: v)(_np.asarray(inputs[name]))
        a = _np.ascontiguousarray(a)
        arrays[f"in_{name}"] = a
        args.append(nc.dram_tensor(f"in_{name}", a.shape, _mybir.dt.from_np(a.dtype), kind="ExternalInput").ap())
    shape = arrays["in_L0_attn_x"].shape
    out = nc.dram_tensor("out_0", shape, _mybir.dt.float32, kind="ExternalOutput").ap()
    adaln_attention_moe_lora(nc, *args, out)
    r = _run(nc, [arrays], core_ids=[0])
    return r.results[0]["out_0"]
```

```python
import concourse.bass as bass
from concourse import mybir
from contextlib import ExitStack


class Signal:

    def __init__(self, sem, per_batch, credit=0):
        self.sem, self.n, self.credit = sem, per_batch, credit

    def at(self, b, k):
        return b * self.n + (self.credit + k + 1)


def adaln_attention_moe_lora(nc, x, qkv, o_proj, gamma, beta, Wg, Wu, Wd, Wr, Ag, Bg, Au, Bu, Ad, Bd, c, wmod, out):
    fp32 = mybir.dt.float32
    f32r = mybir.dt.float32r
    bf16 = mybir.dt.bfloat16
    i32 = mybir.dt.int32
    u32 = mybir.dt.uint32
    ALU = mybir.AluOpType
    ACT = mybir.ActivationFunctionType
    X = mybir.AxisListType.X

    P = 128
    B, S, D = x.shape
    F = Wg.shape[1]
    E = Wr.shape[1]
    ER = Ag.shape[1]
    R = ER // E
    KT = D // P
    NT = S // P
    CH = 512
    NC = S // CH
    TC = CH // P
    FT = -(-F // P)
    FP = FT * P
    FREST = F - (FT - 1) * P
    GROUPS = FT // 2
    UPC = 3 * FT
    RING = 8
    EPS = 1e-5
    SCALING = 2.0
    SCORE_SCALE = 1.0 / 16.0
    MASKED = -1e30
    NPT = sum(-(-(i + 1) // TC) for i in range(NT))
    assert ER == P and KT == 2 and D == 256 and FT % 2 == 0 and TC == 4 and NC == 2

    ctx = ExitStack()
    with ctx:
        def sb(name, shape, dt, where=ctx):
            return where.enter_context(nc.sbuf_tensor(name, shape, dt))

        def sem(name):
            return ctx.enter_context(nc.semaphore(name))

        wqk = [sb(f"wqk_{h}", [P, KT, D], f32r) for h in ("hi", "lo")]
        wvo = [sb(f"wvo_{h}", [P, KT, D], f32r) for h in ("hi", "lo")]
        wgT = [sb(f"wgT_{h}", [P, KT, FP], f32r) for h in ("hi", "lo")]
        wuT = [sb(f"wuT_{h}", [P, KT, FP], f32r) for h in ("hi", "lo")]
        aT = [sb(f"aT_{h}", [P, 2, KT, ER], f32r) for h in ("hi", "lo")]
        wr_both = sb("wr_both", [P, KT, 2, E], f32r)
        wrT = [wr_both[:, :, h, :] for h in range(2)]
        bgT = [sb(f"bgT_{h}", [P, FP], f32r) for h in ("hi", "lo")]
        buT = [sb(f"buT_{h}", [P, FP], f32r) for h in ("hi", "lo")]
        wdT = [sb(f"wdT_{h}", [P, FT, D], f32r) for h in ("hi", "lo")]
        adT = [sb(f"adT_{h}", [P, FT, ER], f32r) for h in ("hi", "lo")]
        bdT = [sb(f"bdT_{h}", [P, D], f32r) for h in ("hi", "lo")]
        ident = sb("ident", [P, P], fp32)
        identb = sb("identb", [P, P], bf16)
        causal = sb("causal", [P, P], bf16)
        iota8 = sb("iota8", [P, E], fp32)
        gammaT = sb("gammaT", [P, KT], fp32)
        betaT = sb("betaT", [P, KT], fp32)
        cT = sb("cT", [P, KT, B], fp32)
        scT = sb("scT", [P, KT, B], fp32)
        modT = sb("modT", [P, 2, KT, B], fp32)
        SA, CA, GA, GB = range(4)
        bc = sb("bc", [P, B, 4, D], fp32)

        xs = sb("xs", [P, NT, D], fp32)
        zb = sb("zb", [P, NT, D], fp32)
        xr = sb("xr", [P, NT, D], fp32)
        xT = [sb(f"xT_{h}", [P, 3, KT, CH], f32r) for h in ("hi", "lo")]
        tr_full = sb("tr_full", [P, 2, CH], fp32)
        t_split = [t[:, 1, :, :] for t in xT]
        y_gb = sb("y_gb", [P, 2, D], fp32)
        wmask = sb("wmask", [P, 2, CH], fp32)
        gated = sb("gated", [P, 2, D], fp32)

        stat = sb("stat", [P, NT, 6], fp32)
        mv = sb("mv", [P, NT, 2], fp32)
        rstd = sb("rstd", [P, NT], fp32)
        nr_v = sb("nr_v", [P, NT], fp32)
        nr_h = sb("nr_h", [P, NT], fp32)
        nr_a = sb("nr_a", [P, NT], fp32)
        three_halves = sb("three_halves", [P, NT], fp32)
        nr_i = sb("nr_i", [P, NT], i32)
        rowmax = sb("rowmax", [P, NT], fp32)
        rowsum = sb("rowsum", [P, NT], fp32)
        rinv = sb("rinv", [P, NT], fp32)
        lg = sb("lg", [P, TC, E], fp32)
        pr = sb("pr", [P, TC, E], fp32)
        lmax = sb("lmax", [P, TC], fp32)
        lsum = sb("lsum", [P, TC], fp32)
        top = sb("top", [P, TC, 8], fp32)
        topi = sb("topi", [P, TC, 8], u32)
        topf = sb("topf", [P, TC, 8], fp32)
        onehot = sb("onehot", [P, 2, TC, E], fp32)
        pick = sb("pick", [P, 4, TC, E], fp32)

        stage_ctx = ExitStack()
        with stage_ctx:
            def st(name, shape):
                return sb(name, shape, fp32, stage_ctx)
            s_qkvT = st("s_qkvT", [P, 3, KT, D])
            s_o = st("s_o", [P, KT, D])
            s_mod = st("s_mod", [P, KT, 6 * D])
            s_wg = st("s_wg", [P, KT, F])
            s_wu = st("s_wu", [P, KT, F])
            st("s_rest", [P, 2 * KT * S + 2 * NT * D - (10 * KT * D + 2 * KT * F)])
            s_wd = st("s_wd", [P, FT, D])
            s_a = st("s_a", [P, 2, KT, ER])
            s_wr = st("s_wr", [P, KT, E])
            s_bd = st("s_bd", [P, D])
        s_scb = tr_full[:, :, :].rearrange("p k (b n) -> p k b n", n=P)
        s_bg = xr[:, 0:3, :].rearrange("p i d -> p (i d)")[:, 0:F]
        s_bu = xr[:, 3:6, :].rearrange("p i d -> p (i d)")[:, 0:F]
        s_ad = wmask[:, :, :].rearrange("p s n -> p (s n)")[:, 0:FT * ER].rearrange("p (j e) -> p j e", e=ER)

        at_ctx = ExitStack()
        with at_ctx:
            qT = [sb(f"qT_{h}", [P, KT, S], f32r, at_ctx) for h in ("hi", "lo")]
            vv = [sb(f"vv_{h}", [P, NT, D], f32r, at_ctx) for h in ("hi", "lo")]
            pT = [sb(f"pT_{h}", [P, 2, NT, P], f32r, at_ctx) for h in ("hi", "lo")]
            probs = sb("probs", [P, 2, S], fp32, at_ctx)
        mask_ctx = ExitStack()
        with mask_ctx:
            sb("ring_front", [P, RING - 4, CH], f32r, mask_ctx)
            pick_er = sb("pick_er", [P, 4, TC, ER], fp32, mask_ctx)
        ring = [sb(f"ring_{h}", [P, RING, CH], f32r) for h in ("hi", "lo")]
        tm = [sb(f"tm_{h}", [P, 4, CH], f32r) for h in ("hi", "lo")]
        act_s = sb("act_s", [P, 2, CH], fp32)
        hid = sb("hid", [P, 2, CH], fp32)

        ps = ctx.enter_context(nc.psum_tensor("ps", [P, 8, 512], fp32))

        consts_made = sem("consts_made")
        pads_made = sem("pads_made")
        loaded = {k: sem("ld_" + k) for k in ("qkv", "o", "mod", "c", "ln", "wg", "wu", "wd", "a", "wr", "bg", "bu", "ad", "bd")}
        sc_ready = sem("sc_ready")
        scb_ready = sem("scb_ready")
        mod_ready = sem("mod_ready")
        mod_copied = sem("mod_copied")
        gates_ready = sem("gates_ready")
        product_ready = sem("product_ready")
        product_hi = sem("product_hi")
        product_lo = sem("product_lo")
        weight_hi = sem("weight_hi")
        weight_lo = sem("weight_lo")
        x_loaded = sem("x_loaded")
        stored = sem("stored")
        vstep = sem("vstep")
        pool_step = sem("pool_step")
        unwaited = sem("unwaited")

        def signal(name, per_batch, credit=0):
            return Signal(sem(name), per_batch, credit)
        z_ready = signal("z_ready", NT)
        t_gated = signal("t_gated", NT)
        r_ready = signal("r_ready", NT)
        TR = 2 * KT * NC
        transposed = signal("transposed", TR)
        tr_full_ready = signal("tr_full_ready", TR)
        tr_hi = signal("tr_hi", TR)
        tr_lo = signal("tr_lo", TR)
        proj_ready = signal("proj_ready", 8)
        proj_hi = signal("proj_hi", 8)
        proj_lo = signal("proj_lo", 8)
        scores_ready = signal("scores_ready", NT)
        rowmax_ready = signal("rowmax_ready", NT)
        probs_ready = signal("probs_ready", NT)
        pt_ready = signal("pt_ready", NPT)
        pt_hi = signal("pt_hi", NPT)
        pt_lo = signal("pt_lo", NPT)
        pv_ready = signal("pv_ready", NT)
        x1_scaled = signal("x1_scaled", NT)
        x1_ready = signal("x1_ready", NT)
        norm_ready = signal("norm_ready", 4)
        rstd_ready = signal("rstd_ready", 4)
        z2_ready = signal("z2_ready", NT)
        logits_ready = signal("logits_ready", NC)
        shifted_ready = signal("shifted_ready", NC)
        rexp_ready = signal("rexp_ready", NC)
        picks_made = signal("picks_made", NC)
        masks_spread = signal("masks_spread", NC)
        weights_spread = signal("weights_spread", NC)
        masks_ready = signal("masks_ready", 4 * NC)
        wmask_ready = signal("wmask_ready", 2 * NC)
        t_ready = signal("t_ready", 2 * NC)
        t_hi = signal("t_hi", 2 * NC)
        t_lo = signal("t_lo", 2 * NC)
        tm_ready = signal("tm_ready", 4 * NC)
        UPB = UPC * NC
        gate_up_ready = signal("gate_up_ready", UPB)
        silu_ready = signal("silu_ready", UPB)
        h_ready = signal("h_ready", UPB, credit=1)
        h_hi = signal("h_hi", UPB)
        h_lo = signal("h_lo", UPB)
        h_used = signal("h_used", UPB)
        dsum_ready = signal("dsum_ready", NC, credit=1)
        dsum_hi = signal("dsum_hi", NC)
        dsum_lo = signal("dsum_lo", NC)
        y_ready = signal("y_ready", NT // 2)
        y_scaled = signal("y_scaled", NT, credit=1)
        out_ready = signal("out_ready", NT, credit=1)

        def unit(ci, g, slot, a):
            return ci * UPC + g * 6 + slot * 2 + a

        def down_order(ci, g):
            slots = (0, 1, 2) if ci or g else (1, 2, 0)
            return [(slot, a) for slot in slots for a in range(2)]

        def down_position(n):
            ci, g, rest = n // UPC, n % UPC // 6, n % 6
            return n - rest + down_order(ci, g).index((rest // 2, rest % 2))

        def pt_banks(i):
            first = sum(-(-(j + 1) // TC) for j in range(i))
            return [(first + q, q * TC, min(TC, i + 1 - q * TC)) for q in range(-(-(i + 1) // TC))]

        LN2_A, LN2_B, LN1_X, LN1_H = range(4)
        NEWTON = 3
        T_BANKS = ((4, 5), (0, 1))
        MASK_BANKS = ((7, 6, 4, 5), (3, 4, 5, 6))
        LOGIT_BANK = (2, 7)
        PV_FIRST = 5

        SPLITS = [("wg", s_wg[:, k, :], [w[:, k, 0:F] for w in wgT]) for k in range(KT)]
        SPLITS += [("wu", s_wu[:, k, :], [w[:, k, 0:F] for w in wuT]) for k in range(KT)]
        EARLY = len(SPLITS)
        SPLITS += [("wd", s_wd[:, 0:FT - 1, :], [w[:, 0:FT - 1, :] for w in wdT]),
                   ("a", s_a[:, :, :, :].rearrange("p g k e -> p (g k e)"), [w[:, :, :, :].rearrange("p g k e -> p (g k e)") for w in aT]),
                   ("wr", s_wr[:, :, :], [w[:, :, :] for w in wrT]),
                   ("bd", s_bd[:, :], [w[:, :] for w in bdT]),
                   ("bg", s_bg, [w[:, 0:F] for w in bgT]), ("bu", s_bu, [w[:, 0:F] for w in buT]),
                   ("ad", s_ad[:, 0:FT - 1, :], [w[:, 0:FT - 1, :] for w in adT])]
        SPLITS += [("wd", s_wd[0:FREST, FT - 1, :], [w[0:FREST, FT - 1, :] for w in wdT]),
                   ("ad", s_ad[0:FREST, FT - 1, :], [w[0:FREST, FT - 1, :] for w in adT])]
        LOADS = {"wd": 2, "ad": 2, "a": 2, "ln": 2}

        MOD_BANKS = (0, 1, 2, 3, 6, 7, 0, 1)

        block = ctx.enter_context(nc.Block())

        def batches(eng, body):
            with eng.Fori(0, B - 1) as b:
                body(b, False)
            body(B - 1, True)

        @block.sync
        def _(sp):
            sp.sem_inc(stored, 16)

            def load(key, dst, src):
                sp.dma_start(dst, src).then_inc(loaded[key], 16)
            load("c", cT[:, :, :], c.rearrange("(k p) b -> p k b", p=P))
            load("mod", s_mod[:, :, :], wmod.rearrange("(k p) n -> p k n", p=P))
            sp.dma_start(xs[:, :, :], x[0].rearrange("(i p) d -> p i d", p=P)).then_inc(x_loaded, 16)
            load("qkv", s_qkvT[:, :, :, :].rearrange("p w k d -> p (w k) d"), qkv.rearrange("(k p) d -> p k d", p=P))
            load("o", s_o[:, :, :], o_proj.rearrange("(k p) n -> p k n", p=P))
            load("ln", gammaT[:, :], gamma)
            load("ln", betaT[:, :], beta)
            load("wg", s_wg[:, :, :], Wg.rearrange("(k p) f -> p k f", p=P))
            load("wu", s_wu[:, :, :], Wu.rearrange("(k p) f -> p k f", p=P))
            load("a", s_a[:, 0, :, :], Ag.rearrange("(k p) e -> p k e", p=P))
            load("a", s_a[:, 1, :, :], Au.rearrange("(k p) e -> p k e", p=P))
            load("wr", s_wr[:, :, :], Wr.rearrange("(k p) e -> p k e", p=P))
            load("bg", s_bg, Bg)
            load("bu", s_bu, Bu)
            for key, dst, src in (("wd", s_wd, Wd), ("ad", s_ad, Ad)):
                load(key, dst[:, 0:FT - 1, :], src[0:(FT - 1) * P, :].rearrange("(j p) n -> p j n", p=P))
                load(key, dst[0:FREST, FT - 1, :], src[(FT - 1) * P:F, :])
            load("bd", s_bd[:, :], Bd)

            def body(b, last):
                if not last:
                    sp.wait_ge(x1_ready.sem, x1_ready.at(b, NT - 1))
                    sp.dma_start(xs[:, :, :], x[b + 1].rearrange("(i p) d -> p i d", p=P)).then_inc(x_loaded, 16)
                for ci in range(NC):
                    sp.wait_ge(out_ready.sem, out_ready.at(b, ci * TC + TC - 1))
                    sp.dma_start(out[b, ci * CH:(ci + 1) * CH, :].rearrange("(i p) d -> p i d", p=P),
                                 xr[:, ci * TC:(ci + 1) * TC, :]).then_inc(stored, 16)
            batches(sp, body)
            sp.wait_ge(stored, 16 + 16 * NC * B)

        @block.gpsimd
        def _(pool):
            pool.memset(ident[:, :], 0.0).then_inc(consts_made, 1)
            pool.memset(causal[:, :], 0.0).then_inc(consts_made, 1)
            pool.wait_ge(consts_made, 2)
            pool.affine_select(out=ident[:, :], in_=ident[:, :], compare_op=ALU.not_equal, fill=1.0, base=0,
                               pattern=[[-1, P]], channel_multiplier=1).then_inc(consts_made, 1)
            pool.affine_select(out=causal[:, :], in_=causal[:, :], compare_op=ALU.is_ge, fill=MASKED, base=0,
                               pattern=[[-1, P]], channel_multiplier=1).then_inc(consts_made, 1)
            pool.iota(iota8[:, :], pattern=[[1, E]], base=0, channel_multiplier=0,
                      allow_small_or_imprecise_dtypes=True).then_inc(consts_made, 1)
            pool.wait_ge(consts_made, 5)
            pool.tensor_copy(identb[:, :], ident[:, :]).then_inc(consts_made, 1)
            pool.memset(three_halves[:, :], 1.5).then_inc(pads_made, 1)
            for w in wgT + wuT:
                pool.memset(w[:, :, F:FP].bitcast(fp32), 0.0).then_inc(pads_made, 1)
            for w in bgT + buT:
                pool.memset(w[:, F:FP].bitcast(fp32), 0.0).then_inc(pads_made, 1)
            pool.wait_ge(pads_made, 9)
            for w in wdT + adT:
                pool.memset(w[FREST:P, FT - 1, :].bitcast(fp32), 0.0).then_inc(pads_made, 1)
            pool.wait_ge(pads_made, 13)

            steps = [0, 0]

            def link(ins):
                steps[1] += 1
                ins.then_inc(pool_step, 1)
                pool.wait_ge(pool_step, steps[0] + steps[1])

            def newton(b, which, lo, n, it):
                h, a, y = nr_h[:, lo:lo + n], nr_a[:, lo:lo + n], rstd[:, lo:lo + n]
                if it == 0:
                    pool.wait_ge(norm_ready.sem, norm_ready.at(b, which))
                link(pool.tensor_mul(a, y, y))
                link(pool.tensor_mul(a, a, h))
                link(pool.tensor_add(a, a, three_halves[:, 0:n]))
                last = pool.tensor_mul(y, y, a)
                if it < NEWTON - 1:
                    link(last)
                else:
                    last.then_inc(rstd_ready.sem, 1)

            def residual(b, i):
                pool.wait_ge(t_gated.sem, t_gated.at(b, i))
                pool.tensor_add(xs[:, i, :], xs[:, i, :], gated[:, i % 2, :]).then_inc(r_ready.sem, 1)

            def x1_row(b, i):
                if i == 0:
                    pool.wait_ge(r_ready.sem, r_ready.at(b, NT - 1))
                pool.wait_ge(x1_scaled.sem, x1_scaled.at(b, i))
                pool.tensor_add(xr[:, i, :], xr[:, i, :], xs[:, i, :]).then_inc(x1_ready.sem, 1)

            def tr_low(b, q, dst):
                pool.wait_ge(tr_hi.sem, tr_hi.at(b, q))
                pool.tensor_sub(dst[1], tr_full[:, q % 2, :], dst[0].bitcast(fp32)).then_inc(tr_lo.sem, 1)

            def attention_inputs(b, q):
                n, k = divmod(q, KT)
                tr_low(b, q, [t[:, n, k, :] for t in xT])

            def hid_low(b, n):
                pool.wait_ge(h_hi.sem, h_hi.at(b, n))
                pool.tensor_sub(ring[1][:, n % RING, :], hid[:, n % 2, :],
                                ring[0][:, n % RING, :].bitcast(fp32)).then_inc(h_lo.sem, 1)

            def weight_low(j):
                _, src, (hi, lo) = SPLITS[j]
                pool.wait_ge(weight_hi, j + 1)
                pool.tensor_sub(lo, src, hi.bitcast(fp32)).then_inc(weight_lo, 1)

            for j in range(EARLY):
                weight_low(j)
            for i in range(NT):
                pool.wait_ge(t_gated.sem, t_gated.at(0, i))
                if i == 0:
                    pool.wait_ge(gates_ready, 1)
                link(pool.tensor_mul(gated[:, i % 2, :], zb[:, i, :], bc[:, 0, GA, :]))
                pool.tensor_add(xs[:, i, :], xs[:, i, :], gated[:, i % 2, :]).then_inc(r_ready.sem, 1)
            setup_steps = steps[1]
            for q in range(KT * NC):
                attention_inputs(0, q)
            for j in range(EARLY, len(SPLITS)):
                if j == len(SPLITS) - 2:
                    pool.wait_ge(weight_lo, j)
                weight_low(j)
            pool.wait_ge(weight_lo, len(SPLITS))
            POOL_STEPS = 4 * (4 * NEWTON - 1)

            def body(b, last):
                steps[0], steps[1] = b * POOL_STEPS + setup_steps, 0
                for i in range(TC):
                    x1_row(b, i)
                for it in range(NEWTON):
                    newton(b, LN2_A, 0, TC, it)
                x1_row(b, TC)
                x1_row(b, TC + 1)
                for k in range(KT):
                    tr_low(b, KT * NC + k, [t[:, 0, k, :] for t in xT])
                x1_row(b, TC + 2)
                x1_row(b, TC + 3)
                for ci in range(NC):
                    for r in range(UPC):
                        if ci == 0:
                            if r < NEWTON:
                                newton(b, LN2_B, TC, TC, r)
                            if r == 6:
                                for k in range(KT):
                                    tr_low(b, KT * NC + KT + k, [t[:, 2, k, :] for t in xT])
                            if not last and 13 <= r < 13 + NEWTON:
                                newton(b, LN1_X, 0, NT, r - 13)
                        elif not last:
                            if 4 <= r < 4 + NT:
                                residual(b + 1, r - 4)
                            if r == 12:
                                newton(b, LN1_H, 0, NT, 0)
                                newton(b, LN1_H, 0, NT, 1)
                            if r == 13:
                                newton(b, LN1_H, 0, NT, 2)
                        hid_low(b, ci * UPC + r)
                    if ci == 1 and not last:
                        for q in range(KT * NC):
                            attention_inputs(b + 1, q)
                    for t in range(TC):
                        i = ci * TC + t
                        pool.wait_ge(y_scaled.sem, y_scaled.at(b, i))
                        pool.tensor_add(xr[:, i, :], xr[:, i, :], y_gb[:, t % 2, :]).then_inc(out_ready.sem, 1)
                if not last:
                    assert steps[1] == POOL_STEPS, steps
            batches(pool, body)

        @block.scalar
        def _(act):
            act.wait_ge(loaded["c"], 16)
            nc.scalar.activation(scT[:, :, :], cT[:, :, :], ACT.Silu).then_inc(sc_ready, 1)

            def modulation(b):
                for h in range(2):
                    act.wait_ge(mod_ready, 2 * b + h + 1)
                    nc.scalar.activation(bc[:, b, 2 * h:2 * h + 2, :].rearrange("p t d -> p (t d)"),
                                         ps[:, MOD_BANKS[2 * b + h], :], ACT.Copy).then_inc(mod_copied, 1)
            modulation(0)

            def weight_high(j):
                key, src, (hi, _) = SPLITS[j]
                act.wait_ge(loaded[key], 16 * LOADS.get(key, 1))
                nc.scalar.activation(hi, src, ACT.Copy).then_inc(weight_hi, 1)
            for j in range(EARLY):
                weight_high(j)
            for j, (w, scale) in enumerate(((wqk, SCORE_SCALE), (wvo, 1.0))):
                act.wait_ge(product_ready, j + 1)
                nc.scalar.activation(w[0][:, :, :].rearrange("p k d -> p (k d)"), ps[:, 4 + j, :], ACT.Copy,
                                     scale=scale).then_inc(product_hi, 1)
            for b in range(1, B):
                modulation(b)
            act.wait_ge(mod_ready, 2 * B + 1)
            nc.scalar.activation(modT[:, :, :, :].rearrange("p t k b -> p (t k b)"), ps[:, 2, 0:2 * KT * B], ACT.Copy).then_inc(mod_copied, 1)
            for j in range(EARLY, len(SPLITS)):
                weight_high(j)

            def tr_high(b, q, dst):
                act.wait_ge(tr_full_ready.sem, tr_full_ready.at(b, q))
                nc.scalar.activation(dst, tr_full[:, q % 2, :], ACT.Copy).then_inc(tr_hi.sem, 1)

            def attention_inputs(b):
                for q in range(KT * NC):
                    tr_high(b, q, xT[0][:, q // KT, q % KT, :])

            def queries_values(b, js):
                for j in js:
                    act.wait_ge(proj_ready.sem, proj_ready.at(b, j))
                    if j < 4:
                        n, m = divmod(j, KT)
                        nc.scalar.activation(qT[0][:, m, n * CH:(n + 1) * CH], ps[:, j, :], ACT.Copy).then_inc(proj_hi.sem, 1)
                    else:
                        i = 2 * (j - 4)
                        nc.scalar.activation(vv[0][:, i:i + 2, :].rearrange("p i d -> p (i d)"), ps[:, j, :], ACT.Copy).then_inc(proj_hi.sem, 1)
            attention_inputs(0)
            act.wait_ge(weight_lo, EARLY)
            queries_values(0, range(6))

            def body(b, last):
                for i in range(NT + 1):
                    if i < NT:
                        w = (i + 1) * P
                        act.wait_ge(rowmax_ready.sem, rowmax_ready.at(b, i))
                        if i >= 2:
                            act.wait_ge(pt_ready.sem, pt_ready.at(b, pt_banks(i - 2)[-1][0]))
                        banks = ps[:, 2 * (i % 2):2 * (i % 2) + 2, :].rearrange("p n s -> p (n s)")
                        nc.scalar.activation(probs[:, i % 2, 0:w], banks[:, 0:w], ACT.Exp, bias=rowmax[:, i:i + 1],
                                             accum_out=rowsum[:, i:i + 1]).then_inc(probs_ready.sem, 1)
                    if i == NT:
                        tr_high(b, KT * NC, xT[0][:, 0, 0, :])
                    if i >= 1:
                        t = i - 1
                        for e, j0, nj in pt_banks(t):
                            if t == 0:
                                act.wait_ge(weight_lo, len(SPLITS))
                            act.wait_ge(pt_ready.sem, pt_ready.at(b, e))
                            if t >= 2:
                                act.wait_ge(pv_ready.sem, pv_ready.at(b, t - 2))
                            nc.scalar.activation(pT[0][:, t % 2, j0:j0 + nj, :].rearrange("p j s -> p (j s)"),
                                                 ps[:, 4 + e % 2, 0:nj * P], ACT.Copy).then_inc(pt_hi.sem, 1)
                    if i == NT:
                        tr_high(b, KT * NC + 1, xT[0][:, 0, 1, :])
                    if i < 2:
                        queries_values(b, (6 + i,))

                def router_exp(ci):
                    act.wait_ge(shifted_ready.sem, shifted_ready.at(b, ci))
                    nc.scalar.activation(pr[:, :, :], lg[:, :, :], ACT.Exp).then_inc(rexp_ready.sem, 1)

                def adapter_input_high(ci, g):
                    act.wait_ge(t_ready.sem, t_ready.at(b, ci * 2 + g))
                    nc.scalar.activation(t_split[0][:, g, :], ps[:, T_BANKS[ci][g], :], ACT.Copy).then_inc(t_hi.sem, 1)

                def spread_weights(ci):
                    act.wait_ge(picks_made.sem, picks_made.at(b, ci))
                    if ci:
                        act.wait_ge(h_used.sem, h_used.at(b, down_position(unit(ci - 1, GROUPS - 1, 1, 1))))
                    nc.scalar.activation(pick_er[:, 2:4, :, :].rearrange("p m t (e r) -> p (m t e) r", r=R),
                                         pick[:, 2:4, :, :].rearrange("p m t e -> p (m t e)").unsqueeze(2)
                                         .to_broadcast([P, 2 * TC * E, R]), ACT.Copy).then_inc(weights_spread.sem, 1)

                def dsum_high(ci):
                    act.wait_ge(dsum_ready.sem, dsum_ready.at(b, ci))
                    nc.scalar.activation(tm[0][:, 3, :], wmask[:, 0, :], ACT.Copy).then_inc(dsum_hi.sem, 1)

                def silu(n):
                    act.wait_ge(gate_up_ready.sem, gate_up_ready.at(b, n))
                    if n >= 2:
                        act.wait_ge(h_ready.sem, h_ready.at(b, n - 2))
                    nc.scalar.activation(act_s[:, n % 2, :], ps[:, 2 * (n % 2), :], ACT.Silu).then_inc(silu_ready.sem, 1)

                def high(n):
                    act.wait_ge(h_ready.sem, h_ready.at(b, n))
                    if n >= RING:
                        act.wait_ge(h_used.sem, h_used.at(b, down_position(n - RING)))
                    nc.scalar.activation(ring[0][:, n % RING, :], hid[:, n % 2, :], ACT.Copy).then_inc(h_hi.sem, 1)

                router_exp(0)
                for g in range(2):
                    adapter_input_high(0, g)
                spread_weights(0)
                for ci in range(NC):
                    n0 = ci * UPC
                    silu(n0)
                    for r in range(1, UPC):
                        silu(n0 + r)
                        if ci == 0 and r == 13:
                            router_exp(1)
                        high(n0 + r - 1)
                        if r in (3, 5):
                            slot = (3, 5).index(r)
                            act.wait_ge(masks_ready.sem, masks_ready.at(b, ci * 4 + 2 + slot))
                            if ci and slot == 0:
                                act.wait_ge(dsum_lo.sem, dsum_lo.at(b, ci - 1))
                            nc.scalar.activation(wmask[:, slot, :], ps[:, MASK_BANKS[ci][2 + slot], :], ACT.Copy).then_inc(wmask_ready.sem, 1)
                        if ci == 0 and r == 6:
                            for k in range(KT):
                                tr_high(b, KT * NC + KT + k, xT[0][:, 2, k, :])
                    high(n0 + UPC - 1)
                    if ci == 0:
                        spread_weights(1)
                        adapter_input_high(1, 0)
                        dsum_high(0)
                        adapter_input_high(1, 1)
                    elif not last:
                        attention_inputs(b + 1)
                        queries_values(b + 1, range(1))
                        dsum_high(1)
                        queries_values(b + 1, range(1, 6))
                    else:
                        dsum_high(1)
            batches(act, body)

        @block.vector
        def _(dve):
            V = nc.vector
            for s in (h_ready, dsum_ready, y_scaled, out_ready):
                dve.sem_inc(s.sem, 1)
            steps = [0, 0]

            def link(ins):
                steps[1] += 1
                ins.then_inc(vstep, 1)
                dve.wait_ge(vstep, steps[0] + steps[1])

            def link_apart(ins):
                link(ins)
                dve.sem_inc(unwaited, 1)

            def mark(ins):
                steps[1] += 1
                ins.then_inc(vstep, 1)

            def settle():
                dve.wait_ge(vstep, steps[0] + steps[1])

            def guess(lo, n):
                v, y = nr_v[:, lo:lo + n], rstd[:, lo:lo + n]
                link(V.tensor_scalar_add(v, mv[:, lo:lo + n, 1], EPS))
                mark(V.tensor_scalar(nr_h[:, lo:lo + n], v, -0.5, None, ALU.mult))
                link(V.tensor_scalar(nr_i[:, lo:lo + n], v.bitcast(i32), 1, None, ALU.logical_shift_right))
                return V.tensor_scalar(y.bitcast(i32), nr_i[:, lo:lo + n], -1.0, float(0x5f3759df), ALU.mult, ALU.add)

            def rsqrt(lo, n):
                v, a, y = nr_v[:, lo:lo + n], nr_a[:, lo:lo + n], rstd[:, lo:lo + n]
                link(guess(lo, n))
                for _ in range(NEWTON):
                    link(V.tensor_mul(a, y, y))
                    link(V.scalar_tensor_tensor(a, a, -0.5, v, ALU.mult, ALU.mult))
                    link(V.scalar_tensor_tensor(y, a, 1.5, y, ALU.add, ALU.mult))

            def moments(tiles):
                settle()
                dve.sem_inc(unwaited, 1)
                for i in tiles:
                    last = V.bn_aggr(mv[:, i, :], stat[:, i, :])
                link(last)

            def x_stats(tiles):
                for i in tiles:
                    mark(V.bn_stats(stat[:, i, :], xs[:, i, :]))

            def ln1_h(b, tiles, gated_here=True):
                for i in tiles:
                    mark(V.scalar_tensor_tensor(zb[:, i, :], xs[:, i, :], mv[:, i, 0:1], bc[:, b, CA, :], ALU.subtract, ALU.mult))
                settle()
                for i in tiles:
                    h_rows = V.scalar_tensor_tensor(zb[:, i, :], zb[:, i, :], rstd[:, i:i + 1], bc[:, b, SA, :], ALU.mult, ALU.add)
                    if gated_here:
                        mark(h_rows)
                    else:
                        h_rows.then_inc(t_gated.sem, 1)
                if gated_here:
                    settle()
                else:
                    dve.wait_ge(t_gated.sem, t_gated.at(b, tiles[-1]))
                for i in tiles if gated_here else ():
                    if i >= 2:
                        dve.wait_ge(r_ready.sem, r_ready.at(b, i - 2))
                    V.tensor_mul(gated[:, i % 2, :], zb[:, i, :], bc[:, b, GA, :]).then_inc(t_gated.sem, 1)
                for i in tiles:
                    mark(V.bn_stats(stat[:, i, :], zb[:, i, :]))

            def normalise(i, src, sig):
                V.tensor_scalar(zb[:, i, :], src[:, i, :], mv[:, i, 0:1], rstd[:, i:i + 1], ALU.subtract, ALU.mult).then_inc(sig.sem, 1)

            def gate(b, step):
                g = bc[:, b, GA:GB + 1, :]
                if step == 0:
                    mark(V.tensor_scalar_add(bc[:, b, CA, :], bc[:, b, CA, :], 1.0))
                    mark(V.tensor_scalar(y_gb[:, :, :], g, 0.0, 2.0, ALU.is_ge, ALU.mult))
                elif step == 1:
                    mark(V.scalar_tensor_tensor(gated[:, :, :], g, -1.0, g, ALU.mult, ALU.max))
                elif step == 2:
                    settle()
                    mark(V.tensor_scalar_max(gated[:, :, :], gated[:, :, :], 0.25))
                else:
                    settle()
                    mark(V.scalar_tensor_tensor(g, y_gb[:, :, :], -1.0, gated[:, :, :], ALU.add, ALU.mult))

            def tr_scale(b, q, bank, scale, bias):
                dve.wait_ge(transposed.sem, transposed.at(b, q))
                if not (isinstance(b, int) and b == 0 and q < 2):
                    dve.wait_ge(tr_lo.sem, tr_lo.at(b, q - 2))
                V.tensor_scalar(tr_full[:, q % 2, :], ps[:, bank, :], scale, bias, ALU.mult, ALU.add).then_inc(tr_full_ready.sem, 1)

            def attention_scale(b):
                for q in range(KT * NC):
                    k = q % KT
                    tr_scale(b, q, q, gammaT[:, k:k + 1], betaT[:, k:k + 1])

            def queries_values(b, js):
                for j in js:
                    dve.wait_ge(proj_hi.sem, proj_hi.at(b, j))
                    if j < 4:
                        n, m = divmod(j, KT)
                        hi, lo = [t[:, m, n * CH:(n + 1) * CH] for t in qT]
                    else:
                        i = 2 * (j - 4)
                        hi, lo = [t[:, i:i + 2, :].rearrange("p i d -> p (i d)") for t in vv]
                    V.tensor_sub(lo, ps[:, j, :], hi.bitcast(fp32)).then_inc(proj_lo.sem, 1)

            dve.wait_ge(sc_ready, 1)
            V.tensor_copy(s_scb[:, :, :, :].rearrange("p k b n -> p (k b) n"),
                          scT[:, :, :].rearrange("p k b -> p (k b)").unsqueeze(2).to_broadcast([P, KT * B, P])).then_inc(scb_ready, 1)
            dve.wait_ge(x_loaded, 16)
            x_stats(range(NT))
            moments(range(NT))
            rsqrt(0, NT)
            dve.wait_ge(mod_copied, 2)
            for step in range(4):
                gate(0, step)
            settle()
            dve.sem_inc(gates_ready, 1)
            for i in range(0, NT, 2):
                ln1_h(0, (i, i + 1), gated_here=False)
            for j, (w, scale) in enumerate(((wqk, SCORE_SCALE), (wvo, 1.0))):
                dve.wait_ge(product_hi, j + 1)
                hi, lo = [t[:, :, :].rearrange("p k d -> p (k d)") for t in w]
                V.scalar_tensor_tensor(lo, ps[:, 4 + j, :], scale, hi.bitcast(fp32), ALU.mult, ALU.subtract).then_inc(product_lo, 1)
            moments(range(NT))
            rsqrt(0, NT)
            dve.wait_ge(r_ready.sem, r_ready.at(0, NT - 1))
            for i in range(NT):
                normalise(i, zb, z_ready)
            dve.wait_ge(loaded["ln"], 32)
            attention_scale(0)
            dve.wait_ge(mod_copied, 2 * B + 1)
            link(V.tensor_scalar_add(modT[:, 1, :, :], modT[:, 1, :, :], 1.0))
            dve.wait_ge(weight_lo, EARLY)
            queries_values(0, range(6))
            setup_steps = steps[1]
            VSTEPS = 95

            def body(b, last):
                steps[0], steps[1] = b * VSTEPS + setup_steps, 0

                def ffn_scale(c2, bank0):
                    for k in range(KT):
                        tr_scale(b, KT * NC + c2 * KT + k, bank0 + k, modT[:, 1, k, bass.ds(b, 1)], modT[:, 0, k, bass.ds(b, 1)])

                def x1_stats(i):
                    dve.wait_ge(x1_ready.sem, x1_ready.at(b, i))
                    mark(V.bn_stats(stat[:, i, :], xr[:, i, :]))

                def x1_product(t):
                    if t == 0:
                        dve.wait_ge(stored, b * (16 * NC) + 16)
                        dve.wait_ge(weight_lo, len(SPLITS))
                    dve.wait_ge(pv_ready.sem, pv_ready.at(b, t))
                    settle()
                    V.scalar_tensor_tensor(xr[:, t, :], ps[:, 6 + t % 2, 0:D], rinv[:, t:t + 1], bc[:, b, GA, :],
                                           ALU.mult, ALU.mult).then_inc(x1_scaled.sem, 1)

                for i in range(NT + 1):
                    if i < NT:
                        w = (i + 1) * P
                        banks = ps[:, 2 * (i % 2):2 * (i % 2) + 2, :].rearrange("p n s -> p (n s)")
                        dve.wait_ge(scores_ready.sem, scores_ready.at(b, i))
                        V.tensor_reduce(rowmax[:, i:i + 1], banks[:, 0:w], X, ALU.max, negate=True).then_inc(rowmax_ready.sem, 1)
                    if 3 <= i < 3 + TC:
                        x1_stats(i - 3)
                    if i == 3 + TC - 1:
                        moments(range(TC))
                        guess(0, TC).then_inc(norm_ready.sem, 1)
                    if i == NT:
                        ffn_scale(0, 0)
                    if i >= 1:
                        t = i - 1
                        dve.wait_ge(probs_ready.sem, probs_ready.at(b, t))
                        mark(V.reciprocal(rinv[:, t:t + 1], rowsum[:, t:t + 1]))
                        if i == NT - 1:
                            dve.wait_ge(rstd_ready.sem, rstd_ready.at(b, LN2_A))
                            for tile in range(TC):
                                normalise(tile, xr, z2_ready)
                        for e, j0, nj in pt_banks(t):
                            dve.wait_ge(pt_hi.sem, pt_hi.at(b, e))
                            hi, lo = [p[:, t % 2, j0:j0 + nj, :].rearrange("p j s -> p (j s)") for p in pT]
                            V.tensor_sub(lo, ps[:, 4 + e % 2, 0:nj * P], hi.bitcast(fp32)).then_inc(pt_lo.sem, 1)
                    if i < 2:
                        queries_values(b, (6 + i,))
                    if i >= 2:
                        x1_product(i - 2)

                def router_shift(ci):
                    logits = ps[:, LOGIT_BANK[ci], 0:TC * 2 * E].rearrange("p (t h e) -> p h t e", h=2, e=E)
                    dve.wait_ge(logits_ready.sem, logits_ready.at(b, ci))
                    link(V.tensor_copy(pr[:, :, :], logits[:, 1, :, :]))
                    link(V.tensor_add(lg[:, :, :], logits[:, 0, :, :], pr[:, :, :]))
                    link(V.tensor_reduce(lmax[:, :], lg[:, :, :], X, ALU.max))
                    V.tensor_sub(lg[:, :, :], lg[:, :, :], lmax[:, :].unsqueeze(2).to_broadcast([P, TC, E])).then_inc(shifted_ready.sem, 1)

                def router_probs(ci):
                    dve.wait_ge(rexp_ready.sem, rexp_ready.at(b, ci))
                    link(V.tensor_reduce(lsum[:, :], pr[:, :, :], X, ALU.add))
                    link(V.reciprocal(lsum[:, :], lsum[:, :]))
                    link_apart(V.tensor_mul(pr[:, :, :], pr[:, :, :], lsum[:, :].unsqueeze(2).to_broadcast([P, TC, E])))

                def router_top():
                    for t in range(TC):
                        last_max = V.max(top[:, t, :], pr[:, t, :])
                    link_apart(last_max)
                    for t in range(TC):
                        last_idx = V.max_index(topi[:, t, :], top[:, t, :], pr[:, t, :])
                    mark(last_idx)

                def router_picks():
                    settle()
                    link(V.tensor_copy(topf[:, :, 0:2], topi[:, :, 0:2]))
                    for s in range(2):
                        last_hot = V.tensor_tensor(onehot[:, s, :, :], iota8[:, :].unsqueeze(1).to_broadcast([P, TC, E]),
                                                   topf[:, :, s:s + 1].to_broadcast([P, TC, E]), ALU.is_equal)
                    link(last_hot)
                    mark(V.tensor_sub(pick[:, 1, :, :], onehot[:, 1, :, :], onehot[:, 0, :, :]))
                    V.tensor_scalar_mul(pick[:, 0, :, :], onehot[:, 0, :, :], SCALING)
                    for s in range(2):
                        V.scalar_tensor_tensor(pick[:, 2 + s, :, :], onehot[:, s, :, :], SCALING,
                                               top[:, :, s:s + 1].to_broadcast([P, TC, E]), ALU.mult, ALU.mult)
                    settle()
                    V.tensor_scalar_mul(pick[:, 1, :, :], pick[:, 1, :, :], SCALING).then_inc(picks_made.sem, 1)

                def spread_masks(ci):
                    if ci:
                        dve.wait_ge(h_used.sem, h_used.at(b, down_position(unit(ci - 1, GROUPS - 1, 1, 1))))
                    dve.wait_ge(picks_made.sem, picks_made.at(b, ci))
                    V.tensor_copy(pick_er[:, 0:2, :, :].rearrange("p m t (e r) -> p (m t e) r", r=R),
                                  pick[:, 0:2, :, :].rearrange("p m t e -> p (m t e)").unsqueeze(2)
                                  .to_broadcast([P, 2 * TC * E, R])).then_inc(masks_spread.sem, 1)

                def adapter_input_low(ci, g):
                    dve.wait_ge(t_hi.sem, t_hi.at(b, ci * 2 + g))
                    V.tensor_sub(t_split[1][:, g, :], ps[:, T_BANKS[ci][g], :], t_split[0][:, g, :].bitcast(fp32)).then_inc(t_lo.sem, 1)

                def masked(ci, m):
                    which, g = divmod(m, 2)
                    dve.wait_ge(masks_ready.sem, masks_ready.at(b, ci * 4 + which))
                    dve.wait_ge(t_lo.sem, t_lo.at(b, ci * 2 + g))
                    if m == 3 and ci == 1:
                        dve.wait_ge(y_ready.sem, y_ready.at(b, TC // 2 - 1))
                    for h in range(2):
                        last = V.tensor_mul(tm[h][:, m, :], t_split[h][:, g, :].bitcast(fp32), ps[:, MASK_BANKS[ci][which], :])
                    last.then_inc(tm_ready.sem, 1)

                def hidden(n):
                    dve.wait_ge(silu_ready.sem, silu_ready.at(b, n))
                    if n >= 2:
                        dve.wait_ge(h_lo.sem, h_lo.at(b, n - 2))
                    V.tensor_mul(hid[:, n % 2, :], act_s[:, n % 2, :], ps[:, 2 * (n % 2) + 1, :]).then_inc(h_ready.sem, 1)

                def dsum(ci):
                    for s in range(2):
                        dve.wait_ge(wmask_ready.sem, wmask_ready.at(b, ci * 2 + s))
                        dve.wait_ge(h_used.sem, h_used.at(b, down_position(unit(ci, GROUPS - 1, 1 + s, 1))))
                        mark(V.tensor_mul(wmask[:, s, :], wmask[:, s, :], ps[:, 4 + s, :]))
                    settle()
                    V.tensor_add(wmask[:, 0, :], wmask[:, 0, :], wmask[:, 1, :]).then_inc(dsum_ready.sem, 1)

                def dsum_low(ci):
                    dve.wait_ge(dsum_hi.sem, dsum_hi.at(b, ci))
                    V.tensor_sub(tm[1][:, 3, :], wmask[:, 0, :], tm[0][:, 3, :].bitcast(fp32)).then_inc(dsum_lo.sem, 1)

                def scaled_sums(ci):
                    for t in range(TC):
                        i = ci * TC + t
                        dve.wait_ge(y_ready.sem, y_ready.at(b, i // 2))
                        if ci or t >= 2:
                            dve.wait_ge(out_ready.sem, out_ready.at(b, i - 2))
                        V.tensor_mul(y_gb[:, t % 2, :], ps[:, 6 + t // 2, t % 2 * D:(t % 2 + 1) * D], bc[:, b, GB, :]).then_inc(y_scaled.sem, 1)

                router_shift(0)
                x1_stats(TC)
                x1_stats(TC + 1)
                router_probs(0)
                router_top()
                router_picks()
                spread_masks(0)
                x1_product(NT - 1)
                x1_stats(TC + 2)
                for g in range(2):
                    adapter_input_low(0, g)
                masked(0, 0)
                masked(0, 1)
                x1_stats(TC + 3)
                moments(range(TC, NT))
                guess(TC, TC).then_inc(norm_ready.sem, 1)
                hidden(0)
                masked(0, 2)
                hidden(1)
                masked(0, 3)
                for r in range(2, UPC):
                    hidden(r)
                    if r == 4:
                        dve.wait_ge(rstd_ready.sem, rstd_ready.at(b, LN2_B))
                    if r in (4, 5):
                        for i in (2 * r - 4, 2 * r - 3):
                            normalise(i, xr, z2_ready)
                    if r == 6:
                        ffn_scale(1, 6)
                    if r == 9:
                        router_shift(1)
                    if r == 13:
                        router_probs(1)
                    if r == 14:
                        router_top()
                    if r == 15:
                        router_picks()
                    if not last:
                        if r == 6:
                            dve.wait_ge(x_loaded, (b + 1) * 16 + 16)
                        if r in (6, 8, 10, 11):
                            i = 2 * (6, 8, 10, 11).index(r)
                            x_stats((i, i + 1))
                        if r == 11:
                            moments(range(NT))
                            guess(0, NT).then_inc(norm_ready.sem, 1)
                        if r == 12:
                            dve.wait_ge(out_ready.sem, out_ready.at(b, -1))
                            gate(b + 1, 0)
                        if r == 16:
                            gate(b + 1, 1)
                            gate(b + 1, 2)
                        if r == 17:
                            gate(b + 1, 3)
                spread_masks(1)
                dsum(0)
                adapter_input_low(1, 0)
                dsum_low(0)
                adapter_input_low(1, 1)
                masked(1, 0)
                masked(1, 1)
                scaled_sums(0)
                n0 = UPC
                hidden(n0)
                masked(1, 2)
                hidden(n0 + 1)
                masked(1, 3)
                for r in range(2, UPC):
                    hidden(n0 + r)
                    if not last:
                        if r == 3:
                            dve.wait_ge(rstd_ready.sem, rstd_ready.at(b, LN1_X))
                        if 3 <= r < 3 + NT:
                            ln1_h(b + 1, (r - 3,))
                        if r == 3 + NT:
                            moments(range(NT))
                            guess(0, NT).then_inc(norm_ready.sem, 1)
                        if r == 13:
                            dve.wait_ge(rstd_ready.sem, rstd_ready.at(b, LN1_H))
                        if 13 <= r < 17:
                            normalise(2 * (r - 13), zb, z_ready)
                            normalise(2 * (r - 13) + 1, zb, z_ready)
                if not last:
                    attention_scale(b + 1)
                dsum(1)
                if not last:
                    queries_values(b + 1, range(1))
                dsum_low(1)
                if not last:
                    queries_values(b + 1, range(1, 4))
                scaled_sums(1)
                if not last:
                    queries_values(b + 1, range(4, 6))
                    assert steps[1] == VSTEPS, steps
            batches(dve, body)

        @block.tensor
        def _(pe):
            def mm(o, w, v, start, stop):
                return nc.tensor.matmul(o, w, v, start=start, stop=stop, skip_group_check=True)

            def product(o, w, v, start, stop):
                mm(o, w[0], v[0], start, False)
                mm(o, w[0], v[1], False, False)
                return mm(o, w[1], v[0], False, stop)

            def transpose(o, src, idn):
                return nc.tensor.transpose(o, src, idn)

            def modulation(b):
                for h in range(2):
                    if b == B - 1:
                        pe.wait_ge(mod_copied, h + 1)
                    for p0, c0, w in (((0, 0, 2 * D),), ((0, 2 * D, D), (D, 5 * D, D)))[h]:
                        for k in range(KT):
                            last_mm = mm(ps[:, MOD_BANKS[2 * b + h], p0:p0 + w], s_scb[:, k, b, :], s_mod[:, k, c0:c0 + w], k == 0, k == KT - 1)
                    last_mm.then_inc(mod_ready, 1)
            pe.wait_ge(loaded["mod"], 16)
            pe.wait_ge(scb_ready, 1)
            modulation(0)
            pe.wait_ge(loaded["qkv"], 16)
            pe.wait_ge(loaded["o"], 16)
            for j, (left, right) in enumerate(((0, s_qkvT[:, 1, :, :]), (2, s_o))):
                for d in range(KT):
                    for k in range(KT):
                        last_mm = mm(ps[:, 4 + j, d * D:(d + 1) * D], s_qkvT[:, left, k, d * P:(d + 1) * P], right[:, k, :],
                                     k == 0, k == KT - 1)
                last_mm.then_inc(product_ready, 1)
            for b in range(1, B):
                modulation(b)
            pe.wait_ge(mod_copied, 4)
            for t in range(2):
                for m in range(KT):
                    o = ps[:, 2, (t * KT + m) * B:(t * KT + m + 1) * B]
                    for k in range(KT):
                        last_mm = mm(o, s_mod[:, k, (3 + t) * D + m * P:(3 + t) * D + (m + 1) * P], scT[:, k, :], k == 0, k == KT - 1)
            last_mm.then_inc(mod_ready, 1)
            pe.wait_ge(consts_made, 6)
            pe.wait_ge(mod_copied, 2 * B + 1)

            def transposes(b, q, bank, k, tiles):
                for t, i in enumerate(tiles):
                    last = transpose(ps[:, bank, t * P:(t + 1) * P], zb[:, i, k * P:(k + 1) * P], ident[:, :])
                last.then_inc(transposed.sem, 1)

            def attention_transposes(b, n):
                for k in range(KT):
                    q = n * KT + k
                    pe.wait_ge(z_ready.sem, z_ready.at(b, (n + 1) * TC - 1))
                    transposes(b, q, q, k, range(n * TC, (n + 1) * TC))

            def queries(b):
                for j in range(4):
                    n, m = divmod(j, KT)
                    pe.wait_ge(tr_lo.sem, tr_lo.at(b, n * KT + 1))
                    for k in range(KT):
                        last_mm = product(ps[:, j, :], [w[:, k, m * P:(m + 1) * P] for w in wqk],
                                          [t[:, n, k, :] for t in xT], k == 0, k == KT - 1)
                    last_mm.then_inc(proj_ready.sem, 1)

            def values(b, tiles):
                for i in tiles:
                    n, t = divmod(i, TC)
                    if i == 0:
                        pe.wait_ge(dsum_ready.sem, dsum_ready.at(b, -1))
                    if i == NT // 2:
                        pe.wait_ge(y_scaled.sem, y_scaled.at(b, -1))
                    for k in range(KT):
                        last_mm = product(ps[:, 4 + i // 2, i % 2 * D:(i % 2 + 1) * D], [x_[:, n, k, t * P:(t + 1) * P] for x_ in xT],
                                          [w[:, k, :] for w in wvo], k == 0, k == KT - 1)
                    if i % 2:
                        last_mm.then_inc(proj_ready.sem, 1)
            for n in range(NC):
                attention_transposes(0, n)
            pe.wait_ge(product_lo, 2)
            queries(0)
            values(0, range(NT // 2))
            pe.wait_ge(pads_made, 13)

            def body(b, last):
                def probs_values(t, blocks=None):
                    if blocks is None:
                        blocks = range(t + 1)
                    if blocks[0] > 0:
                        for j in blocks:
                            last_mm = product(ps[:, 6 + t % 2, 0:D], [p[:, t % 2, j, :] for p in pT], [v[:, j, :] for v in vv],
                                              False, j == t)
                        last_mm.then_inc(pv_ready.sem, 1)
                        return
                    pe.wait_ge(pt_lo.sem, pt_lo.at(b, pt_banks(t)[-1][0]))
                    if t >= 2:
                        pe.wait_ge(x1_scaled.sem, x1_scaled.at(b, t - 2))
                    else:
                        pe.wait_ge(proj_lo.sem, proj_lo.at(b, 6 + t))
                    for j in blocks:
                        last_mm = product(ps[:, 6 + t % 2, 0:D], [p[:, t % 2, j, :] for p in pT], [v[:, j, :] for v in vv],
                                          j == 0, j == t)
                    if blocks[-1] == t:
                        last_mm.then_inc(pv_ready.sem, 1)

                for i in range(NT + 1):
                    if i < NT:
                        w = (i + 1) * P
                        if i < 2:
                            pe.wait_ge(proj_lo.sem, proj_lo.at(b, 3))
                        else:
                            pe.wait_ge(probs_ready.sem, probs_ready.at(b, i - 2))
                        for n in range(-(-w // CH)):
                            cw = min(CH, w - n * CH)
                            o = ps[:, 2 * (i % 2) + n, 0:cw]
                            diagonal = (n + 1) * CH >= w
                            for k in range(KT):
                                last_mm = product(o, [q[:, k, i * P:(i + 1) * P] for q in qT],
                                                  [t[:, n, k, 0:cw] for t in xT], k == 0, k == KT - 1 and not diagonal)
                            if diagonal:
                                last_mm = mm(ps[:, 2 * (i % 2) + n, cw - P:cw], identb[:, :], causal[:, :], False, True)
                        last_mm.then_inc(scores_ready.sem, 1)
                        if i < 2:
                            values(b, range(NT // 2 + 2 * i, NT // 2 + 2 * i + 2))
                    else:
                        for k in range(KT):
                            pe.wait_ge(z2_ready.sem, z2_ready.at(b, TC - 1))
                            pe.wait_ge(probs_ready.sem, probs_ready.at(b, NT - 2))
                            transposes(b, KT * NC + k, k, k, range(TC))
                    if i >= 1:
                        t = i - 1
                        pe.wait_ge(probs_ready.sem, probs_ready.at(b, t))
                        for e, j0, nj in pt_banks(t):
                            if e >= 2:
                                pe.wait_ge(pt_lo.sem, pt_lo.at(b, e - 2))
                            else:
                                pe.wait_ge(proj_lo.sem, proj_lo.at(b, 4 + e))
                            for j in range(nj):
                                last_mm = transpose(ps[:, 4 + e % 2, j * P:(j + 1) * P],
                                                    probs[:, t % 2, (j0 + j) * P:(j0 + j + 1) * P], ident[:, :])
                            last_mm.then_inc(pt_ready.sem, 1)
                    if i >= 2:
                        probs_values(i - 2)

                def inputs(ci):
                    return [[t[:, 2 * ci, k, :] for t in xT] for k in range(KT)]

                def logits(ci):
                    pe.wait_ge(tr_lo.sem, tr_lo.at(b, KT * NC + ci * KT + 1))
                    for t in range(TC):
                        o = ps[:, LOGIT_BANK[ci], 2 * t * E:2 * (t + 1) * E]
                        for k in range(KT):
                            x_hi, x_lo = [x_[:, t * P:(t + 1) * P] for x_ in inputs(ci)[k]]
                            mm(o, x_hi, wr_both[:, k, :, :].rearrange("p h e -> p (h e)"), k == 0, False)
                            last_mm = mm(o[:, 0:E], x_lo, wr_both[:, k, 0, :], False, k == KT - 1)
                    last_mm.then_inc(logits_ready.sem, 1)

                def adapter_inputs(ci):
                    for g in range(2):
                        for k in range(KT):
                            last_mm = product(ps[:, T_BANKS[ci][g], :], [w[:, g, k, :] for w in aT], inputs(ci)[k], k == 0, k == KT - 1)
                        last_mm.then_inc(t_ready.sem, 1)

                def mask(ci, m):
                    for t in range(TC):
                        last_mm = transpose(ps[:, MASK_BANKS[ci][m], t * P:(t + 1) * P], pick_er[:, m, t, :], ident[:, :])
                    last_mm.then_inc(masks_ready.sem, 1)

                def base(ci, g, a):
                    n = unit(ci, g, 0, a)
                    j = 2 * g + a
                    if g:
                        pe.wait_ge(h_ready.sem, h_ready.at(b, n - 2))
                    for w, bank in ((wgT, 2 * a), (wuT, 2 * a + 1)):
                        for k in range(KT):
                            last_mm = product(ps[:, bank, :], [h[:, k, j * P:(j + 1) * P] for h in w], inputs(ci)[k], k == 0, k == KT - 1)
                    last_mm.then_inc(gate_up_ready.sem, 1)

                def adapters(ci, g, slot, a):
                    n = unit(ci, g, slot, a)
                    j = 2 * g + a
                    pe.wait_ge(h_ready.sem, h_ready.at(b, n - 2))
                    if g == 0 and a == 0:
                        pe.wait_ge(tm_ready.sem, tm_ready.at(b, ci * 4 + 2 * slot - 1))
                    for m, (w, bank) in enumerate(((bgT, 2 * a), (buT, 2 * a + 1))):
                        last_mm = product(ps[:, bank, :], [h[:, j * P:(j + 1) * P] for h in w],
                                          [t[:, 2 * (slot - 1) + m, :] for t in tm], False, True)
                    last_mm.then_inc(gate_up_ready.sem, 1)

                def down(ci, g, slot, a):
                    n = unit(ci, g, slot, a)
                    j = 2 * g + a
                    pe.wait_ge(h_lo.sem, h_lo.at(b, n))
                    hn = [t[:, n % RING, :] for t in ring]
                    if slot == 0:
                        if j == 0 and ci == 0:
                            pe.wait_ge(shifted_ready.sem, shifted_ready.at(b, 1))
                        elif j == 0:
                            pe.wait_ge(wmask_ready.sem, wmask_ready.at(b, 3))
                        for t in range(TC):
                            last_mm = product(ps[:, 6 + t // 2, t % 2 * D:(t % 2 + 1) * D], [h[:, t * P:(t + 1) * P] for h in hn],
                                              [w[:, j, :] for w in wdT], j == 0 and t % 2 == 0, False)
                    else:
                        if j == 0:
                            pe.wait_ge(wmask_ready.sem, wmask_ready.at(b, ci * 2 + 1))
                        last_mm = product(ps[:, 3 + slot, :], [w[:, j, :] for w in adT], hn, j == 0, j == FT - 1)
                    last_mm.then_inc(h_used.sem, 1)

                def up_adapters(ci):
                    pe.wait_ge(dsum_lo.sem, dsum_lo.at(b, ci))
                    for t in range(TC):
                        last_mm = product(ps[:, 6 + t // 2, t % 2 * D:(t % 2 + 1) * D], [h[:, 3, t * P:(t + 1) * P] for h in tm],
                                          [w[:, :] for w in bdT], False, True)
                        if t % 2:
                            last_mm.then_inc(y_ready.sem, 1)

                def units(ci):
                    for g in range(GROUPS):
                        fill = [(ci, g - 1, s, a) for s, a in down_order(ci, g - 1)] if g else []
                        if g:
                            base(ci, g, 0)
                        if ci == 0 and g == 1:
                            for k in range(KT):
                                pe.wait_ge(z2_ready.sem, z2_ready.at(b, NT - 1))
                                pe.wait_ge(tm_ready.sem, tm_ready.at(b, 3))
                                transposes(b, KT * NC + KT + k, 6 + k, k, range(TC, NT))
                        if g:
                            base(ci, g, 1)
                        for slot in (1, 2):
                            for a in range(2):
                                if ci == 0 and g == 1 and slot == 2 and a == 0:
                                    logits(1)
                                else:
                                    for f in fill[:2]:
                                        down(*f)
                                    fill = fill[2:]
                                adapters(ci, g, slot, a)
                                if g == 0 and a == 1:
                                    if slot == 1:
                                        pe.wait_ge(weights_spread.sem, weights_spread.at(b, ci))
                                    if ci == 0:
                                        pe.wait_ge(t_lo.sem, t_lo.at(b, slot - 1))
                                    elif slot == 2:
                                        pe.wait_ge(y_scaled.sem, y_scaled.at(b, TC - 1))
                                    mask(ci, 1 + slot)
                        for f in fill:
                            down(*f)

                def last_downs(ci):
                    return [(ci, GROUPS - 1, s, a) for s, a in down_order(ci, GROUPS - 1)]

                pe.wait_ge(weight_lo, len(SPLITS))
                pe.wait_ge(probs_ready.sem, probs_ready.at(b, NT - 1))
                probs_values(NT - 1, range(PV_FIRST))
                logits(0)
                probs_values(NT - 1, range(PV_FIRST, NT))
                adapter_inputs(0)
                base(0, 0, 0)
                pe.wait_ge(x1_scaled.sem, x1_scaled.at(b, NT - 1))
                for m in range(2):
                    pe.wait_ge(masks_spread.sem, masks_spread.at(b, 0))
                    mask(0, m)
                pe.wait_ge(shifted_ready.sem, shifted_ready.at(b, 0))
                base(0, 0, 1)
                units(0)
                for f in last_downs(0):
                    down(*f)
                pe.wait_ge(h_ready.sem, h_ready.at(b, UPC - 1))
                adapter_inputs(1)
                pe.wait_ge(masks_spread.sem, masks_spread.at(b, 1))
                mask(1, 0)
                pe.wait_ge(dsum_ready.sem, dsum_ready.at(b, 0))
                mask(1, 1)
                up_adapters(0)
                pe.wait_ge(t_lo.sem, t_lo.at(b, 3))
                base(1, 0, 0)
                pe.wait_ge(tm_ready.sem, tm_ready.at(b, 5))
                base(1, 0, 1)
                units(1)
                for d, f in enumerate(last_downs(1)):
                    if not last and d < NC:
                        pe.wait_ge(h_ready.sem, h_ready.at(b, 2 * UPC - 2 + d))
                        attention_transposes(b + 1, d)
                    down(*f)
                if not last:
                    queries(b + 1)
                up_adapters(1)
                if not last:
                    values(b + 1, range(NT // 2))
            batches(pe, body)


_INS = ['L0_attn_x', 'L0_attn_qkv', 'L0_attn_o_proj', 'L0_attn_gamma', 'L0_attn_beta', 'L0_ffn_Wg', 'L0_ffn_Wu', 'L0_ffn_Wd',
        'L0_ffn_Wr', 'L0_ffn_Ag', 'L0_ffn_Bg', 'L0_ffn_Au', 'L0_ffn_Bu', 'L0_ffn_Ad', 'L0_ffn_Bd', 'L0_c', 'L0_wmod']


_LAYOUT = {
    'L0_attn_qkv': lambda a: a.T, 'L0_attn_gamma': lambda a: a.reshape(-1, 128).T, 'L0_attn_beta': lambda a: a.reshape(-1, 128).T,
    'L0_ffn_Wg': lambda a: a.T, 'L0_ffn_Wu': lambda a: a.T, 'L0_ffn_Wd': lambda a: a.T, 'L0_ffn_Wr': lambda a: a.T,
    'L0_ffn_Ag': lambda a: a.reshape(-1, a.shape[2]).T, 'L0_ffn_Au': lambda a: a.reshape(-1, a.shape[2]).T,
    'L0_ffn_Ad': lambda a: a.reshape(-1, a.shape[2]).T,
    'L0_ffn_Bg': lambda a: a.transpose(0, 2, 1).reshape(-1, a.shape[1]),
    'L0_ffn_Bu': lambda a: a.transpose(0, 2, 1).reshape(-1, a.shape[1]),
    'L0_ffn_Bd': lambda a: a.transpose(0, 2, 1).reshape(-1, a.shape[1]),
    'L0_c': lambda a: a.T,
}


def kernel(**inputs):
    import numpy as _np
    import concourse.bacc as _bacc
    from concourse import mybir as _mybir
    from concourse.bass_utils import run_bass_kernel_spmd as _run

    nc = _bacc.Bacc("TRN2", target_bir_lowering=False, num_devices=1)
    arrays, args = {}, []
    for name in _INS:
        a = _LAYOUT.get(name, lambda v: v)(_np.asarray(inputs[name]))
        a = _np.ascontiguousarray(a)
        arrays[f"in_{name}"] = a
        args.append(nc.dram_tensor(f"in_{name}", a.shape, _mybir.dt.from_np(a.dtype), kind="ExternalInput").ap())
    shape = arrays["in_L0_attn_x"].shape
    out = nc.dram_tensor("out_0", shape, _mybir.dt.float32, kind="ExternalOutput").ap()
    adaln_attention_moe_lora(nc, *args, out)
    r = _run(nc, [arrays], core_ids=[0])
    return r.results[0]["out_0"]
```

```python
import concourse.bass as bass
from concourse import mybir
from contextlib import ExitStack


class Signal:

    def __init__(self, sem, per_batch, credit=0):
        self.sem, self.n, self.credit = sem, per_batch, credit

    def at(self, b, k):
        return b * self.n + (self.credit + k + 1)


def adaln_attention_moe_lora(nc, x, qkv, o_proj, gamma, beta, Wg, Wu, Wd, Wr, Ag, Bg, Au, Bu, Ad, Bd, c, wmod, out):
    fp32 = mybir.dt.float32
    f32r = mybir.dt.float32r
    bf16 = mybir.dt.bfloat16
    i32 = mybir.dt.int32
    u32 = mybir.dt.uint32
    ALU = mybir.AluOpType
    ACT = mybir.ActivationFunctionType
    X = mybir.AxisListType.X

    P = 128
    B, S, D = x.shape
    F = Wg.shape[1]
    E = Wr.shape[1]
    ER = Ag.shape[1]
    R = ER // E
    KT = D // P
    NT = S // P
    CH = 512
    NC = S // CH
    TC = CH // P
    FT = -(-F // P)
    FP = FT * P
    FULL = (FT - 1) * P
    FREST = F - FULL
    GROUPS = FT // 2
    UPC = 3 * FT
    HID = 3
    RING = 8
    EPS = 1e-5
    SCALING = 2.0
    SCORE_SCALE = 1.0 / 16.0
    MASKED = -1e30
    NPT = sum(-(-(i + 1) // TC) for i in range(NT))
    assert ER == P and KT == 2 and D == 256 and FT % 2 == 0 and 2 * FREST == P and TC == 4 and NC == 2 and B == 4

    ctx = ExitStack()
    with ctx:
        def sb(name, shape, dt, where=ctx):
            return where.enter_context(nc.sbuf_tensor(name, shape, dt))

        def sem(name):
            return ctx.enter_context(nc.semaphore(name))

        wqk = [sb(f"wqk_{h}", [P, KT, D], f32r) for h in ("hi", "lo")]
        wvo = [sb(f"wvo_{h}", [P, KT, D], f32r) for h in ("hi", "lo")]
        wgT = [sb(f"wgT_{h}", [P, KT, FP], f32r) for h in ("hi", "lo")]
        wuT = [sb(f"wuT_{h}", [P, KT, FULL], f32r) for h in ("hi", "lo")]
        aT = [sb(f"aT_{h}", [P, 2, KT, ER], f32r) for h in ("hi", "lo")]
        wr_both = sb("wr_both", [P, KT, 2, E], f32r)
        wrT = [wr_both[:, :, h, :] for h in range(2)]
        bgT = [sb(f"bgT_{h}", [P, FP], f32r) for h in ("hi", "lo")]
        buT = [sb(f"buT_{h}", [P, FP], f32r) for h in ("hi", "lo")]
        wdT = [sb(f"wdT_{h}", [P, FT, D], f32r) for h in ("hi", "lo")]
        adT = [sb(f"adT_{h}", [P, FT, ER], f32r) for h in ("hi", "lo")]
        bdT = [sb(f"bdT_{h}", [P, D], f32r) for h in ("hi", "lo")]
        ident = sb("ident", [P, P], fp32)
        identb = sb("identb", [P, P], bf16)
        causal = sb("causal", [P, P], bf16)
        iota8 = sb("iota8", [P, E], fp32)
        gammaT = sb("gammaT", [P, KT], fp32)
        betaT = sb("betaT", [P, KT], fp32)
        cT = sb("cT", [P, KT, B], fp32)
        scT = sb("scT", [P, KT, B], fp32)
        modT = sb("modT", [P, 2, KT, B], fp32)
        SA, CA, GA, GB = range(4)
        bc = sb("bc", [P, B, 4, D], fp32)

        xs = sb("xs", [P, NT, D], fp32)
        zb = sb("zb", [P, NT, D], fp32)
        xr = sb("xr", [P, NT, D], fp32)
        xT = [sb(f"xT_{h}", [P, 3, KT, CH], f32r) for h in ("hi", "lo")]
        tr_full = sb("tr_full", [P, 2, CH], fp32)
        t_split = [t[:, 1, :, :] for t in xT]
        y_gb = sb("y_gb", [P, 2, D], fp32)
        wmask = sb("wmask", [P, 2, CH], fp32)
        gated = sb("gated", [P, 2, D], fp32)

        stat = sb("stat", [P, NT, 6], fp32)
        mv = sb("mv", [P, NT, 2], fp32)
        rstd = sb("rstd", [P, NT], fp32)
        nr_v = sb("nr_v", [P, NT], fp32)
        nr_h = sb("nr_h", [P, NT], fp32)
        nr_a = sb("nr_a", [P, NT], fp32)
        three_halves = sb("three_halves", [P, NT], fp32)
        nr_i = sb("nr_i", [P, NT], i32)
        neg_mean = sb("neg_mean", [P, NT - TC], fp32)
        rowmax = sb("rowmax", [P, NT], fp32)
        rowsum = sb("rowsum", [P, NT], fp32)
        rinv = sb("rinv", [P, NT], fp32)
        lg = sb("lg", [P, TC, E], fp32)
        pr = sb("pr", [P, TC, E], fp32)
        lmax = sb("lmax", [P, TC], fp32)
        lsum = sb("lsum", [P, TC], fp32)
        top = sb("top", [P, TC, 8], fp32)
        topi = sb("topi", [P, TC, 8], u32)
        topf = sb("topf", [P, TC, 8], fp32)
        onehot = sb("onehot", [P, 2, TC, E], fp32)
        pick = sb("pick", [P, 4, TC, E], fp32)

        stage_ctx = ExitStack()
        with stage_ctx:
            def st(name, shape):
                return sb(name, shape, fp32, stage_ctx)
            s_qkvT = st("s_qkvT", [P, 3, KT, D])
            s_o = st("s_o", [P, KT, D])
            s_mod = st("s_mod", [P, KT, 6 * D])
            s_wg = st("s_wg", [P, KT, F])
            s_wu = st("s_wu", [P, KT, F])
            st("s_rest", [P, 2 * KT * S + 2 * NT * D - (10 * KT * D + 2 * KT * F)])
            s_wd = st("s_wd", [P, FT, D])
            s_a = st("s_a", [P, 2, KT, ER])
            s_wr = st("s_wr", [P, KT, E])
            s_bd = st("s_bd", [P, D])
            s_bg = st("s_bg", [P, F])
            s_bu = st("s_bu", [P, F])
        s_ad = wmask[:, :, :].rearrange("p s n -> p (s n)")[:, 0:FT * ER].rearrange("p (j e) -> p j e", e=ER)

        at_ctx = ExitStack()
        with at_ctx:
            qT = [sb(f"qT_{h}", [P, KT, S], f32r, at_ctx) for h in ("hi", "lo")]
            vv = [sb(f"vv_{h}", [P, NT, D], f32r, at_ctx) for h in ("hi", "lo")]
            pT = [sb(f"pT_{h}", [P, 2, NT, P], f32r, at_ctx) for h in ("hi", "lo")]
            probs = sb("probs", [P, 2, S], fp32, at_ctx)
        mask_ctx = ExitStack()
        with mask_ctx:
            sb("ring_front", [P, RING - 4, CH], f32r, mask_ctx)
            pick_er = sb("pick_er", [P, 4, TC, ER], fp32, mask_ctx)
        ring = [sb(f"ring_{h}", [P, RING, CH], f32r) for h in ("hi", "lo")]
        tm = [sb(f"tm_{h}", [P, 4, CH], f32r) for h in ("hi", "lo")]
        act_s = sb("act_s", [P, 2, CH], fp32)
        s_scb = act_s[:, :, :].rearrange("p k (b n) -> p k b n", n=P)
        hid = sb("hid", [P, HID, CH], fp32)

        ps = ctx.enter_context(nc.psum_tensor("ps", [P, 8, 512], fp32))

        consts_made = sem("consts_made")
        pads_made = sem("pads_made")
        loaded = {k: sem("ld_" + k) for k in ("qkv", "o", "mod", "mod_rest", "c", "ln", "wg", "wu", "wd", "a", "wr", "bg", "bu", "ad", "bd")}
        sc_ready = sem("sc_ready")
        scb_ready = sem("scb_ready")
        mod_ready = sem("mod_ready")
        mod_copied = sem("mod_copied")
        gates_ready = sem("gates_ready")
        product_ready = sem("product_ready")
        product_hi = sem("product_hi")
        product_lo = sem("product_lo")
        weight_hi = sem("weight_hi")
        early_lo = sem("early_lo")
        weight_lo = sem("weight_lo")
        first_mean = sem("first_mean")
        first_scale = sem("first_scale")
        first_ca = sem("first_ca")
        first_centred = sem("first_centred")
        first_scaled = sem("first_scaled")
        first_h = sem("first_h")
        first_h_pool = sem("first_h_pool")
        first_guess = sem("first_guess")
        first_rstd = sem("first_rstd")
        x_loaded = sem("x_loaded")
        stored = sem("stored")
        vstep = sem("vstep")
        pool_step = sem("pool_step")
        unwaited = sem("unwaited")

        def signal(name, per_batch, credit=0):
            return Signal(sem(name), per_batch, credit)
        z_ready = signal("z_ready", NT)
        t_gated = signal("t_gated", NT, credit=-NT)
        r_ready = signal("r_ready", NT)
        TR = 2 * KT * NC
        transposed = signal("transposed", TR)
        tr_full_ready = signal("tr_full_ready", TR)
        tr_hi = signal("tr_hi", TR)
        tr_lo = signal("tr_lo", TR)
        proj_ready = signal("proj_ready", 8)
        proj_hi = signal("proj_hi", 8)
        proj_lo = signal("proj_lo", 8)
        scores_ready = signal("scores_ready", NT)
        rowmax_ready = signal("rowmax_ready", NT)
        probs_ready = signal("probs_ready", NT)
        pt_ready = signal("pt_ready", NPT)
        pt_hi = signal("pt_hi", NPT)
        pt_lo = signal("pt_lo", NPT)
        pv_ready = signal("pv_ready", NT)
        x1_scaled = signal("x1_scaled", NT)
        x1_ready = signal("x1_ready", NT)
        norm_ready = signal("norm_ready", 4)
        rstd_ready = signal("rstd_ready", 4)
        z2_ready = signal("z2_ready", NT)
        logits_ready = signal("logits_ready", NC)
        shifted_ready = signal("shifted_ready", NC)
        rexp_ready = signal("rexp_ready", NC)
        picks_made = signal("picks_made", NC)
        masks_spread = signal("masks_spread", NC)
        weights_spread = signal("weights_spread", NC)
        masks_ready = signal("masks_ready", 4 * NC)
        wmask_ready = signal("wmask_ready", 2 * NC)
        t_ready = signal("t_ready", 2 * NC)
        t_hi = signal("t_hi", 2 * NC)
        t_lo = signal("t_lo", 2 * NC)
        tm_ready = signal("tm_ready", 4 * NC)
        tm_low_ready = signal("tm_low_ready", 3)
        masks_copied = signal("masks_copied", 2)
        UPB = UPC * NC
        gate_up_ready = signal("gate_up_ready", UPB)
        silu_ready = signal("silu_ready", UPB)
        h_ready = signal("h_ready", UPB, credit=1)
        h_hi = signal("h_hi", UPB)
        h_lo = signal("h_lo", UPB)
        stacked = signal("stacked", 3 * NC)
        h_used = signal("h_used", UPB)
        dsum_ready = signal("dsum_ready", NC, credit=1)
        dsum_hi = signal("dsum_hi", NC)
        dsum_lo = signal("dsum_lo", NC)
        y_ready = signal("y_ready", NT // 2)
        y_scaled = signal("y_scaled", NT, credit=1)
        out_ready = signal("out_ready", NT, credit=1)

        def unit(ci, g, slot, a):
            return ci * UPC + g * 6 + slot * 2 + a

        def half(n):
            return n % UPC // 6 == GROUPS - 1 and n % 2 == 1

        def half_unit(ci, slot):
            return unit(ci, GROUPS - 1, slot, 1)

        def down_order(ci, g):
            slots = (0, 1, 2) if ci or g else (1, 2, 0)
            return [(slot, a) for slot in slots for a in range(2)]

        def down_unit(q):
            ci, g, rest = q // UPC, q % UPC // 6, q % 6
            slot, a = down_order(ci, g)[rest]
            return unit(ci, g, slot, a)

        def down_position(n):
            return [down_unit(q) for q in range(UPB)].index(n)

        def place(n):
            return n if n < RING else place(down_unit(n - RING))

        def pt_banks(i):
            first = sum(-(-(j + 1) // TC) for j in range(i))
            return [(first + q, q * TC, min(TC, i + 1 - q * TC)) for q in range(-(-(i + 1) // TC))]

        LN2_A, LN2_B, LN1_X, LN1_H = range(4)
        NEWTON = 3
        T_BANKS = ((4, 5), (0, 1))
        MASK_BANKS = ((7, 6, 4, 5), (3, 4, 5, 6))
        LOGIT_BANK = (2, 7)
        PV_FIRST = TC

        SPLITS = [("wg", s_wg[:, k, :], [w[:, k, 0:F] for w in wgT]) for k in range(KT)]
        SPLITS += [("wu", s_wu[:, k, 0:FULL], [w[:, k, :] for w in wuT]) for k in range(KT)]
        SPLITS += [("wu", s_wu[:, :, FULL:F], [w[:, :, F:FP] for w in wgT])]
        EARLY = len(SPLITS)
        SPLITS += [("a", s_a[:, :, :, :].rearrange("p g k e -> p (g k e)"), [w[:, :, :, :].rearrange("p g k e -> p (g k e)") for w in aT]),
                   ("wr", s_wr[:, :, :], [w[:, :, :] for w in wrT]),
                   ("bd", s_bd[:, :], [w[:, :] for w in bdT]),
                   ("bg", s_bg[:, :], [w[:, 0:F] for w in bgT]),
                   ("bu", s_bu[:, 0:FULL], [w[:, 0:FULL] for w in buT]), ("bu", s_bu[:, FULL:F], [w[:, F:FP] for w in buT]),
                   ("wd", s_wd[:, 0:FT - 1, :], [w[:, 0:FT - 1, :] for w in wdT]),
                   ("ad", s_ad[:, 0:FT - 1, :], [w[:, 0:FT - 1, :] for w in adT])]
        W_A, W_R, W_BD, W_BG, W_BU, W_BU_REST, W_D, W_AD = range(EARLY, len(SPLITS))
        HALVES = len(SPLITS)
        SPLITS += [("wd", s_wd[:, FT - 1, :], [w[:, FT - 1, :] for w in wdT]),
                   ("ad", s_ad[:, FT - 1, :], [w[:, FT - 1, :] for w in adT])]
        W_D_HALF, W_AD_HALF = range(HALVES, len(SPLITS))
        LATE = len(SPLITS) - EARLY
        LOADS = {"wd": 3, "ad": 3, "a": 2, "ln": 2}

        MOD_BANKS = (0, 1, 2, 3, 6, 7, 2, 3)
        MODT_BANK = 6

        LAST_PIECES = 2

        block = ctx.enter_context(nc.Block())

        def batches(eng, body):
            with eng.Fori(0, B - 1) as b:
                body(b, False)
            body(B - 1, True)

        @block.sync
        def _(sp):
            sp.sem_inc(stored, 16)

            def load(key, dst, src):
                sp.dma_start(dst, src).then_inc(loaded[key], 16)
            load("c", cT[:, :, :], c.rearrange("(k p) b -> p k b", p=P))
            sp.dma_start(xs[:, :, :], x[0].rearrange("(i p) d -> p i d", p=P)).then_inc(x_loaded, 16)
            load("mod", s_mod[:, :, 0:2 * D], wmod[:, 0:2 * D].rearrange("(k p) n -> p k n", p=P))
            load("mod_rest", s_mod[:, :, 2 * D:6 * D], wmod[:, 2 * D:6 * D].rearrange("(k p) n -> p k n", p=P))
            load("qkv", s_qkvT[:, :, :, :].rearrange("p w k d -> p (w k) d"), qkv.rearrange("(k p) d -> p k d", p=P))
            load("o", s_o[:, :, :], o_proj.rearrange("(k p) n -> p k n", p=P))
            load("ln", gammaT[:, :], gamma)
            load("ln", betaT[:, :], beta)
            load("wg", s_wg[:, :, :], Wg.rearrange("(k p) f -> p k f", p=P))
            load("wu", s_wu[:, :, :], Wu.rearrange("(k p) f -> p k f", p=P))
            load("a", s_a[:, 0, :, :], Ag.rearrange("(k p) e -> p k e", p=P))
            load("a", s_a[:, 1, :, :], Au.rearrange("(k p) e -> p k e", p=P))
            load("wr", s_wr[:, :, :], Wr.rearrange("(k p) e -> p k e", p=P))
            load("bd", s_bd[:, :], Bd)
            load("bg", s_bg[:, :], Bg)
            load("bu", s_bu[:, :], Bu)
            for key, dst, src in (("wd", s_wd, Wd), ("ad", s_ad, Ad)):
                load(key, dst[:, 0:FT - 1, :], src[0:(FT - 1) * P, :].rearrange("(j p) n -> p j n", p=P))
                for p0 in (0, FREST):
                    load(key, dst[p0:p0 + FREST, FT - 1, :], src[FULL:F, :])

            def body(b, last):
                if not last:
                    sp.wait_ge(x1_ready.sem, x1_ready.at(b, NT - 1))
                    sp.dma_start(xs[:, :, :], x[b + 1].rearrange("(i p) d -> p i d", p=P)).then_inc(x_loaded, 16)
                for ci in range(NC):
                    n = TC // LAST_PIECES if last and ci == NC - 1 else TC
                    for i in range(ci * TC, (ci + 1) * TC, n):
                        sp.wait_ge(out_ready.sem, out_ready.at(b, i + n - 1))
                        sp.dma_start(out[b, i * P:(i + n) * P, :].rearrange("(i p) d -> p i d", p=P), xr[:, i:i + n, :]).then_inc(stored, 16)
            batches(sp, body)
            sp.wait_ge(stored, 16 + 16 * (NC * B + LAST_PIECES - 1))

        @block.gpsimd
        def _(pool):
            pool.memset(ident[:, :], 0.0).then_inc(consts_made, 1)
            pool.memset(causal[:, :], 0.0).then_inc(consts_made, 1)
            pool.wait_ge(consts_made, 2)
            pool.affine_select(out=ident[:, :], in_=ident[:, :], compare_op=ALU.not_equal, fill=1.0, base=0,
                               pattern=[[-1, P]], channel_multiplier=1).then_inc(consts_made, 1)
            pool.affine_select(out=causal[:, :], in_=causal[:, :], compare_op=ALU.is_ge, fill=MASKED, base=0,
                               pattern=[[-1, P]], channel_multiplier=1).then_inc(consts_made, 1)
            pool.iota(iota8[:, :], pattern=[[1, E]], base=0, channel_multiplier=0,
                      allow_small_or_imprecise_dtypes=True).then_inc(consts_made, 1)
            pool.wait_ge(consts_made, 5)
            pool.tensor_copy(identb[:, :], ident[:, :]).then_inc(consts_made, 1)
            pool.memset(three_halves[:, :], 1.5).then_inc(pads_made, 1)
            for w, f in ((bgT, F), (buT, FULL)):
                for part in w:
                    pool.memset(part[:, f:f + FREST].bitcast(fp32), 0.0).then_inc(pads_made, 1)
            pool.wait_ge(pads_made, 5)
            for w in (wdT[1], adT[1]):
                pool.memset(w[0:FREST, FT - 1, :].bitcast(fp32), 0.0).then_inc(pads_made, 1)
            pool.wait_ge(pads_made, 7)
            steps = [0, 0]

            def link(ins):
                steps[1] += 1
                ins.then_inc(pool_step, 1)
                pool.wait_ge(pool_step, steps[0] + steps[1])

            def newton_step(lo, n, it, done):
                h, a, y = nr_h[:, lo:lo + n], nr_a[:, lo:lo + n], rstd[:, lo:lo + n]
                link(pool.tensor_mul(a, y, y))
                link(pool.tensor_mul(a, a, h))
                link(pool.tensor_add(a, a, three_halves[:, 0:n]))
                last = pool.tensor_mul(y, y, a)
                if it < NEWTON - 1:
                    link(last)
                else:
                    last.then_inc(done, 1)

            def newton(b, which, lo, n, it):
                if it == 0:
                    pool.wait_ge(norm_ready.sem, norm_ready.at(b, which))
                newton_step(lo, n, it, rstd_ready.sem)

            def residual(b, i):
                pool.wait_ge(t_gated.sem, t_gated.at(b, i))
                pool.tensor_add(xs[:, i, :], xs[:, i, :], gated[:, i % 2, :]).then_inc(r_ready.sem, 1)

            def x1_row(b, i):
                if i == 0:
                    pool.wait_ge(r_ready.sem, r_ready.at(b, NT - 1))
                pool.wait_ge(x1_scaled.sem, x1_scaled.at(b, i))
                pool.tensor_add(xr[:, i, :], xr[:, i, :], xs[:, i, :]).then_inc(x1_ready.sem, 1)

            def tr_low(b, q, dst):
                pool.wait_ge(tr_hi.sem, tr_hi.at(b, q))
                pool.tensor_sub(dst[1], tr_full[:, q % 2, :], dst[0].bitcast(fp32)).then_inc(tr_lo.sem, 1)

            def attention_inputs(b, q):
                n, k = divmod(q, KT)
                tr_low(b, q, [t[:, n, k, :] for t in xT])

            def hid_low(b, n):
                pool.wait_ge(h_hi.sem, h_hi.at(b, n))
                pool.tensor_sub(ring[1][:, place(n), :], hid[:, n % HID, :],
                                ring[0][:, place(n), :].bitcast(fp32)).then_inc(h_lo.sem, 1)

            def out_rows(b, tiles):
                for i in tiles:
                    pool.wait_ge(y_scaled.sem, y_scaled.at(b, i))
                    pool.tensor_add(xr[:, i, :], xr[:, i, :], y_gb[:, i % 2, :]).then_inc(out_ready.sem, 1)

            def weight_low(j, done):
                _, src, (hi, lo) = SPLITS[j]
                pool.wait_ge(weight_hi, j + 1)
                pool.tensor_sub(lo, src, hi.bitcast(fp32)).then_inc(done, 1)

            pool.wait_ge(first_ca, 1)
            for i in range(TC, NT):
                pool.wait_ge(first_scaled, i - TC + 1)
                link(pool.tensor_mul(zb[:, i, :], zb[:, i, :], bc[:, 0, CA, :]))
                pool.tensor_add(zb[:, i, :], zb[:, i, :], bc[:, 0, SA, :]).then_inc(first_h_pool, 1)
            for half_tiles in range(2):
                pool.wait_ge(first_guess, half_tiles + 1)
                for it in range(NEWTON):
                    newton_step(half_tiles * TC, TC, it, first_rstd)
            for j in range(EARLY):
                weight_low(j, early_lo)
            for j in (W_A, W_R, W_BD, W_AD):
                weight_low(j, weight_lo)
            pool.wait_ge(first_h, TC)
            pool.wait_ge(gates_ready, 1)
            for i in range(NT):
                if i >= TC:
                    pool.wait_ge(first_h_pool, i - TC + 1)
                link(pool.tensor_mul(gated[:, i % 2, :], zb[:, i, :], bc[:, 0, GA, :]))
                pool.tensor_add(xs[:, i, :], xs[:, i, :], gated[:, i % 2, :]).then_inc(r_ready.sem, 1)
            setup_steps = steps[1]
            POOL_STEPS = 4 * (4 * NEWTON - 1)

            def body(b, last):
                steps[0], steps[1] = b * POOL_STEPS + setup_steps, 0
                for i in range(TC):
                    x1_row(b, i)
                for it in range(NEWTON):
                    newton(b, LN2_A, 0, TC, it)
                x1_row(b, TC)
                x1_row(b, TC + 1)
                for k in range(KT):
                    tr_low(b, KT * NC + k, [t[:, 0, k, :] for t in xT])
                x1_row(b, TC + 2)
                x1_row(b, TC + 3)
                for ci in range(NC):
                    for r in range(UPC):
                        if ci == 0:
                            if r == 0:
                                for m in range(1, 4):
                                    which, g = divmod(m, 2)
                                    pool.wait_ge(masks_copied.sem, masks_copied.at(b, which))
                                    pool.wait_ge(t_lo.sem, t_lo.at(b, g))
                                    pool.tensor_mul(tm[1][:, m, :], t_split[1][:, g, :].bitcast(fp32), wmask[:, which, :]).then_inc(tm_low_ready.sem, 1)
                            if r == 2:
                                newton(b, LN2_B, TC, TC, 0)
                                newton(b, LN2_B, TC, TC, 1)
                            if r == 3:
                                newton(b, LN2_B, TC, TC, 2)
                            if r == 7:
                                for k in range(KT):
                                    tr_low(b, KT * NC + KT + k, [t[:, 2, k, :] for t in xT])
                            if not last and 13 <= r < 13 + NEWTON:
                                newton(b, LN1_X, 0, NT, r - 13)
                        elif not last:
                            if 5 <= r < 5 + NT:
                                residual(b + 1, r - 5)
                            if r == 13:
                                newton(b, LN1_H, 0, NT, 0)
                                newton(b, LN1_H, 0, NT, 1)
                            if r == 14:
                                newton(b, LN1_H, 0, NT, 2)
                        hid_low(b, ci * UPC + r)
                        if ci == 1 and r == 0:
                            out_rows(b, (2, 3))
                    if ci == 0:
                        pool.wait_ge(dsum_hi.sem, dsum_hi.at(b, 0))
                        pool.tensor_sub(tm[1][:, 3, :], wmask[:, 0, :], tm[0][:, 3, :].bitcast(fp32)).then_inc(dsum_lo.sem, 1)
                        out_rows(b, (0, 1))
                    elif not last:
                        for q in range(KT * NC):
                            attention_inputs(b + 1, q)
                out_rows(b, range(TC, NT))
                if not last:
                    assert steps[1] == POOL_STEPS, steps
            batches(pool, body)

        @block.scalar
        def _(act):
            act.wait_ge(loaded["c"], 16)
            nc.scalar.activation(scT[:, :, :], cT[:, :, :], ACT.Silu).then_inc(sc_ready, 1)

            def modulation(b, halves=(0, 1)):
                for h in halves:
                    act.wait_ge(mod_ready, 2 * b + h + 1)
                    nc.scalar.activation(bc[:, b, 2 * h:2 * h + 2, :].rearrange("p t d -> p (t d)"),
                                         ps[:, MOD_BANKS[2 * b + h], :], ACT.Copy).then_inc(mod_copied, 1)

            act.wait_ge(x_loaded, 16)
            act.wait_ge(first_mean, 1)
            for i in range(TC, NT):
                nc.scalar.activation(zb[:, i, :], xs[:, i, :], ACT.Identity, bias=neg_mean[:, i - TC:i - TC + 1]).then_inc(first_centred, 1)
            modulation(0, (0,))
            act.wait_ge(first_centred, NT - TC)
            act.wait_ge(first_scale, 1)
            for i in range(TC, NT):
                nc.scalar.activation(zb[:, i, :], zb[:, i, :], ACT.Copy, scale=rstd[:, i:i + 1]).then_inc(first_scaled, 1)
            modulation(0, (1,))

            def weight_high(j):
                key, src, (hi, _) = SPLITS[j]
                act.wait_ge(loaded[key], 16 * LOADS.get(key, 1))
                nc.scalar.activation(hi, src, ACT.Copy).then_inc(weight_hi, 1)

            def tr_high(b, q, dst):
                act.wait_ge(tr_full_ready.sem, tr_full_ready.at(b, q))
                nc.scalar.activation(dst, tr_full[:, q % 2, :], ACT.Copy).then_inc(tr_hi.sem, 1)

            def attention_inputs(b, qs):
                for q in qs:
                    tr_high(b, q, xT[0][:, q // KT, q % KT, :])

            def queries_values(b, js):
                for j in js:
                    act.wait_ge(proj_ready.sem, proj_ready.at(b, j))
                    if j < 4:
                        n, m = divmod(j, KT)
                        nc.scalar.activation(qT[0][:, m, n * CH:(n + 1) * CH], ps[:, j, :], ACT.Copy).then_inc(proj_hi.sem, 1)
                    else:
                        i = 2 * (j - 4)
                        nc.scalar.activation(vv[0][:, i:i + 2, :].rearrange("p i d -> p (i d)"), ps[:, j, :], ACT.Copy).then_inc(proj_hi.sem, 1)

            for j in range(KT):
                weight_high(j)
            for j, (w, scale) in enumerate(((wqk, SCORE_SCALE), (wvo, 1.0))):
                act.wait_ge(product_ready, j + 1)
                nc.scalar.activation(w[0][:, :, :].rearrange("p k d -> p (k d)"), ps[:, 4 + j, :], ACT.Copy,
                                     scale=scale).then_inc(product_hi, 1)
            for j in range(KT, EARLY):
                weight_high(j)
            modulation(1)
            for j in range(EARLY, W_D):
                weight_high(j)
            modulation(2)
            weight_high(W_D)
            attention_inputs(0, range(KT))
            for b in range(3, B):
                modulation(b)
            act.wait_ge(mod_ready, 2 * B + 1)
            nc.scalar.activation(modT[:, :, :, :].rearrange("p t k b -> p (t k b)"), ps[:, MODT_BANK, 0:2 * KT * B], ACT.Copy).then_inc(mod_copied, 1)
            for j in range(W_AD, len(SPLITS)):
                weight_high(j)
            attention_inputs(0, range(KT, KT * NC))
            act.wait_ge(early_lo, EARLY)
            queries_values(0, range(6))

            def body(b, last):
                def scores_exp(i):
                    w = (i + 1) * P
                    act.wait_ge(rowmax_ready.sem, rowmax_ready.at(b, i))
                    if i >= 2:
                        act.wait_ge(pt_ready.sem, pt_ready.at(b, pt_banks(i - 2)[-1][0]))
                    banks = ps[:, 2 * (i % 2):2 * (i % 2) + 2, :].rearrange("p n s -> p (n s)")
                    nc.scalar.activation(probs[:, i % 2, 0:w], banks[:, 0:w], ACT.Exp, bias=rowmax[:, i:i + 1],
                                         accum_out=rowsum[:, i:i + 1]).then_inc(probs_ready.sem, 1)

                def probs_high(t):
                    for e, j0, nj in pt_banks(t):
                        if t == 0:
                            act.wait_ge(weight_lo, LATE)
                        act.wait_ge(pt_ready.sem, pt_ready.at(b, e))
                        if t >= 2:
                            act.wait_ge(pv_ready.sem, pv_ready.at(b, t - 2))
                        nc.scalar.activation(pT[0][:, t % 2, j0:j0 + nj, :].rearrange("p j s -> p (j s)"),
                                             ps[:, 4 + e % 2, 0:nj * P], ACT.Copy).then_inc(pt_hi.sem, 1)

                for i in range(NT):
                    if i >= 2:
                        probs_high(i - 1)
                    scores_exp(i)
                    if i == 1:
                        probs_high(0)
                    if i < 2:
                        queries_values(b, (6 + i,))
                tr_high(b, KT * NC, xT[0][:, 0, 0, :])
                probs_high(NT - 1)
                tr_high(b, KT * NC + 1, xT[0][:, 0, 1, :])

                def router_exp(ci):
                    act.wait_ge(shifted_ready.sem, shifted_ready.at(b, ci))
                    nc.scalar.activation(pr[:, :, :], lg[:, :, :], ACT.Exp).then_inc(rexp_ready.sem, 1)

                def adapter_input_high(ci, g):
                    act.wait_ge(t_ready.sem, t_ready.at(b, ci * 2 + g))
                    nc.scalar.activation(t_split[0][:, g, :], ps[:, T_BANKS[ci][g], :], ACT.Copy).then_inc(t_hi.sem, 1)

                def spread_weights(ci):
                    act.wait_ge(picks_made.sem, picks_made.at(b, ci))
                    if ci:
                        act.wait_ge(h_used.sem, h_used.at(b, down_position(unit(ci - 1, GROUPS - 1, 1, 1))))
                    nc.scalar.activation(pick_er[:, 2:4, :, :].rearrange("p m t (e r) -> p (m t e) r", r=R),
                                         pick[:, 2:4, :, :].rearrange("p m t e -> p (m t e)").unsqueeze(2)
                                         .to_broadcast([P, 2 * TC * E, R]), ACT.Copy).then_inc(weights_spread.sem, 1)

                def dsum_high(ci):
                    act.wait_ge(dsum_ready.sem, dsum_ready.at(b, ci))
                    nc.scalar.activation(tm[0][:, 3, :], wmask[:, 0, :], ACT.Copy).then_inc(dsum_hi.sem, 1)

                def silu(n):
                    act.wait_ge(gate_up_ready.sem, gate_up_ready.at(b, n))
                    if n >= 2:
                        act.wait_ge(h_ready.sem, h_ready.at(b, n - 2))
                    if half(n):
                        nc.scalar.activation(act_s[FREST:P, n % 2, :], ps[0:FREST, 2 * (n % 2), :], ACT.Silu).then_inc(silu_ready.sem, 1)
                    else:
                        nc.scalar.activation(act_s[:, n % 2, :], ps[:, 2 * (n % 2), :], ACT.Silu).then_inc(silu_ready.sem, 1)

                def high(n):
                    act.wait_ge(h_ready.sem, h_ready.at(b, n))
                    if n >= RING:
                        act.wait_ge(h_used.sem, h_used.at(b, n - RING))
                    p0 = FREST if half(n) else 0
                    nc.scalar.activation(ring[0][p0:P, place(n), :], hid[p0:P, n % HID, :], ACT.Copy).then_inc(h_hi.sem, 1)

                def stack(n):
                    act.wait_ge(h_lo.sem, h_lo.at(b, n))
                    nc.scalar.activation(ring[0][0:FREST, place(n), :], ring[1][FREST:P, place(n), :].bitcast(fp32), ACT.Copy).then_inc(stacked.sem, 1)

                router_exp(0)
                for g in range(2):
                    adapter_input_high(0, g)
                spread_weights(0)
                for m in range(2):
                    act.wait_ge(masks_ready.sem, masks_ready.at(b, m))
                    nc.scalar.activation(wmask[:, m, :], ps[:, MASK_BANKS[0][m], :], ACT.Copy).then_inc(masks_copied.sem, 1)
                for ci in range(NC):
                    n0 = ci * UPC
                    silu(n0)
                    for r in range(1, UPC):
                        silu(n0 + r)
                        if ci == 0 and r == 13:
                            router_exp(1)
                        high(n0 + r - 1)
                        if r in (15, 17):
                            stack(n0 + r - 2)
                        if r in (3, 5):
                            slot = (3, 5).index(r)
                            act.wait_ge(masks_ready.sem, masks_ready.at(b, ci * 4 + 2 + slot))
                            if ci == 0:
                                act.wait_ge(tm_ready.sem, tm_ready.at(b, 2 * slot + 1))
                                act.wait_ge(tm_low_ready.sem, tm_low_ready.at(b, 2 * slot))
                            elif slot == 0:
                                act.wait_ge(dsum_lo.sem, dsum_lo.at(b, ci - 1))
                            nc.scalar.activation(wmask[:, slot, :], ps[:, MASK_BANKS[ci][2 + slot], :], ACT.Copy).then_inc(wmask_ready.sem, 1)
                        if ci == 0 and r == 7:
                            for k in range(KT):
                                tr_high(b, KT * NC + KT + k, xT[0][:, 2, k, :])
                    high(n0 + UPC - 1)
                    if ci == 1 and not last:
                        attention_inputs(b + 1, range(KT))
                    stack(n0 + UPC - 1)
                    if ci == 0:
                        spread_weights(1)
                        adapter_input_high(1, 0)
                        adapter_input_high(1, 1)
                        dsum_high(0)
                    elif not last:
                        attention_inputs(b + 1, range(KT, KT * NC))
                        queries_values(b + 1, range(1))
                        dsum_high(1)
                        queries_values(b + 1, range(1, 6))
                    else:
                        dsum_high(1)
            batches(act, body)

        @block.vector
        def _(dve):
            V = nc.vector
            for s in (h_ready, dsum_ready, y_scaled, out_ready):
                dve.sem_inc(s.sem, 1)
            steps = [0, 0]

            def link(ins):
                steps[1] += 1
                ins.then_inc(vstep, 1)
                dve.wait_ge(vstep, steps[0] + steps[1])

            def link_apart(ins):
                link(ins)
                dve.sem_inc(unwaited, 1)

            def mark(ins):
                steps[1] += 1
                ins.then_inc(vstep, 1)

            def settle():
                dve.wait_ge(vstep, steps[0] + steps[1])

            def guess(lo, n):
                v, y = nr_v[:, lo:lo + n], rstd[:, lo:lo + n]
                link(V.tensor_scalar_add(v, mv[:, lo:lo + n, 1], EPS))
                mark(V.tensor_scalar(nr_h[:, lo:lo + n], v, -0.5, None, ALU.mult))
                link(V.tensor_scalar(nr_i[:, lo:lo + n], v.bitcast(i32), 1, None, ALU.logical_shift_right))
                return V.tensor_scalar(y.bitcast(i32), nr_i[:, lo:lo + n], -1.0, float(0x5f3759df), ALU.mult, ALU.add)

            def rsqrt(lo, n):
                v, a, y = nr_v[:, lo:lo + n], nr_a[:, lo:lo + n], rstd[:, lo:lo + n]
                link(guess(lo, n))
                for _ in range(NEWTON):
                    link(V.tensor_mul(a, y, y))
                    link(V.scalar_tensor_tensor(a, a, -0.5, v, ALU.mult, ALU.mult))
                    link(V.scalar_tensor_tensor(y, a, 1.5, y, ALU.add, ALU.mult))

            def moments(tiles):
                settle()
                dve.sem_inc(unwaited, 1)
                for i in tiles:
                    last = V.bn_aggr(mv[:, i, :], stat[:, i, :])
                link(last)

            def x_stats(tiles):
                for i in tiles:
                    mark(V.bn_stats(stat[:, i, :], xs[:, i, :]))

            def h_rows(b, i):
                return V.scalar_tensor_tensor(zb[:, i, :], zb[:, i, :], rstd[:, i:i + 1], bc[:, b, SA, :], ALU.mult, ALU.add)

            def ln1_h(b, tiles):
                for i in tiles:
                    mark(V.scalar_tensor_tensor(zb[:, i, :], xs[:, i, :], mv[:, i, 0:1], bc[:, b, CA, :], ALU.subtract, ALU.mult))
                settle()
                for i in tiles:
                    mark(h_rows(b, i))
                settle()
                for i in tiles:
                    if i >= 2:
                        dve.wait_ge(r_ready.sem, r_ready.at(b, i - 2))
                    V.tensor_mul(gated[:, i % 2, :], zb[:, i, :], bc[:, b, GA, :]).then_inc(t_gated.sem, 1)
                for i in tiles:
                    mark(V.bn_stats(stat[:, i, :], zb[:, i, :]))

            def normalise(i, src, sig, dst=zb):
                V.tensor_scalar(dst[:, i, :], src[:, i, :], mv[:, i, 0:1], rstd[:, i:i + 1], ALU.subtract, ALU.mult).then_inc(sig.sem, 1)

            def gate(b, step):
                g = bc[:, b, GA:GB + 1, :]
                if step == 0:
                    mark(V.tensor_scalar_add(bc[:, b, CA, :], bc[:, b, CA, :], 1.0))
                elif step == 1:
                    mark(V.tensor_scalar(y_gb[:, :, :], g, 0.0, 2.0, ALU.is_ge, ALU.mult))
                    mark(V.scalar_tensor_tensor(gated[:, :, :], g, -1.0, g, ALU.mult, ALU.max))
                elif step == 2:
                    settle()
                    mark(V.tensor_scalar_max(gated[:, :, :], gated[:, :, :], 0.25))
                else:
                    settle()
                    mark(V.scalar_tensor_tensor(g, y_gb[:, :, :], -1.0, gated[:, :, :], ALU.add, ALU.mult))

            def tr_scale(b, q, bank, scale, bias):
                dve.wait_ge(transposed.sem, transposed.at(b, q))
                if not (isinstance(b, int) and b == 0 and q < 2):
                    dve.wait_ge(tr_lo.sem, tr_lo.at(b, q - 2))
                V.tensor_scalar(tr_full[:, q % 2, :], ps[:, bank, :], scale, bias, ALU.mult, ALU.add).then_inc(tr_full_ready.sem, 1)

            def attention_scale(b, qs=range(KT * NC)):
                for q in qs:
                    k = q % KT
                    tr_scale(b, q, q, gammaT[:, k:k + 1], betaT[:, k:k + 1])

            def attention_low(q):
                n, k = divmod(q, KT)
                hi, lo = [t[:, n, k, :] for t in xT]
                dve.wait_ge(tr_hi.sem, tr_hi.at(0, q))
                V.tensor_sub(lo, tr_full[:, q % 2, :], hi.bitcast(fp32)).then_inc(tr_lo.sem, 1)

            def queries_values(b, js):
                for j in js:
                    dve.wait_ge(proj_hi.sem, proj_hi.at(b, j))
                    if j < 4:
                        n, m = divmod(j, KT)
                        hi, lo = [t[:, m, n * CH:(n + 1) * CH] for t in qT]
                    else:
                        i = 2 * (j - 4)
                        hi, lo = [t[:, i:i + 2, :].rearrange("p i d -> p (i d)") for t in vv]
                    V.tensor_sub(lo, ps[:, j, :], hi.bitcast(fp32)).then_inc(proj_lo.sem, 1)

            def weight_low(j):
                _, src, (hi, lo) = SPLITS[j]
                if j >= HALVES:
                    src, hi, lo = src[FREST:P], hi[FREST:P], lo[FREST:P]
                dve.wait_ge(weight_hi, j + 1)
                V.tensor_sub(lo, src, hi.bitcast(fp32)).then_inc(weight_lo, 1)

            dve.wait_ge(sc_ready, 1)
            V.tensor_copy(s_scb[:, :, :, :].rearrange("p k b n -> p (k b) n"),
                          scT[:, :, :].rearrange("p k b -> p (k b)").unsqueeze(2).to_broadcast([P, KT * B, P])).then_inc(scb_ready, 1)
            dve.wait_ge(x_loaded, 16)
            first, second = range(TC), range(TC, NT)
            x_stats(range(NT))
            moments(range(NT))
            V.tensor_scalar(neg_mean[:, :], mv[:, TC:NT, 0], -1.0, None, ALU.mult).then_inc(first_mean, 1)
            rsqrt(0, NT)
            dve.sem_inc(first_scale, 1)
            dve.wait_ge(mod_copied, 1)
            gate(0, 0)
            settle()
            dve.sem_inc(first_ca, 1)
            for i in first:
                mark(V.scalar_tensor_tensor(zb[:, i, :], xs[:, i, :], mv[:, i, 0:1], bc[:, 0, CA, :], ALU.subtract, ALU.mult))
            settle()
            for i in first:
                h_rows(0, i).then_inc(first_h, 1)
            for i in first:
                dve.wait_ge(first_h, i + 1)
                mark(V.bn_stats(stat[:, i, :], zb[:, i, :]))
            moments(first)
            guess(0, TC).then_inc(first_guess, 1)
            for j, (w, scale) in enumerate(((wqk, SCORE_SCALE), (wvo, 1.0))):
                dve.wait_ge(product_hi, j + 1)
                hi, lo = [t[:, :, :].rearrange("p k d -> p (k d)") for t in w]
                V.scalar_tensor_tensor(lo, ps[:, 4 + j, :], scale, hi.bitcast(fp32), ALU.mult, ALU.subtract).then_inc(product_lo, 1)
            for i in second:
                dve.wait_ge(first_h_pool, i - TC + 1)
                mark(V.bn_stats(stat[:, i, :], zb[:, i, :]))
            moments(second)
            guess(TC, TC).then_inc(first_guess, 1)
            dve.wait_ge(first_rstd, 1)
            for i in first:
                normalise(i, zb, z_ready, xr)
            dve.wait_ge(mod_copied, 2)
            gate(0, 1)
            gate(0, 2)
            weight_low(W_BG)
            dve.wait_ge(loaded["ln"], 32)
            attention_scale(0, range(KT))
            for q in range(KT):
                attention_low(q)
            dve.wait_ge(first_rstd, 2)
            for i in second:
                normalise(i, zb, z_ready, xr)
            gate(0, 3)
            settle()
            dve.sem_inc(gates_ready, 1)
            weight_low(W_BU_REST)
            attention_scale(0, range(KT, KT * NC))
            for q in range(KT, KT * NC):
                attention_low(q)
            dve.wait_ge(mod_copied, 2 * B + 1)
            link(V.tensor_scalar_add(modT[:, 1, :, :], modT[:, 1, :, :], 1.0))
            dve.wait_ge(early_lo, EARLY)
            queries_values(0, (0,))
            weight_low(W_D)
            queries_values(0, (1, 2))
            weight_low(W_BU)
            queries_values(0, (3, 4))
            weight_low(W_D_HALF)
            weight_low(W_AD_HALF)
            queries_values(0, (5,))
            setup_steps = steps[1]
            VSTEPS = 95

            def body(b, last):
                steps[0], steps[1] = b * VSTEPS + setup_steps, 0

                def ffn_scale(c2, bank0):
                    for k in range(KT):
                        tr_scale(b, KT * NC + c2 * KT + k, bank0 + k, modT[:, 1, k, bass.ds(b, 1)], modT[:, 0, k, bass.ds(b, 1)])

                def x1_stats(i):
                    dve.wait_ge(x1_ready.sem, x1_ready.at(b, i))
                    mark(V.bn_stats(stat[:, i, :], xr[:, i, :]))

                def x1_product(t):
                    if t == 0:
                        dve.wait_ge(stored, b * (16 * NC) + 16)
                    dve.wait_ge(pv_ready.sem, pv_ready.at(b, t))
                    settle()
                    V.scalar_tensor_tensor(xr[:, t, :], ps[:, 6 + t % 2, 0:D], rinv[:, t:t + 1], bc[:, b, GA, :],
                                           ALU.mult, ALU.mult).then_inc(x1_scaled.sem, 1)

                for i in range(NT + 1):
                    if i < NT:
                        w = (i + 1) * P
                        banks = ps[:, 2 * (i % 2):2 * (i % 2) + 2, :].rearrange("p n s -> p (n s)")
                        dve.wait_ge(scores_ready.sem, scores_ready.at(b, i))
                        V.tensor_reduce(rowmax[:, i:i + 1], banks[:, 0:w], X, ALU.max, negate=True).then_inc(rowmax_ready.sem, 1)
                    if 3 <= i < 3 + TC:
                        x1_stats(i - 3)
                    if i == 3 + TC - 1:
                        moments(range(TC))
                        guess(0, TC).then_inc(norm_ready.sem, 1)
                    if i == NT:
                        ffn_scale(0, 0)
                    if i >= 1:
                        t = i - 1
                        dve.wait_ge(probs_ready.sem, probs_ready.at(b, t))
                        mark(V.reciprocal(rinv[:, t:t + 1], rowsum[:, t:t + 1]))
                        if i == NT - 1:
                            dve.wait_ge(rstd_ready.sem, rstd_ready.at(b, LN2_A))
                            for tile in range(TC):
                                normalise(tile, xr, z2_ready)
                        for e, j0, nj in pt_banks(t):
                            dve.wait_ge(pt_hi.sem, pt_hi.at(b, e))
                            hi, lo = [p[:, t % 2, j0:j0 + nj, :].rearrange("p j s -> p (j s)") for p in pT]
                            V.tensor_sub(lo, ps[:, 4 + e % 2, 0:nj * P], hi.bitcast(fp32)).then_inc(pt_lo.sem, 1)
                    if i < 2:
                        queries_values(b, (6 + i,))
                    if i >= 2:
                        x1_product(i - 2)

                def router_shift(ci):
                    logits = ps[:, LOGIT_BANK[ci], 0:TC * 2 * E].rearrange("p (t h e) -> p h t e", h=2, e=E)
                    dve.wait_ge(logits_ready.sem, logits_ready.at(b, ci))
                    link(V.tensor_copy(pr[:, :, :], logits[:, 1, :, :]))
                    link(V.tensor_add(lg[:, :, :], logits[:, 0, :, :], pr[:, :, :]))
                    link(V.tensor_reduce(lmax[:, :], lg[:, :, :], X, ALU.max))
                    V.tensor_sub(lg[:, :, :], lg[:, :, :], lmax[:, :].unsqueeze(2).to_broadcast([P, TC, E])).then_inc(shifted_ready.sem, 1)

                def router_probs(ci):
                    dve.wait_ge(rexp_ready.sem, rexp_ready.at(b, ci))
                    link(V.tensor_reduce(lsum[:, :], pr[:, :, :], X, ALU.add))
                    link(V.reciprocal(lsum[:, :], lsum[:, :]))
                    link_apart(V.tensor_mul(pr[:, :, :], pr[:, :, :], lsum[:, :].unsqueeze(2).to_broadcast([P, TC, E])))

                def router_top():
                    for t in range(TC):
                        last_max = V.max(top[:, t, :], pr[:, t, :])
                    link_apart(last_max)
                    for t in range(TC):
                        last_idx = V.max_index(topi[:, t, :], top[:, t, :], pr[:, t, :])
                    mark(last_idx)

                def router_picks():
                    settle()
                    link(V.tensor_copy(topf[:, :, 0:2], topi[:, :, 0:2]))
                    for s in range(2):
                        last_hot = V.tensor_tensor(onehot[:, s, :, :], iota8[:, :].unsqueeze(1).to_broadcast([P, TC, E]),
                                                   topf[:, :, s:s + 1].to_broadcast([P, TC, E]), ALU.is_equal)
                    link(last_hot)
                    mark(V.tensor_sub(pick[:, 1, :, :], onehot[:, 1, :, :], onehot[:, 0, :, :]))
                    V.tensor_scalar_mul(pick[:, 0, :, :], onehot[:, 0, :, :], SCALING)
                    for s in range(2):
                        V.scalar_tensor_tensor(pick[:, 2 + s, :, :], onehot[:, s, :, :], SCALING,
                                               top[:, :, s:s + 1].to_broadcast([P, TC, E]), ALU.mult, ALU.mult)
                    settle()
                    V.tensor_scalar_mul(pick[:, 1, :, :], pick[:, 1, :, :], SCALING).then_inc(picks_made.sem, 1)

                def spread_masks(ci):
                    if ci:
                        dve.wait_ge(h_used.sem, h_used.at(b, down_position(unit(ci - 1, GROUPS - 1, 1, 1))))
                    dve.wait_ge(picks_made.sem, picks_made.at(b, ci))
                    V.tensor_copy(pick_er[:, 0:2, :, :].rearrange("p m t (e r) -> p (m t e) r", r=R),
                                  pick[:, 0:2, :, :].rearrange("p m t e -> p (m t e)").unsqueeze(2)
                                  .to_broadcast([P, 2 * TC * E, R])).then_inc(masks_spread.sem, 1)

                def adapter_input_low(ci, g):
                    dve.wait_ge(t_hi.sem, t_hi.at(b, ci * 2 + g))
                    V.tensor_sub(t_split[1][:, g, :], ps[:, T_BANKS[ci][g], :], t_split[0][:, g, :].bitcast(fp32)).then_inc(t_lo.sem, 1)

                def masked(ci, m):
                    which, g = divmod(m, 2)
                    if ci:
                        dve.wait_ge(masks_ready.sem, masks_ready.at(b, ci * 4 + which))
                        mask = ps[:, MASK_BANKS[ci][which], :]
                    else:
                        dve.wait_ge(masks_copied.sem, masks_copied.at(b, which))
                        mask = wmask[:, which, :]
                    dve.wait_ge(t_lo.sem, t_lo.at(b, ci * 2 + g))
                    if m == 3 and ci == 1:
                        dve.wait_ge(y_ready.sem, y_ready.at(b, TC // 2 - 1))
                    for h in range(1 if ci == 0 and m else 2):
                        last = V.tensor_mul(tm[h][:, m, :], t_split[h][:, g, :].bitcast(fp32), mask)
                    last.then_inc(tm_ready.sem, 1)

                def hidden(n):
                    dve.wait_ge(silu_ready.sem, silu_ready.at(b, n))
                    if n >= HID:
                        dve.wait_ge(h_lo.sem, h_lo.at(b, n - HID))
                    if half(n):
                        V.tensor_mul(hid[FREST:P, n % HID, :], act_s[FREST:P, n % 2, :], ps[FREST:P, 2 * (n % 2), :]).then_inc(h_ready.sem, 1)
                    else:
                        V.tensor_mul(hid[:, n % HID, :], act_s[:, n % 2, :], ps[:, 2 * (n % 2) + 1, :]).then_inc(h_ready.sem, 1)

                def dsum(ci):
                    for s in range(2):
                        dve.wait_ge(wmask_ready.sem, wmask_ready.at(b, ci * 2 + s))
                        dve.wait_ge(h_used.sem, h_used.at(b, down_position(unit(ci, GROUPS - 1, 1 + s, 1))))
                        mark(V.tensor_mul(wmask[:, s, :], wmask[:, s, :], ps[:, 4 + s, :]))
                    settle()
                    V.tensor_add(wmask[:, 0, :], wmask[:, 0, :], wmask[:, 1, :]).then_inc(dsum_ready.sem, 1)

                def dsum_low(ci):
                    dve.wait_ge(dsum_hi.sem, dsum_hi.at(b, ci))
                    V.tensor_sub(tm[1][:, 3, :], wmask[:, 0, :], tm[0][:, 3, :].bitcast(fp32)).then_inc(dsum_lo.sem, 1)

                def scaled_sums(ci, tiles=range(TC)):
                    for t in tiles:
                        i = ci * TC + t
                        dve.wait_ge(y_ready.sem, y_ready.at(b, i // 2))
                        if ci or t >= 2:
                            dve.wait_ge(out_ready.sem, out_ready.at(b, i - 2))
                        V.tensor_mul(y_gb[:, t % 2, :], ps[:, 6 + t // 2, t % 2 * D:(t % 2 + 1) * D], bc[:, b, GB, :]).then_inc(y_scaled.sem, 1)

                router_shift(0)
                x1_stats(TC)
                x1_stats(TC + 1)
                router_probs(0)
                router_top()
                router_picks()
                spread_masks(0)
                x1_product(NT - 1)
                x1_stats(TC + 2)
                for g in range(2):
                    adapter_input_low(0, g)
                masked(0, 0)
                masked(0, 1)
                hidden(0)
                masked(0, 2)
                hidden(1)
                masked(0, 3)
                for r in range(2, UPC):
                    hidden(r)
                    if r == 2:
                        x1_stats(TC + 3)
                        moments(range(TC, NT))
                        guess(TC, TC).then_inc(norm_ready.sem, 1)
                    if r == 5:
                        dve.wait_ge(rstd_ready.sem, rstd_ready.at(b, LN2_B))
                        for i in range(TC, NT):
                            normalise(i, xr, z2_ready)
                    if r == 7:
                        ffn_scale(1, 6)
                    if r == 9:
                        router_shift(1)
                    if r == 13:
                        router_probs(1)
                    if r == 14:
                        router_top()
                    if r == 15:
                        router_picks()
                    if not last:
                        if r == 7:
                            dve.wait_ge(x_loaded, (b + 1) * 16 + 16)
                        if r in (7, 8, 10, 11):
                            i = 2 * (7, 8, 10, 11).index(r)
                            x_stats((i, i + 1))
                        if r == 11:
                            moments(range(NT))
                            guess(0, NT).then_inc(norm_ready.sem, 1)
                        if r == 12:
                            dve.wait_ge(out_ready.sem, out_ready.at(b, -1))
                            gate(b + 1, 0)
                        if r == 16:
                            gate(b + 1, 1)
                            gate(b + 1, 2)
                        if r == 17:
                            gate(b + 1, 3)
                spread_masks(1)
                adapter_input_low(1, 0)
                dsum(0)
                adapter_input_low(1, 1)
                masked(1, 0)
                masked(1, 1)
                n0 = UPC
                hidden(n0)
                masked(1, 2)
                scaled_sums(0, (0, 1))
                masked(1, 3)
                hidden(n0 + 1)
                scaled_sums(0, (2, 3))
                for r in range(2, UPC):
                    hidden(n0 + r)
                    if not last:
                        if r == 4:
                            dve.wait_ge(rstd_ready.sem, rstd_ready.at(b, LN1_X))
                        if 4 <= r < 4 + NT:
                            ln1_h(b + 1, (r - 4,))
                        if r == 4 + NT:
                            moments(range(NT))
                            guess(0, NT).then_inc(norm_ready.sem, 1)
                        if r == 15:
                            dve.wait_ge(rstd_ready.sem, rstd_ready.at(b, LN1_H))
                        if r >= 15:
                            for i in range(3 * (r - 15), min(3 * (r - 14), NT)):
                                normalise(i, zb, z_ready)
                if not last:
                    attention_scale(b + 1)
                dsum(1)
                if not last:
                    queries_values(b + 1, range(1))
                dsum_low(1)
                if not last:
                    queries_values(b + 1, range(1, 4))
                scaled_sums(1)
                if not last:
                    queries_values(b + 1, range(4, 6))
                    assert steps[1] == VSTEPS, steps
            batches(dve, body)

        @block.tensor
        def _(pe):
            def mm(o, w, v, start, stop):
                return nc.tensor.matmul(o, w, v, start=start, stop=stop, skip_group_check=True)

            def product(o, w, v, start, stop):
                mm(o, w[0], v[0], start, False)
                mm(o, w[0], v[1], False, False)
                return mm(o, w[1], v[0], False, stop)

            def transpose(o, src, idn):
                return nc.tensor.transpose(o, src, idn)

            def modulation(b):
                for h in range(2):
                    if b == B - 1:
                        pe.wait_ge(mod_copied, 2 + h + 1)
                    if b == 0:
                        pe.wait_ge(loaded[("mod", "mod_rest")[h]], 16)
                    for p0, c0, w in (((0, 0, 2 * D),), ((0, 2 * D, D), (D, 5 * D, D)))[h]:
                        for k in range(KT):
                            last_mm = mm(ps[:, MOD_BANKS[2 * b + h], p0:p0 + w], s_scb[:, k, b, :], s_mod[:, k, c0:c0 + w], k == 0, k == KT - 1)
                    last_mm.then_inc(mod_ready, 1)
            pe.wait_ge(scb_ready, 1)
            modulation(0)
            pe.wait_ge(loaded["qkv"], 16)
            pe.wait_ge(loaded["o"], 16)
            for j, (left, right) in enumerate(((0, s_qkvT[:, 1, :, :]), (2, s_o))):
                for d in range(KT):
                    for k in range(KT):
                        last_mm = mm(ps[:, 4 + j, d * D:(d + 1) * D], s_qkvT[:, left, k, d * P:(d + 1) * P], right[:, k, :],
                                     k == 0, k == KT - 1)
                last_mm.then_inc(product_ready, 1)
            def transposes(b, q, bank, k, tiles, src=zb):
                for t, i in enumerate(tiles):
                    last = transpose(ps[:, bank, t * P:(t + 1) * P], src[:, i, k * P:(k + 1) * P], ident[:, :])
                last.then_inc(transposed.sem, 1)

            def attention_transposes(b, n, src=zb):
                for k in range(KT):
                    q = n * KT + k
                    pe.wait_ge(z_ready.sem, z_ready.at(b, (n + 1) * TC - 1))
                    transposes(b, q, q, k, range(n * TC, (n + 1) * TC), src)

            def queries(b, js=range(4)):
                for j in js:
                    n, m = divmod(j, KT)
                    pe.wait_ge(tr_lo.sem, tr_lo.at(b, n * KT + 1))
                    for k in range(KT):
                        last_mm = product(ps[:, j, :], [w[:, k, m * P:(m + 1) * P] for w in wqk],
                                          [t[:, n, k, :] for t in xT], k == 0, k == KT - 1)
                    last_mm.then_inc(proj_ready.sem, 1)

            def values(b, tiles):
                for i in tiles:
                    n, t = divmod(i, TC)
                    if i == 0:
                        pe.wait_ge(dsum_ready.sem, dsum_ready.at(b, -1))
                    if i == NT // 2:
                        pe.wait_ge(y_scaled.sem, y_scaled.at(b, -1))
                    for k in range(KT):
                        last_mm = product(ps[:, 4 + i // 2, i % 2 * D:(i % 2 + 1) * D], [x_[:, n, k, t * P:(t + 1) * P] for x_ in xT],
                                          [w[:, k, :] for w in wvo], k == 0, k == KT - 1)
                    if i % 2:
                        last_mm.then_inc(proj_ready.sem, 1)
            modulation(1)
            modulation(2)
            pe.wait_ge(consts_made, 6)
            attention_transposes(0, 0, xr)
            for b in range(3, B):
                modulation(b)
            pe.wait_ge(mod_copied, 6)
            for t in range(2):
                for m in range(KT):
                    o = ps[:, MODT_BANK, (t * KT + m) * B:(t * KT + m + 1) * B]
                    for k in range(KT):
                        last_mm = mm(o, s_mod[:, k, (3 + t) * D + m * P:(3 + t) * D + (m + 1) * P], scT[:, k, :], k == 0, k == KT - 1)
            last_mm.then_inc(mod_ready, 1)
            pe.wait_ge(product_lo, 2)
            pe.wait_ge(mod_copied, 2 * B)
            attention_transposes(0, 1, xr)
            queries(0)
            pe.wait_ge(mod_copied, 2 * B + 1)
            values(0, range(NT // 2))
            pe.wait_ge(pads_made, 7)

            def body(b, last):
                def probs_values(t, blocks=None):
                    for j in blocks or range(t + 1):
                        if j % TC == 0:
                            pe.wait_ge(pt_lo.sem, pt_lo.at(b, pt_banks(t)[j // TC][0]))
                        if j == 0 and t >= 2:
                            pe.wait_ge(x1_scaled.sem, x1_scaled.at(b, t - 2))
                        elif j == 0:
                            pe.wait_ge(proj_lo.sem, proj_lo.at(b, 6 + t))
                        last_mm = product(ps[:, 6 + t % 2, 0:D], [p[:, t % 2, j, :] for p in pT], [v[:, j, :] for v in vv],
                                          j == 0, j == t)
                    if j == t:
                        last_mm.then_inc(pv_ready.sem, 1)

                for i in range(NT + 1):
                    if i < NT:
                        w = (i + 1) * P
                        if i < 2:
                            pe.wait_ge(proj_lo.sem, proj_lo.at(b, 3))
                        else:
                            pe.wait_ge(probs_ready.sem, probs_ready.at(b, i - 2))
                        for n in range(-(-w // CH)):
                            cw = min(CH, w - n * CH)
                            o = ps[:, 2 * (i % 2) + n, 0:cw]
                            diagonal = (n + 1) * CH >= w
                            for k in range(KT):
                                last_mm = product(o, [q[:, k, i * P:(i + 1) * P] for q in qT],
                                                  [t[:, n, k, 0:cw] for t in xT], k == 0, k == KT - 1 and not diagonal)
                            if diagonal:
                                last_mm = mm(ps[:, 2 * (i % 2) + n, cw - P:cw], identb[:, :], causal[:, :], False, True)
                        last_mm.then_inc(scores_ready.sem, 1)
                        if i < 2:
                            values(b, range(NT // 2 + 2 * i, NT // 2 + 2 * i + 2))
                    else:
                        for k in range(KT):
                            pe.wait_ge(z2_ready.sem, z2_ready.at(b, TC - 1))
                            pe.wait_ge(probs_ready.sem, probs_ready.at(b, NT - 2))
                            transposes(b, KT * NC + k, k, k, range(TC))
                    if i >= 1:
                        t = i - 1
                        pe.wait_ge(probs_ready.sem, probs_ready.at(b, t))
                        for e, j0, nj in pt_banks(t):
                            if e >= 2:
                                pe.wait_ge(pt_lo.sem, pt_lo.at(b, e - 2))
                            else:
                                pe.wait_ge(proj_lo.sem, proj_lo.at(b, 4 + e))
                            for j in range(nj):
                                last_mm = transpose(ps[:, 4 + e % 2, j * P:(j + 1) * P],
                                                    probs[:, t % 2, (j0 + j) * P:(j0 + j + 1) * P], ident[:, :])
                            last_mm.then_inc(pt_ready.sem, 1)
                    if i >= 2:
                        probs_values(i - 2)

                def inputs(ci):
                    return [[t[:, 2 * ci, k, :] for t in xT] for k in range(KT)]

                def logits(ci):
                    pe.wait_ge(tr_lo.sem, tr_lo.at(b, KT * NC + ci * KT + 1))
                    for t in range(TC):
                        o = ps[:, LOGIT_BANK[ci], 2 * t * E:2 * (t + 1) * E]
                        for k in range(KT):
                            x_hi, x_lo = [x_[:, t * P:(t + 1) * P] for x_ in inputs(ci)[k]]
                            mm(o, x_hi, wr_both[:, k, :, :].rearrange("p h e -> p (h e)"), k == 0, False)
                            last_mm = mm(o[:, 0:E], x_lo, wr_both[:, k, 0, :], False, k == KT - 1)
                    last_mm.then_inc(logits_ready.sem, 1)

                def adapter_inputs(ci, gs=(0, 1)):
                    for g in gs:
                        for k in range(KT):
                            last_mm = product(ps[:, T_BANKS[ci][g], :], [w[:, g, k, :] for w in aT], inputs(ci)[k], k == 0, k == KT - 1)
                        last_mm.then_inc(t_ready.sem, 1)

                def mask(ci, m):
                    for t in range(TC):
                        last_mm = transpose(ps[:, MASK_BANKS[ci][m], t * P:(t + 1) * P], pick_er[:, m, t, :], ident[:, :])
                    last_mm.then_inc(masks_ready.sem, 1)

                def base(ci, g, a, parts=(0, 1)):
                    n = unit(ci, g, 0, a)
                    j = 2 * g + a
                    if g:
                        pe.wait_ge(h_ready.sem, h_ready.at(b, n - 2))
                    for part in parts[:1] if half(n) else parts:
                        for k in range(KT):
                            last_mm = product(ps[:, 2 * a + part, :], [h[:, k, j * P:(j + 1) * P] for h in (wgT, wuT)[part]], inputs(ci)[k],
                                              k == 0, k == KT - 1)
                    if parts[-1] == 1:
                        last_mm.then_inc(gate_up_ready.sem, 1)

                def adapters(ci, g, slot, a):
                    n = unit(ci, g, slot, a)
                    j = 2 * g + a
                    pe.wait_ge(h_ready.sem, h_ready.at(b, n - 2))
                    if g == 0 and a == 0:
                        pe.wait_ge(tm_ready.sem, tm_ready.at(b, ci * 4 + 2 * slot - 1))
                        if ci == 0:
                            pe.wait_ge(tm_low_ready.sem, tm_low_ready.at(b, 2 * slot - 2))
                    for m, (w, bank) in enumerate(((bgT, 2 * a), (buT, 2 * a + (0 if half(n) else 1)))):
                        last_mm = product(ps[:, bank, :], [h[:, j * P:(j + 1) * P] for h in w],
                                          [t[:, 2 * (slot - 1) + m, :] for t in tm], False, True)
                    last_mm.then_inc(gate_up_ready.sem, 1)

                def down(ci, g, slot, a):
                    n = unit(ci, g, slot, a)
                    j = 2 * g + a
                    hn = [t[:, place(n), :] for t in ring]
                    if half(n):
                        pe.wait_ge(stacked.sem, stacked.at(b, 3 * ci + slot))
                        passes = ((0, 0), (0, 1))
                    else:
                        pe.wait_ge(h_lo.sem, h_lo.at(b, n))
                        passes = ((0, 0), (0, 1), (1, 0))
                    if slot == 0:
                        if j == 0 and ci == 0:
                            pe.wait_ge(shifted_ready.sem, shifted_ready.at(b, 1))
                        elif j == 0:
                            pe.wait_ge(wmask_ready.sem, wmask_ready.at(b, 3))
                        for t in range(TC):
                            for ph, pw in passes:
                                last_mm = mm(ps[:, 6 + t // 2, t % 2 * D:(t % 2 + 1) * D], hn[ph][:, t * P:(t + 1) * P], wdT[pw][:, j, :],
                                             j == 0 and t % 2 == 0 and (ph, pw) == (0, 0), False)
                    else:
                        if j == 0:
                            pe.wait_ge(wmask_ready.sem, wmask_ready.at(b, ci * 2 + 1))
                        for ph, pw in passes:
                            last_mm = mm(ps[:, 3 + slot, :], adT[pw][:, j, :], hn[ph], j == 0 and (ph, pw) == (0, 0),
                                         j == FT - 1 and (ph, pw) == passes[-1])
                    last_mm.then_inc(h_used.sem, 1)

                def up_adapters(ci):
                    pe.wait_ge(dsum_lo.sem, dsum_lo.at(b, ci))
                    for t in range(TC):
                        last_mm = product(ps[:, 6 + t // 2, t % 2 * D:(t % 2 + 1) * D], [h[:, 3, t * P:(t + 1) * P] for h in tm],
                                          [w[:, :] for w in bdT], False, True)
                        if t % 2:
                            last_mm.then_inc(y_ready.sem, 1)

                FILL = (1, 2, 1, 1)

                def units(ci):
                    for g in range(GROUPS):
                        fill = [(ci, g - 1, s, a) for s, a in down_order(ci, g - 1)] if g else []
                        if g:
                            base(ci, g, 0)
                        if g:
                            base(ci, g, 1)
                        if ci == 0 and g == 1:
                            for k in range(KT):
                                pe.wait_ge(z2_ready.sem, z2_ready.at(b, NT - 1))
                                pe.wait_ge(masks_copied.sem, masks_copied.at(b, 1))
                                transposes(b, KT * NC + KT + k, 6 + k, k, range(TC, NT))
                        for slot in (1, 2):
                            for a in range(2):
                                if ci == 0 and g == 1 and slot == 2 and a == 0:
                                    logits(1)
                                else:
                                    count = FILL[(slot - 1) * 2 + a]
                                    for f in fill[:count]:
                                        down(*f)
                                    fill = fill[count:]
                                if g == 0 and a == 1:
                                    if slot == 1:
                                        pe.wait_ge(weights_spread.sem, weights_spread.at(b, ci))
                                    if ci == 0:
                                        pe.wait_ge(t_lo.sem, t_lo.at(b, slot - 1))
                                    elif slot == 2:
                                        pe.wait_ge(y_scaled.sem, y_scaled.at(b, TC - 1))
                                    mask(ci, 1 + slot)
                                adapters(ci, g, slot, a)
                        for f in fill:
                            down(*f)

                def last_downs(ci):
                    return [(ci, GROUPS - 1, s, a) for s, a in down_order(ci, GROUPS - 1)]

                pe.wait_ge(weight_lo, LATE)
                pe.wait_ge(probs_ready.sem, probs_ready.at(b, NT - 1))
                probs_values(NT - 1, range(PV_FIRST))
                logits(0)
                probs_values(NT - 1, range(PV_FIRST, NT))
                adapter_inputs(0)
                base(0, 0, 0, (0,))
                pe.wait_ge(x1_scaled.sem, x1_scaled.at(b, NT - 1))
                for m in range(2):
                    pe.wait_ge(masks_spread.sem, masks_spread.at(b, 0))
                    mask(0, m)
                base(0, 0, 0, (1,))
                pe.wait_ge(shifted_ready.sem, shifted_ready.at(b, 0))
                base(0, 0, 1)
                units(0)
                for f in last_downs(0)[:-2]:
                    down(*f)
                pe.wait_ge(h_ready.sem, h_ready.at(b, UPC - 1))
                adapter_inputs(1, (0,))
                for f in last_downs(0)[-2:]:
                    down(*f)
                adapter_inputs(1, (1,))
                pe.wait_ge(masks_spread.sem, masks_spread.at(b, 1))
                mask(1, 0)
                pe.wait_ge(t_lo.sem, t_lo.at(b, 2))
                base(1, 0, 0, (0,))
                pe.wait_ge(dsum_ready.sem, dsum_ready.at(b, 0))
                mask(1, 1)
                pe.wait_ge(t_lo.sem, t_lo.at(b, 3))
                base(1, 0, 0, (1,))
                up_adapters(0)
                pe.wait_ge(tm_ready.sem, tm_ready.at(b, 5))
                base(1, 0, 1)
                units(1)
                for d, f in enumerate(last_downs(1)):
                    if not last and d < NC:
                        pe.wait_ge(h_ready.sem, h_ready.at(b, 2 * UPC - 2 + d))
                        attention_transposes(b + 1, d)
                    down(*f)
                if not last:
                    queries(b + 1)
                up_adapters(1)
                if not last:
                    values(b + 1, range(NT // 2))
            batches(pe, body)


_INS = ['L0_attn_x', 'L0_attn_qkv', 'L0_attn_o_proj', 'L0_attn_gamma', 'L0_attn_beta', 'L0_ffn_Wg', 'L0_ffn_Wu', 'L0_ffn_Wd',
        'L0_ffn_Wr', 'L0_ffn_Ag', 'L0_ffn_Bg', 'L0_ffn_Au', 'L0_ffn_Bu', 'L0_ffn_Ad', 'L0_ffn_Bd', 'L0_c', 'L0_wmod']


_LAYOUT = {
    'L0_attn_qkv': lambda a: a.T, 'L0_attn_gamma': lambda a: a.reshape(-1, 128).T, 'L0_attn_beta': lambda a: a.reshape(-1, 128).T,
    'L0_ffn_Wg': lambda a: a.T, 'L0_ffn_Wu': lambda a: a.T, 'L0_ffn_Wd': lambda a: a.T, 'L0_ffn_Wr': lambda a: a.T,
    'L0_ffn_Ag': lambda a: a.reshape(-1, a.shape[2]).T, 'L0_ffn_Au': lambda a: a.reshape(-1, a.shape[2]).T,
    'L0_ffn_Ad': lambda a: a.reshape(-1, a.shape[2]).T,
    'L0_ffn_Bg': lambda a: a.transpose(0, 2, 1).reshape(-1, a.shape[1]),
    'L0_ffn_Bu': lambda a: a.transpose(0, 2, 1).reshape(-1, a.shape[1]),
    'L0_ffn_Bd': lambda a: a.transpose(0, 2, 1).reshape(-1, a.shape[1]),
    'L0_c': lambda a: a.T,
}


def kernel(**inputs):
    import numpy as _np
    import concourse.bacc as _bacc
    from concourse import mybir as _mybir
    from concourse.bass_utils import run_bass_kernel_spmd as _run

    nc = _bacc.Bacc("TRN2", target_bir_lowering=False, num_devices=1)
    arrays, args = {}, []
    for name in _INS:
        a = _LAYOUT.get(name, lambda v: v)(_np.asarray(inputs[name]))
        a = _np.ascontiguousarray(a)
        arrays[f"in_{name}"] = a
        args.append(nc.dram_tensor(f"in_{name}", a.shape, _mybir.dt.from_np(a.dtype), kind="ExternalInput").ap())
    shape = arrays["in_L0_attn_x"].shape
    out = nc.dram_tensor("out_0", shape, _mybir.dt.float32, kind="ExternalOutput").ap()
    adaln_attention_moe_lora(nc, *args, out)
    r = _run(nc, [arrays], core_ids=[0])
    return r.results[0]["out_0"]
```
